# Optimizing a Trainium2 kernel written in Bass

```python
import numpy as np
import jax
import jax.numpy as jnp

def _softmax(x, axis=-1):
    return jax.nn.softmax(x, axis=axis)

def _gelu(x):
    return jax.nn.gelu(x, approximate=True)

def _silu(x):
    return jax.nn.silu(x)

def _sigmoid(x):
    return jax.nn.sigmoid(x)

def _layernorm(x, axis=-1, eps=1e-05):
    m = jnp.mean(x, axis=axis, keepdims=True)
    v = jnp.var(x, axis=axis, keepdims=True)
    return (x - m) / jnp.sqrt(v + eps)

def _scatter_add(tgt, idx, src, axis=0):
    return tgt.at[idx].add(src)

def _segment_sum(src, seg, n):
    return jax.ops.segment_sum(src, seg, n)
kernel_name = 'mk_prb_d2_jaxref_r8_49e8df'

def setup_inputs(seed: int=0):
    np.random.seed(seed)
    _w = jnp.asarray

    def _L0_attn_setup():
        import jax, jax.numpy as jnp
        import numpy as np
        B, T, D, H = (1, 512, 128, 16)
        DK = D // H
        SCALE = 1.0 / float(np.sqrt(DK))
        NEG = -1000000000.0
        key = jax.random.key(seed)
        k1, k2, k3 = jax.random.split(key, 3)
        x = jax.random.normal(k1, (B, T, D), dtype=jnp.float32)
        Wqkv = jax.random.normal(k2, (3 * D, D), dtype=jnp.float32) * 0.02
        Wout = jax.random.normal(k3, (D, D), dtype=jnp.float32) * 0.02
        return {'x': x, 'Wqkv': Wqkv, 'Wout': Wout}
    _L0_attn_in = _L0_attn_setup()

    def _L0_ffn_setup():
        import jax, jax.numpy as jnp
        import numpy as np
        H = 128
        E = 8
        B, S = (4, 256)
        key = jax.random.key(seed)
        k1, k2, k3, k4 = jax.random.split(key, 4)
        x = jax.random.normal(k1, (B, S, H), dtype=jnp.float32)
        wg = jax.random.normal(k2, (H, E), dtype=jnp.float32) * 0.02
        W = jax.random.normal(k3, (E, H, H), dtype=jnp.float32) * 0.02
        b = jax.random.normal(k4, (E, H), dtype=jnp.float32) * 0.02
        return {'x': x, 'wg': wg, 'W': W, 'b': b}
    _L0_ffn_in = _L0_ffn_setup()

    def _L1_attn_setup():
        import jax, jax.numpy as jnp
        import numpy as np
        OFFSETS = np.array(sorted(set(range(0, 33)) | {48, 64, 96, 128, 192, 32, 48, 64, 96, 128, 192}), dtype=np.int32)
        NUM_HEADS = 16
        key = jax.random.key(seed)
        ks = jax.random.split(key, 8)
        B, N, D = (1, 256, 128)
        H = NUM_HEADS
        O = len(OFFSETS)
        s = 0.02
        x = jax.random.normal(ks[0], (B, N, D), dtype=jnp.float32)
        Wqkv = jax.random.normal(ks[1], (3 * D, D), dtype=jnp.float32) * s
        bqkv = jnp.zeros((3 * D,), dtype=jnp.float32)
        Wout = jax.random.normal(ks[2], (D, D), dtype=jnp.float32) * s
        bout = jnp.zeros((D,), dtype=jnp.float32)
        Wgate = jax.random.normal(ks[3], (D, D), dtype=jnp.float32) * s
        bgate = jnp.full((D,), 2.0, dtype=jnp.float32)
        alphas = jnp.linspace(0.2, 2.0, H)
        delta = jnp.log1p(jnp.asarray(OFFSETS, dtype=jnp.float32))
        pos_bias = -delta[:, None] * alphas[None, :]
        return {'x': x, 'Wqkv': Wqkv, 'bqkv': bqkv, 'Wout': Wout, 'bout': bout, 'Wgate': Wgate, 'bgate': bgate, 'pos_bias': pos_bias}
    _L1_attn_in = _L1_attn_setup()

    def _L1_ffn_setup():
        import jax, jax.numpy as jnp
        import numpy as np
        B, S, DIM = (4, 256, 128)
        E, K, HID = (8, 2, 512)
        key = jax.random.key(seed)
        ks = jax.random.split(key, 8)
        init = lambda k, sh: jax.random.normal(k, sh, jnp.float32) * 0.02
        return {'x': jax.random.normal(ks[0], (B, S, DIM), jnp.float32), 'gate_w': init(ks[1], (DIM, E)), 'gate_b': jnp.zeros((E,), jnp.float32), 'w1': init(ks[2], (E, DIM, HID)), 'b1': jnp.zeros((E, HID), jnp.float32), 'w2': init(ks[3], (E, HID, DIM)), 'b2': jnp.zeros((E, DIM), jnp.float32), 'ws1': init(ks[4], (DIM, HID)), 'bs1': jnp.zeros((HID,), jnp.float32), 'ws2': init(ks[5], (HID, DIM)), 'bs2': jnp.zeros((DIM,), jnp.float32)}
    _L1_ffn_in = _L1_ffn_setup()
    _d = {'L0_attn_x': _L0_attn_in['x'], 'L0_attn_Wqkv': _L0_attn_in['Wqkv'], 'L0_attn_Wout': _L0_attn_in['Wout'], 'L0_ffn_wg': _L0_ffn_in['wg'], 'L0_ffn_W': _L0_ffn_in['W'], 'L0_ffn_b': _L0_ffn_in['b'], 'L1_attn_Wqkv': _L1_attn_in['Wqkv'], 'L1_attn_bqkv': _L1_attn_in['bqkv'], 'L1_attn_Wout': _L1_attn_in['Wout'], 'L1_attn_bout': _L1_attn_in['bout'], 'L1_attn_Wgate': _L1_attn_in['Wgate'], 'L1_attn_bgate': _L1_attn_in['bgate'], 'L1_attn_pos_bias': _L1_attn_in['pos_bias'], 'L1_ffn_gate_w': _L1_ffn_in['gate_w'], 'L1_ffn_gate_b': _L1_ffn_in['gate_b'], 'L1_ffn_w1': _L1_ffn_in['w1'], 'L1_ffn_b1': _L1_ffn_in['b1'], 'L1_ffn_w2': _L1_ffn_in['w2'], 'L1_ffn_b2': _L1_ffn_in['b2'], 'L1_ffn_ws1': _L1_ffn_in['ws1'], 'L1_ffn_bs1': _L1_ffn_in['bs1'], 'L1_ffn_ws2': _L1_ffn_in['ws2'], 'L1_ffn_bs2': _L1_ffn_in['bs2']}
    _x0 = _d['L0_attn_x']
    _d['L0_attn_x'] = jax.random.normal(jax.random.fold_in(jax.random.key(seed), 1), (16, 256, 128), dtype=_x0.dtype)
    del _x0
    return _d

def reference(L0_attn_x, L0_attn_Wqkv, L0_attn_Wout, L0_ffn_wg, L0_ffn_W, L0_ffn_b, L1_attn_Wqkv, L1_attn_bqkv, L1_attn_Wout, L1_attn_bout, L1_attn_Wgate, L1_attn_bgate, L1_attn_pos_bias, L1_ffn_gate_w, L1_ffn_gate_b, L1_ffn_w1, L1_ffn_b1, L1_ffn_w2, L1_ffn_b2, L1_ffn_ws1, L1_ffn_bs1, L1_ffn_ws2, L1_ffn_bs2):

    def _L0_attn_ref(x, Wqkv, Wout):
        import jax, jax.numpy as jnp
        import numpy as np
        B, T, D, H = (1, 512, 128, 16)
        DK = D // H
        SCALE = 1.0 / float(np.sqrt(DK))
        NEG = -1000000000.0
        b, t, d = x.shape
        qkv = jnp.einsum('btd,ed->bte', x, Wqkv)
        qkv = qkv.reshape(b, t, 3, H, DK).transpose(2, 0, 3, 1, 4)
        q, k, v = (qkv[0], qkv[1], qkv[2])
        scores = jnp.einsum('bhtd,bhsd->bhts', q, k) * SCALE
        scores = jnp.clip(scores, -10.0, 10.0)
        mask = jnp.triu(jnp.full((t, t), NEG, dtype=scores.dtype), k=1)
        scores = scores + mask[None, None, :, :]
        attn = jax.nn.softmax(scores, axis=-1)
        out = jnp.einsum('bhts,bhsd->bhtd', attn, v)
        out = out.transpose(0, 2, 1, 3).reshape(b, t, d)
        return jnp.einsum('btd,ed->bte', out, Wout)

    def _L0_ffn_ref(x, wg, W, b):
        import jax, jax.numpy as jnp
        import numpy as np
        H = 128
        E = 8
        B, S = (4, 256)
        Bb, Ss, Hh = x.shape
        Ee = wg.shape[1]
        T = Bb * Ss
        C = T // Ee
        xt = x.reshape(T, Hh)
        logits = xt @ wg
        probs = jax.nn.softmax(logits, axis=-1)
        idx = jnp.argmax(probs, axis=-1)
        mask = jax.nn.one_hot(idx, Ee, dtype=xt.dtype)
        locations = jnp.cumsum(mask, axis=0) - mask
        mask = mask * (locations < C).astype(xt.dtype)
        gate = jnp.sum(probs * mask, axis=-1)
        loc_s = jnp.sum(locations * mask, axis=-1).astype(jnp.int32)
        loc_oh = jax.nn.one_hot(loc_s, C, dtype=xt.dtype)
        dispatch = mask[:, :, None] * loc_oh[:, None, :]
        combine = gate[:, None, None] * dispatch
        exp_in = jnp.einsum('tec,th->ech', dispatch, xt)
        exp_out = jnp.einsum('ech,efh->ecf', exp_in, W) + b[:, None, :]
        out = jnp.einsum('tec,ecf->tf', combine, exp_out)
        return out.reshape(Bb, Ss, Hh)

    def _L1_attn_ref(x, Wqkv, bqkv, Wout, bout, Wgate, bgate, pos_bias):
        import jax, jax.numpy as jnp
        import numpy as np
        OFFSETS = np.array(sorted(set(range(0, 33)) | {48, 64, 96, 128, 192, 32, 48, 64, 96, 128, 192}), dtype=np.int32)
        NUM_HEADS = 16
        B, N, D = x.shape
        H = NUM_HEADS
        HD = D // H
        offs = jnp.asarray(OFFSETS)
        max_off = int(OFFSETS[-1])
        scale = HD ** (-0.5)
        qkv = x @ Wqkv.T + bqkv
        q, k, v = jnp.split(qkv, 3, axis=-1)
        q = q.reshape(B, N, H, HD).transpose(0, 2, 1, 3)
        k = k.reshape(B, N, H, HD).transpose(0, 2, 1, 3)
        v = v.reshape(B, N, H, HD).transpose(0, 2, 1, 3)
        k_pad = jnp.pad(k, ((0, 0), (0, 0), (max_off, 0), (0, 0)))
        v_pad = jnp.pad(v, ((0, 0), (0, 0), (max_off, 0), (0, 0)))
        n_idx = jnp.arange(N)
        gather_idx = max_off - offs[:, None] + n_idx[None, :]
        K_all = k_pad[:, :, gather_idx, :]
        V_all = v_pad[:, :, gather_idx, :]
        scores = jnp.einsum('bhnd,bhond->bhno', q, K_all) * scale
        scores = scores + pos_bias.T[None, :, None, :]
        invalid = n_idx[:, None] < offs[None, :]
        scores = jnp.where(invalid[None, None], -jnp.inf, scores)
        alpha = jax.nn.softmax(scores, axis=-1)
        out = jnp.einsum('bhno,bhond->bhnd', alpha, V_all)
        flat = out.transpose(0, 2, 1, 3).reshape(B, N, D)
        gate = jax.nn.sigmoid(x @ Wgate.T + bgate)
        return flat * gate @ Wout.T + bout

    def _L1_ffn_ref(x, gate_w, gate_b, w1, b1, w2, b2, ws1, bs1, ws2, bs2):
        import jax, jax.numpy as jnp
        import numpy as np
        B, S, DIM = (4, 256, 128)
        E, K, HID = (8, 2, 512)
        orig_shape = x.shape
        xf = x.reshape(-1, DIM)
        logits = xf @ gate_w + gate_b
        top_w, top_i = jax.lax.top_k(logits, K)
        gw = jax.nn.softmax(top_w, axis=-1).astype(xf.dtype)
        combine = (gw[:, :, None] * jax.nn.one_hot(top_i, E, dtype=xf.dtype)).sum(axis=1)
        out = jnp.zeros_like(xf)
        for e in range(E):
            h = jax.nn.gelu(xf @ w1[e] + b1[e], approximate=False)
            out = out + combine[:, e:e + 1] * (h @ w2[e] + b2[e])
        shared = jax.nn.gelu(xf @ ws1 + bs1, approximate=False) @ ws2 + bs2
        return (out + shared).reshape(orig_shape)
    x = L0_attn_x
    xn = _layernorm(x, axis=-1)
    x = x + _L0_attn_ref(xn, L0_attn_Wqkv, L0_attn_Wout) + _L0_ffn_ref(xn, L0_ffn_wg, L0_ffn_W, L0_ffn_b)
    xn = _layernorm(x, axis=-1)
    x = x + _L1_attn_ref(xn, L1_attn_Wqkv, L1_attn_bqkv, L1_attn_Wout, L1_attn_bout, L1_attn_Wgate, L1_attn_bgate, L1_attn_pos_bias) + _L1_ffn_ref(xn, L1_ffn_gate_w, L1_ffn_gate_b, L1_ffn_w1, L1_ffn_b1, L1_ffn_w2, L1_ffn_b2, L1_ffn_ws1, L1_ffn_bs1, L1_ffn_ws2, L1_ffn_bs2)
    return x

_drawn_inputs = setup_inputs


def setup_inputs(seed=0):
    import zlib

    import numpy as np

    out = dict(_drawn_inputs(seed))
    spreads = {'L1_attn_bqkv': (0.0, 0.396),
     'L1_attn_bout': (0.0, 0.1),
     'L1_attn_bgate': (2.0, 0.6),
     'L1_ffn_gate_b': (0.0, 0.1),
     'L1_ffn_b1': (0.0, 0.468),
     'L1_ffn_b2': (0.0, 0.1),
     'L1_ffn_bs1': (0.0, 0.371),
     'L1_ffn_bs2': (0.0, 0.1)}
    factors = {'L0_attn_Wqkv': 6.321,
     'L0_attn_Wout': 5.883,
     'L0_ffn_b': 8.0,
     'L1_attn_Wqkv': 3.083,
     'L1_attn_Wgate': 8.0,
     'L1_attn_pos_bias': 3.354}
    for name, (base, spread) in spreads.items():
        noise = np.random.default_rng([zlib.crc32(name.encode()), seed]).standard_normal(out[name].shape)
        drawn = base * np.exp(spread * noise) if base else spread * noise
        out[name] = jnp.asarray(drawn.astype(out[name].dtype))
    for name, factor in factors.items():
        out[name] = (out[name] * factor).astype(out[name].dtype)
    return out
```

```python
from contextlib import ExitStack

import concourse.bass as bass
from concourse import mybir

F32 = mybir.dt.float32
BF16 = mybir.dt.bfloat16
I32 = mybir.dt.int32
ALU = mybir.AluOpType
ACT = mybir.ActivationFunctionType
AX = mybir.AxisListType

P = 128
B, T, D = 16, 256, 128
H, DK = 16, 8
NT = B * T // P
ST = 4
NS = NT // ST
SC = ST * P
E = 8
CAP = B * T // E
TERMS = 6
Q_PARTS = (0, 0, 0, 1, 1, 2)
K_PARTS = (0, 1, 2, 0, 1, 0)
SROWS = 96
MROWS = 99
EPS = 1e-5
SCALE = DK ** -0.5
CLIP_HI = 22026.465794806718
CLIP_LO = 4.5399929762484854e-05
QW = 384
VW = 32


OFFSETS = tuple(range(33)) + (48, 64, 96, 128, 192)
MASKED = -1e30
LINE = 640
HID = 512
HC = HID // P
LW = 4 * P


def build(nc, x, wqkv0, wout0, wg0, w_exp0, b_exp0, wqkv1, bqkv1, wout1, bout1, wgate1, bgate1, pos_bias,
          gate_w, gate_b, w1, b1, w2, b2, ws1, bs1, ws2, bs2, out):
    scr_q = nc.dram_tensor("scr_q", (3, P, SC), BF16, kind="Internal").ap()
    scr_k = nc.dram_tensor("scr_k", (3, P, SC), BF16, kind="Internal").ap()
    scr_line = nc.dram_tensor("scr_line", (2, H, LINE), F32, kind="Internal").ap()
    ctx = ExitStack()
    with ctx:
        def sb(name, shape, dt=F32):
            return ctx.enter_context(nc.sbuf_tensor(name, shape, dt))

        def sem(name):
            return ctx.enter_context(nc.semaphore(name))

        X = sb("X", [P, NT, D])
        XNT = sb("XNT", [P, NT * P])
        logit0 = sb("logit0", [P, NT, E])
        ident = sb("ident", [P, P])
        ident16 = sb("ident16", [P, P], BF16)
        flip = sb("flip", [P, P])
        diagcap = sb("diagcap", [P, 2 * P])
        wT1 = sb("wT1", [P, 5, P])
        wv1 = sb("wv1", [P, P + E])
        w0T = sb("w0T", [P, E, P])
        bcol = sb("bcol", [P, E * HC + HC + 3])
        bqkg = sb("bqkg", [P, 3])
        one_row = sb("one_row", [1, P])
        bias_v = sb("bias_v", [1, P + E])
        bias_o = sb("bias_o", [1, P])
        bdiag0 = sb("bdiag0", [4 * E, ST, D])
        bdiag1 = sb("bdiag1", [4 * E + 1, ST, D])
        upper = sb("upper", [P, P])
        ones_sq = sb("ones_sq", [P, P])
        rank8 = sb("rank8", [P, E])
        tables = sb("tables", [P, H * QW + H * T])
        btab = tables[:, 0:H * QW].rearrange("p (h c) -> p h c", h=H)
        btabq = tables[:, H * QW:H * (QW + T)].rearrange("p (h c) -> p h c", h=H)
        w1_sb = tables[:, 0:E * HID].rearrange("p (e n) -> p e n", e=E)
        w2_sb = tables[:, E * HID:2 * E * HID].rearrange("p (e c n) -> p e c n", e=E, c=HC)
        ws1_sb = sb("ws1_sb", [P, HID])
        ws2_sb = sb("ws2_sb", [P, HC, D])
        pbT = sb("pbT", [H, len(OFFSETS)])
        lines = tables[0:H, 0:2 * LINE].rearrange("h (a c) -> h a c", a=2)
        xstat = sb("xstat", [P, SC])
        wraw = xstat[:].rearrange("p (c n) -> p c n", c=4)
        comb = sb("comb", [P, NT, E])
        comb_s = sb("comb_s", [P, ST, E])
        combT = sb("combT", [4 * E + 1, P])
        acc = [sb(f"acc{i}", [P, ST, D]) for i in range(2)]
        x1 = acc[1]
        routes = sb("routes", [P, 3 * NT * E])
        rt = [routes[:, i * NT * E:(i + 1) * NT * E].rearrange("p (t e) -> p t e", e=E) for i in range(3)]
        wraw1 = routes[:, 0:5 * P].rearrange("p (c n) -> p c n", c=5)
        rs = [sb(f"rs{i}", [P, NT]) for i in range(4)]
        egraw = sb("egraw", [P, SC])
        brow = egraw[0:E * HC + HC + 3, 0:P]
        eg = [sb(f"eg{u}", [P, T]) for u in range(2)]
        unused = sb("unused", [P, 9])
        smax = sb("smax", [P, 2, H])
        mrest = sb("mrest", [P, 2, H])
        mparts = sb("mparts", [P, 2, 3, H], BF16)
        mT = sb("mT", [3 * H, T], BF16)
        wT0 = sb("wT0", [P, 4, P])
        wv0 = sb("wv0", [P, P + E])
        stats = sb("stats", [P, ST, 6])
        moments = sb("moments", [P, ST, 2])
        var_eps = sb("var_eps", [P, ST])
        minus_half = sb("minus_half", [P, ST])
        rstd0 = sb("rstd0", [P, ST])
        newton = sb("newton", [P, ST])
        rstd = sb("rstd", [P, ST])
        xn = sb("xn", [P, ST, D])
        xnT = sb("xnT", [P, SC])
        parts = {}
        for w in "qk":
            parts[w] = [sb(f"{w}_hi", [P, SC], BF16), sb(f"{w}_mid", [P, SC], BF16), sb(f"{w}_lo", [P, SC], BF16)]
        rest = {w: sb(f"{w}_rest", [P, SC]) for w in "qk"}
        qs = [sb(f"qs{u}", [MROWS, H, T], BF16) for u in range(2)]
        ks = [sb(f"ks{u}", [MROWS, H, T], BF16) for u in range(2)]
        vraw = sb("vraw", [P, ST, D])
        vpad = [sb(f"vpad{u}", [P, 2, H, VW]) for u in range(2)]
        ones_pad = sb("ones_pad", [P, 4, VW])
        wide = [sb(f"wide{q}", [P, 4 * LW]) for q in range(4)]
        probs = [w[:, 0:4 * QW].rearrange("p (g c) -> p g c", g=4) for w in wide]
        rden = sb("rden", [P, T])
        heads = sb("heads", [P, T])

        psS = [ctx.enter_context(nc.psum_tensor(f"psS{i}", [P, 2, 512], F32)) for i in range(2)]
        psN = [ctx.enter_context(nc.psum_tensor(f"psN{i}", [P, 512], F32)) for i in range(2)]
        psA = ctx.enter_context(nc.psum_tensor("psA", [P, 512], F32))
        psB = ctx.enter_context(nc.psum_tensor("psB", [P, 512], F32))

        x_first, x_rest = sem("x_first"), sem("x_rest")
        w_in, wt_ps, wt_done, consts = sem("w_in"), sem("wt_ps"), sem("wt_done"), sem("consts")
        stat_done, mom_done, var_done, pow_done = sem("stat_done"), sem("mom_done"), sem("var_done"), sem("pow_done")
        newt, xn_done, xn_turned, xnT_done, xnT_kept = sem("newt"), sem("xn_done"), sem("xn_turned"), sem("xnT_done"), sem("xnT_kept")
        q_ps, k_ps, v_ps = sem("q_ps"), sem("k_ps"), sem("v_ps")
        hi_done, rest_done, mid_done, lo_done = sem("hi_done"), sem("rest_done"), sem("mid_done"), sem("lo_done")
        v_out, logits_out, vpad_done = sem("v_out"), sem("logits_out"), sem("vpad_done")
        scratch_in = sem("scratch_in")
        qk_in = [sem("qk_in0"), sem("qk_in1")]
        scored, exp_done, clipped, weighed = sem("scored"), sem("exp_done"), sem("clipped"), sem("weighed")
        rden_done, heads_done, out_ps, x_done = sem("rden_done"), sem("heads_done"), sem("out_ps"), sem("x_done")
        stored = sem("stored")
        masks_done, ones_done = sem("masks_done"), sem("ones_done")
        late_in, later_in, wt1_ps, wt1_done = sem("late_in"), sem("later_in"), sem("wt1_ps"), sem("wt1_done")
        lines_done, lines_in, tables_in = sem("lines_done"), sem("lines_in"), sem("tables_in")
        pos_in, key_ps, key_done = sem("pos_in"), sem("key_ps"), sem("key_done")
        query_ps, query_done, table_copied = sem("query_ps"), sem("query_done"), sem("table_copied")
        routing, loc_ps, route_exp, comb_done = sem("routing"), sem("loc_ps"), sem("route_exp"), sem("comb_done")
        stat_in, comb_s_done, combT_ps, combT_done = sem("stat_in"), sem("comb_s_done"), sem("combT_ps"), sem("combT_done")
        bias_ps, mix_ps, mixed, x1_kept = sem("bias_ps"), sem("mix_ps"), sem("mixed"), sem("x1_kept")
        gate_ps, eg_out, eg_done = sem("gate_ps"), sem("eg_out"), sem("eg_done")
        ranked, maxed, neg_done, negT_ps, negT_done = sem("ranked"), sem("maxed"), sem("neg_done"), sem("negT_ps"), sem("negT_done")
        neg_step, gated, lined, bias_added = sem("neg_step"), sem("gated"), sem("lined"), sem("bias_added")
        y_banks = [psN[0], psN[1], psB]
        ONEHOT_AT, SHIFTED_AT, SECOND_AT = 5, 6, 29
        WT1 = 6
        LATE, LATER = 9, 18
        m_in = [sem("m_in0"), sem("m_in1")]
        biased, exp1_done = sem("biased"), sem("exp1_done")
        w_exp_in = [sem(f"w_exp_in{i}") for i in range(4)]
        hid_ps, gelu_done, y_ps, y_used = sem("hid_ps"), sem("gelu_done"), sem("y_ps"), sem("y_used")

        block = ctx.enter_context(nc.Block())

        def steps(engine, body, base=0):
            body(base, True, False)
            with engine.Fori(base + 1, base + NS - 1) as s:
                body(s, False, False)
            body(base + NS - 1, False, True)

        def spread_over(t, pattern):
            return bass.AP(tensor=t[:].tensor, offset=t[:].offset, ap=pattern)

        x_tiles = x.rearrange("b (t p) d -> p (b t) d", p=P)

        @block.sync
        def _(sp):
            sp.dma_start(X[:, 0:ST, :], x_tiles[:, 0:ST, :]).then_inc(x_first, 16)
            sp.dma_start(pbT[:], pos_bias.rearrange("o h -> h o"), allow_slow_non_contiguous=True).then_inc(pos_in, 16)
            sp.dma_start(wraw[:, 0:3, :], wqkv0.rearrange("(c p) d -> p c d", p=P)).then_inc(w_in, 16)
            sp.dma_start(wraw[:, 3, :], wout0).then_inc(w_in, 16)
            sp.dma_start(wv0[:, P:P + E], wg0).then_inc(w_in, 16)
            sp.dma_start(X[:, ST:NT, :], x_tiles[:, ST:NT, :]).then_inc(x_rest, 16)

            def late(dst, src):
                sp.dma_start(dst, src).then_inc(late_in, 16)

            def later(dst, src):
                sp.dma_start(dst, src).then_inc(later_in, 16)

            late(wraw1[:, 0:3, :], wqkv1.rearrange("(c p) d -> p c d", p=P))
            late(wraw1[:, 3, :], wout1)
            late(wraw1[:, 4, :], wgate1)
            for i in range(2):
                late(acc[i][:], w_exp0[4 * i:4 * i + 4].rearrange("e f h -> f e h"))
            late(brow[0:E * HC, :], b1.rearrange("e (c p) -> (e c) p", p=P))
            late(brow[E * HC:E * HC + HC, :], bs1.rearrange("(c p) -> c p", p=P))
            late(brow[E * HC + HC:E * HC + HC + 2, :], bqkv1[0:2 * P].rearrange("(c p) -> c p", p=P))
            late(brow[E * HC + HC + 2:E * HC + HC + 3, :], bgate1.rearrange("(c p) -> c p", p=P))

            def spread(step, at, read=None):
                sp.wait_ge(hi_done, 2 * (step + 1))
                sp.wait_ge(mid_done, 2 * (step + 1))
                sp.wait_ge(lo_done, 2 * (step + 1))
                for scr, w in ((scr_q, "q"), (scr_k, "k")):
                    for i in range(3):
                        sp.dma_start(scr[i], parts[w][i][:]).then_inc(scratch_in, 16)
                if read is not None:
                    sp.wait_ge(stat_in, read)
                sp.dma_start(XNT[:, bass.ds(at * SC, SC)], xnT[:]).then_inc(xnT_kept, 16)
                sp.wait_ge(scratch_in, 96 * (step + 1))

            def load(u):
                for scr, to, which in ((scr_q, qs, Q_PARTS), (scr_k, ks, K_PARTS)):
                    for r, i in enumerate(which):
                        sp.dma_start(to[u][DK * r:DK * (r + 1), :, :],
                                     scr[i][:, u * T:(u + 1) * T].rearrange("(h d) t -> d h t", d=DK))\
                          .then_inc(qk_in[u], 16)

            sp.wait_ge(lines_done, 1)
            sp.dma_start(scr_line.rearrange("a h c -> h a c"), lines).then_inc(lines_in, 16)
            sp.wait_ge(lines_in, 16)
            by_key = bass.AP(tensor=scr_line.tensor, offset=scr_line.offset + T - (P - 1), ap=[[1, P], [LINE, H], [1, T]])
            sp.dma_start(btab[:, :, P:QW], by_key).then_inc(tables_in, 16)
            by_query = bass.AP(tensor=scr_line.tensor, offset=scr_line.offset + H * LINE + LINE - 2 * T,
                               ap=[[1, P], [LINE, H], [1, T]])
            sp.dma_start(btabq, by_query).then_inc(tables_in, 16)

            sp.wait_ge(consts, 7)
            spread(0, 0)
            load(0)
            load(1)
            later(bias_v[:, 0:P], bqkv1[2 * P:3 * P].rearrange("(a n) -> a n", a=1))
            later(bias_v[:, P:P + E], gate_b.rearrange("(a n) -> a n", a=1))
            later(bias_o[:], bout1.rearrange("(a n) -> a n", a=1))
            later(wv1[:, P:P + E], gate_w)
            later(ws1_sb[:], ws1)
            later(ws2_sb[:], ws2.rearrange("(c p) n -> p c n", p=P))
            for t in range(ST):
                later(bdiag0[E * t:E * (t + 1), t, :], b_exp0)
                later(bdiag1[E * t:E * (t + 1), t, :], b2)
                later(bdiag1[4 * E:4 * E + 1, t, :], bs2.rearrange("(a n) -> a n", a=1))

            def body(s, first, last):
                if last:
                    return
                sp.wait_ge(qk_in[1], 192 * (s + 1))
                spread(s + 1, s + 1)
                sp.wait_ge(scored, 16 * s + 8)
                load(0)
                sp.wait_ge(scored, 16 * s + 16)
                load(1)
            steps(sp, body)

            def fetch(at):
                sp.dma_start(xstat[:], XNT[:, bass.ds(at * SC, SC)]).then_inc(stat_in, 16)

            def keep(at):
                sp.wait_ge(mixed, E * (at + 1))
                sp.dma_start(X[:, bass.ds(at * ST, ST), :], x1[:]).then_inc(x1_kept, 16)

            def load_maxima(u, n):
                sp.wait_ge(negT_done, n + 1)
                for i in range(3):
                    sp.dma_start(qs[u][SROWS + i:SROWS + i + 1, :, :], mT[H * i:H * (i + 1), :]).then_inc(m_in[u], 16)

            sp.wait_ge(xnT_kept, 16 * NS)
            fetch(0)
            keep(0)
            sp.wait_ge(qk_in[1], 192 * NS)
            spread(NS, 0, 16)
            sp.wait_ge(scored, 16 * NS)
            load(0)
            load(1)
            load_maxima(0, 0)

            def body1(s, first, last):
                if not last:
                    sp.wait_ge(mix_ps, E * (s - NS + 1))
                    fetch(s - NS + 1)
                    keep(s - NS + 1)
                    sp.wait_ge(qk_in[1], 192 * (s + 1))
                    spread(s + 1, s - NS + 1, 16 * (s - NS + 2))
                    sp.wait_ge(scored, 16 * s + 8)
                    load(0)
                load_maxima(1, 2 * (s - NS) + 1)
                if not last:
                    load_maxima(0, 2 * (s - NS) + 2)
                    sp.wait_ge(scored, 16 * s + 16)
                    load(1)
            steps(sp, body1, NS)

            sp.wait_ge(maxed, 16 * NS)
            sp.wait_ge(biased, 16 * NS)
            for i in range(4):
                sp.dma_start(w1_sb[:, 2 * i:2 * i + 2, :], w1[2 * i:2 * i + 2].rearrange("e p n -> p e n")).then_inc(w_exp_in[i], 16)
                for e in (2 * i, 2 * i + 1):
                    sp.dma_start(w2_sb[:, e, :, :], w2[e].rearrange("(c p) n -> p c n", p=P)).then_inc(w_exp_in[i], 16)

            out_tiles = out.rearrange("b (t p) d -> p (b t) d", p=P)

            def body2(s, first, last):
                sp.wait_ge(y_used, (E + 1) * (s + 1))
                sp.dma_start(out_tiles[:, bass.ds(s * ST, ST), :], acc[0][:]).then_inc(stored, 16)
            steps(sp, body2)
            sp.wait_ge(stored, 16 * NS)

        @block.gpsimd
        def _(pool):
            pool.memset(ident[:], 0.0).then_inc(consts, 1)
            pool.memset(diagcap[:], CLIP_HI).then_inc(consts, 1)
            pool.memset(flip[:], 0.0).then_inc(consts, 1)
            pool.memset(ones_sq[:], 1.0).then_inc(consts, 1)
            pool.wait_ge(consts, 4)
            pool.affine_select(out=ident[:], in_=ident[:], compare_op=ALU.not_equal, fill=1.0, base=0,
                               pattern=[[-1, P]], channel_multiplier=1).then_inc(masks_done, 1)
            pool.affine_select(out=upper[:], in_=ones_sq[:], compare_op=ALU.is_gt, fill=0.0, base=0,
                               pattern=[[1, P]], channel_multiplier=-1).then_inc(masks_done, 1)
            pool.affine_select(out=flip[:], in_=flip[:], compare_op=ALU.not_equal, fill=1.0, base=-(P - 1),
                               pattern=[[1, P]], channel_multiplier=1).then_inc(masks_done, 1)
            both = diagcap[:].rearrange("p (a n) -> p a n", a=2)
            pool.affine_select(out=both, in_=both, compare_op=ALU.is_ge, fill=0.0, base=0,
                               pattern=[[0, 2], [1, P]], channel_multiplier=-1).then_inc(masks_done, 1)
            pool.wait_ge(masks_done, 1)
            pool.tensor_copy(ident16[:], ident[:]).then_inc(consts, 1)
            pool.memset(minus_half[:], -0.5).then_inc(consts, 1)
            pool.memset(bdiag0[:], 0.0)
            pool.memset(bdiag1[:], 0.0)
            for u in range(2):
                pool.memset(qs[u][:].bitcast(F32)[0:SROWS], 0.0)
                pool.memset(ks[u][:].bitcast(F32)[0:SROWS], 0.0)
                last = pool.memset(vpad[u][:], 0.0)
            last.then_inc(consts, 1)

            def power(step):
                pool.wait_ge(var_done, step + 1)
                pool.tensor_tensor(rstd0[:], var_eps[:], minus_half[:], ALU.pow).then_inc(pow_done, 1)

            def low(step):
                for n, w in enumerate("qk"):
                    pool.wait_ge(mid_done, 2 * step + n + 1)
                    pool.tensor_tensor(parts[w][2][:], rest[w][:], parts[w][1][:], ALU.subtract).then_inc(lo_done, 1)

            def pad(step, u, wait_batch):
                pool.wait_ge(v_out, 2 * (step + 1))
                if wait_batch is not None:
                    pool.wait_ge(weighed, wait_batch)
                pool.tensor_tensor(spread_over(vpad[u], [[2 * H * VW, P], [4 * VW, 8], [VW + DK, 4], [1, DK]]),
                                   vraw[:, 2 * u:2 * u + 2, :].rearrange("p t (g j d) -> p (t g) j d", g=4, j=4),
                                   spread_over(ones_sq, [[P, P], [0, 8], [0, 4], [1, DK]]), ALU.mult).then_inc(vpad_done, 1)

            def gates(step, u, read):
                pool.wait_ge(eg_out, step - NS + 1)
                if read is not None:
                    pool.wait_ge(heads_done, read)
                pool.tensor_tensor(eg[u][:], egraw[:, u * T:(u + 1) * T], spread_over(ones_sq, [[P, P], [0, 2], [1, P]]),
                                   ALU.add).then_inc(eg_done, 1)

            pool.wait_ge(consts, 7)
            power(0)
            low(0)
            pad(0, 0, None)
            pad(0, 1, None)
            pool.wait_ge(key_done, H // 2)
            pool.tensor_tensor(btab[:, :, 0:P], btab[:, :, P:2 * P], spread_over(ones_sq, [[P, P], [0, H], [1, P]]),
                               ALU.mult).then_inc(table_copied, 1)

            def body(s, first, last):
                if last:
                    return
                power(s + 1)
                low(s + 1)
                pad(s + 1, 0, 8 * s + 4)
                pad(s + 1, 1, 8 * s + 8)
            steps(pool, body)

            power(NS)
            low(NS)
            pad(NS, 0, 8 * NS - 4)
            pad(NS, 1, 8 * NS)
            gates(NS, 0, None)
            gates(NS, 1, None)

            def body1(s, first, last):
                if last:
                    return
                power(s + 1)
                low(s + 1)
                pad(s + 1, 0, 8 * s + 4)
                gates(s + 1, 0, 2 * s + 1)
                pad(s + 1, 1, 8 * s + 8)
                gates(s + 1, 1, 2 * s + 2)
            steps(pool, body1, NS)

        @block.vector
        def _(dve):
            def tokens(step, t):
                if layer[0]:
                    return x1[:, t, :]
                return X[:, bass.ds(step * ST + t, 1), :].rearrange("p a d -> p (a d)")

            layer = [0]

            def moments_of(step):
                for t in range(ST):
                    dve.bn_stats(stats[:, t, :], tokens(step, t)).then_inc(stat_done, 1)
                dve.wait_ge(stat_done, (step + 1) * ST)
                dve.memset(unused[:, 8:9], 0.0)
                for t in range(ST):
                    dve.bn_aggr(moments[:, t, :], stats[:, t, :]).then_inc(mom_done, 1)
                dve.wait_ge(mom_done, (step + 1) * ST)
                dve.tensor_scalar(var_eps[:], moments[:, :, 1], EPS, None, ALU.add).then_inc(var_done, 1)

            def normalise(step):
                dve.wait_ge(pow_done, step + 1)
                dve.tensor_tensor(newton[:], rstd0[:], rstd0[:], ALU.mult).then_inc(newt, 1)
                dve.wait_ge(newt, 4 * step + 1)
                dve.tensor_tensor(newton[:], newton[:], var_eps[:], ALU.mult).then_inc(newt, 1)
                dve.wait_ge(newt, 4 * step + 2)
                dve.tensor_scalar(newton[:], newton[:], -0.5, 1.5, ALU.mult, ALU.add).then_inc(newt, 1)
                dve.wait_ge(newt, 4 * step + 3)
                dve.tensor_tensor(rstd[:], rstd0[:], newton[:], ALU.mult).then_inc(newt, 1)
                dve.wait_ge(newt, 4 * step + 4)
                for t in range(ST):
                    last = dve.tensor_scalar(xn[:, t, :], tokens(step, t),
                                             moments[:, t, 0:1], rstd[:, t:t + 1], ALU.subtract, ALU.mult)
                last.then_inc(xn_done, 1)

            def split(step):
                for n, (w, ps) in enumerate((("q", psA), ("k", psB))):
                    dve.wait_ge(hi_done, 2 * step + n + 1)
                    if layer[0]:
                        dve.scalar_tensor_tensor(out=rest[w][:], in0=ps[:], scalar=bqkg[:, n:n + 1], in1=parts[w][0][:],
                                                 op0=ALU.add, op1=ALU.subtract).then_inc(rest_done, 1)
                    else:
                        dve.tensor_tensor(rest[w][:], ps[:], parts[w][0][:], ALU.subtract).then_inc(rest_done, 1)
                    dve.wait_ge(rest_done, 2 * step + n + 1)
                    dve.tensor_copy(parts[w][1][:], rest[w][:]).then_inc(mid_done, 1)

            def clip(s, u, q):
                dve.wait_ge(exp_done, 16 * s + 8 * u + 2 * q + 2)
                dve.scalar_tensor_tensor(out=probs[q][:, :, 0:2 * P], in0=probs[q][:, :, 0:2 * P], scalar=CLIP_LO,
                                         in1=bass.AP(tensor=diagcap[:].tensor, offset=diagcap[:].offset,
                                                     ap=[[2 * P, P], [0, 4], [1, 2 * P]]),
                                         op0=ALU.max, op1=ALU.min).then_inc(clipped, 1)
                dve.tensor_scalar(probs[q][:, :, 2 * P:QW], probs[q][:, :, 2 * P:QW], CLIP_LO, CLIP_HI,
                                  ALU.max, ALU.min).then_inc(clipped, 1)

            def finish(u, n):
                dve.wait_ge(weighed, 4 * n + 4)
                if layer[0]:
                    dve.wait_ge(eg_done, n - B + 1)
                    dve.tensor_tensor(rden[:], psN[u][:, T:2 * T], eg[u][:], ALU.mult).then_inc(gated, 1)
                    dve.wait_ge(gated, n - B + 1)
                    dve.reciprocal(rden[:], rden[:]).then_inc(rden_done, 1)
                else:
                    dve.reciprocal(rden[:], psN[u][:, T:2 * T]).then_inc(rden_done, 1)
                dve.wait_ge(rden_done, n + 1)
                if not (isinstance(n, int) and n == 0):
                    dve.wait_ge(out_ps, n)
                dve.tensor_tensor(heads[:], psN[u][:, 0:T], rden[:], ALU.mult).then_inc(heads_done, 1)

            def add_out(u, n):
                dve.wait_ge(out_ps, n + 1)
                ps = psB if u else psA
                dst = X[:, bass.ds(2 * n, 2), :]
                dve.tensor_tensor(dst, dst, ps[:, 0:2 * D].rearrange("p (t d) -> p t d", t=2), ALU.add).then_inc(x_done, 1)

            dve.memset(ones_pad[:], 0.0).then_inc(ones_done, 1)
            dve.wait_ge(ones_done, 1)
            for j in range(4):
                last = dve.memset(ones_pad[:, j, DK * j:DK * (j + 1)], 1.0)
            last.then_inc(ones_done, 1)
            for e in range(E):
                last = dve.memset(rank8[:, e:e + 1], float(E - e))
            dve.memset(one_row[:], 1.0)
            dve.memset(combT[4 * E:4 * E + 1, :], 1.0)
            for u in range(2):
                last = dve.memset(ks[u][SROWS:MROWS, :, :], 1.0)
            last.then_inc(ones_done, 1)
            dve.memset(lines, MASKED).then_inc(lined, 1)
            dve.wait_ge(lined, 1)
            dve.wait_ge(pos_in, 16)
            run = 33
            dve.tensor_copy(lines[:, 0, T:T + run], pbT[:, 0:run])
            back = LINE - 1 - T
            dve.tensor_copy(lines[:, 1, back - run + 1:back + 1],
                            bass.AP(tensor=pbT[:].tensor, offset=pbT[:].offset + run - 1, ap=[[len(OFFSETS), H], [-1, run]]))
            for n in range(run, len(OFFSETS)):
                dve.tensor_copy(lines[:, 0, T + OFFSETS[n]:T + OFFSETS[n] + 1], pbT[:, n:n + 1])
                last = dve.tensor_copy(lines[:, 1, back - OFFSETS[n]:back - OFFSETS[n] + 1], pbT[:, n:n + 1])
            last.then_inc(lines_done, 1)
            dve.wait_ge(x_first, 16)
            moments_of(0)
            normalise(0)
            dve.wait_ge(masks_done, 4)
            split(0)
            for i in range(H // 2):
                dve.wait_ge(query_ps, i + 1)
                dve.tensor_copy(btabq[:, 2 * i:2 * i + 2, :], psS[1][:, i % 2, :].rearrange("p (h c) -> p h c", h=2)).then_inc(query_done, 1)

            def body(s, first, last):
                if not last:
                    if first:
                        dve.wait_ge(x_rest, 16)
                    moments_of(s + 1)
                clip(s, 0, 0)
                clip(s, 0, 1)
                if not first:
                    finish(1, 2 * s - 1)
                if not last:
                    normalise(s + 1)
                clip(s, 0, 2)
                if not first:
                    add_out(1, 2 * s - 1)
                clip(s, 0, 3)
                if not last:
                    split(s + 1)
                clip(s, 1, 0)
                clip(s, 1, 1)
                finish(0, 2 * s)
                clip(s, 1, 2)
                add_out(0, 2 * s)
                clip(s, 1, 3)
            steps(dve, body)

            count = [0]

            def link(instruction):
                count[0] += 1
                instruction.then_inc(routing, 1)
                dve.wait_ge(routing, count[0])

            def wide3(t):
                return spread_over(t, [[NT, P], [1, NT], [0, E]])

            def first_of(onehot, top, logits):
                ranks = spread_over(rank8, [[E, P], [0, NT], [1, E]])
                link(dve.tensor_tensor(onehot, logits, wide3(top), ALU.is_equal))
                link(dve.tensor_tensor(onehot, onehot, ranks, ALU.mult))
                link(dve.tensor_reduce(out=rs[3][:], in_=onehot, axis=AX.X, op=ALU.max))
                link(dve.tensor_tensor(onehot, onehot, wide3(rs[3]), ALU.is_equal))

            dve.wait_ge(logits_out, 2 * NS)
            link(dve.tensor_reduce(out=rs[0][:], in_=logit0[:], axis=AX.X, op=ALU.max))
            first_of(rt[0], rs[0], logit0[:])
            onehot_done_at = count[0]
            assert onehot_done_at == ONEHOT_AT
            link(dve.tensor_tensor(rt[1], logit0[:], wide3(rs[0]), ALU.subtract))
            dve.wait_ge(route_exp, 1)
            link(dve.tensor_reduce(out=rs[1][:], in_=rt[1], axis=AX.X, op=ALU.add))
            link(dve.reciprocal(rs[2][:], rs[1][:]))
            finish(1, B - 1)
            add_out(1, B - 1)
            dve.wait_ge(loc_ps, 1)
            totals = psB[:, 0:NT * E].rearrange("p (t e) -> p t e", e=E)
            dve.memset(rt[1][:, 0, :], 0.0)
            link(dve.tensor_copy(rt[1][:, 1:NT, :], totals[:, 0:NT - 1, :]))
            a, b, k = 1, 2, 1
            while k < NT:
                dve.tensor_copy(rt[b][:, 0:k, :], rt[a][:, 0:k, :])
                link(dve.tensor_tensor(rt[b][:, k:NT, :], rt[a][:, k:NT, :], rt[a][:, 0:NT - k, :], ALU.add))
                a, b, k = b, a, 2 * k
            link(dve.tensor_tensor(rt[b], psA[:, 0:NT * E].rearrange("p (t e) -> p t e", e=E), rt[a], ALU.add))
            link(dve.tensor_scalar(rt[b], rt[b], float(CAP), None, ALU.is_lt))
            link(dve.tensor_tensor(rt[b], rt[b], rt[0], ALU.mult))
            dve.tensor_tensor(comb[:], rt[b], wide3(rs[2]), ALU.mult).then_inc(comb_done, 1)
            dve.wait_ge(comb_done, 1)

            layer[0] = 1

            def pick(at):
                dve.tensor_copy(comb_s[:], comb[:, bass.ds(at * ST, ST), :]).then_inc(comb_s_done, 1)

            def experts(at, dst):
                dve.wait_ge(bias_ps, at + 1)
                if not (isinstance(at, int) and at == 0):
                    dve.wait_ge(x1_kept, 16 * at)
                dve.tensor_tensor(dst[:], psA[:].rearrange("p (t d) -> p t d", t=ST), X[:, bass.ds(at * ST, ST), :],
                                  ALU.add).then_inc(bias_added, 1)
                dve.wait_ge(bias_added, at + 1)
                for e in range(E):
                    ps = psA if e % 2 else psB
                    dve.wait_ge(mix_ps, E * at + e + 1)
                    if e > 0:
                        dve.wait_ge(mixed, E * at + e)
                    for t in range(ST):
                        last = dve.scalar_tensor_tensor(out=dst[:, t, :], in0=ps[:, t * D:(t + 1) * D],
                                                        scalar=comb_s[:, t, e:e + 1], in1=dst[:, t, :], op0=ALU.mult, op1=ALU.add)
                    last.then_inc(mixed, 1)
                dve.wait_ge(mixed, E * (at + 1))

            def add_bias(s, u, q):
                for half in range(2):
                    dve.wait_ge(scored, 16 * s + 8 * u + 2 * q + half + 1)
                    if half == 0:
                        dve.wait_ge(weighed, 8 * s + 4 * u + q - 3)
                    h = 8 * half + q
                    dve.tensor_tensor(probs[q][:, 2 * half:2 * half + 2, :], psS[half][:, :, 0:QW], btab[:, h:h + 5:4, :],
                                      ALU.add).then_inc(biased, 1)

            def maxima(n, q):
                for half in range(2):
                    dve.wait_ge(ranked, 8 * n + 2 * q + half + 1)
                    at = 2 * q + half
                    dve.memset(unused[:, at:at + 1], 0.0)
                    for i in range(2):
                        h = 4 * (2 * half + i) + q
                        dve.tensor_tensor_reduce(out=psS[half][:, i, 0:P], in0=psS[half][:, i, 0:P], in1=btabq[:, h, P:T], scale=1.0,
                                                 scalar=-3e38, op0=ALU.add, op1=ALU.max, accum_out=smax[:, 0, h:h + 1])
                        last = dve.tensor_tensor_reduce(out=psS[half][:, i, P:QW], in0=psS[half][:, i, P:QW], in1=btabq[:, h, :], scale=1.0,
                                                        scalar=-3e38, op0=ALU.add, op1=ALU.max, accum_out=smax[:, 1, h:h + 1])
                    last.then_inc(maxed, 1)

            def negate(n):
                dve.wait_ge(maxed, 8 * n + 8)
                if not (isinstance(n, int) and n == 0):
                    dve.wait_ge(negT_ps, n)
                dve.tensor_scalar(mparts[:, :, 0, :], smax[:], -1.0, None, ALU.mult).then_inc(neg_step, 1)
                dve.wait_ge(neg_step, 3 * n + 1)
                dve.scalar_tensor_tensor(out=mrest[:], in0=smax[:], scalar=-1.0, in1=mparts[:, :, 0, :], op0=ALU.mult,
                                         op1=ALU.subtract).then_inc(neg_step, 1)
                dve.wait_ge(neg_step, 3 * n + 2)
                dve.tensor_copy(mparts[:, :, 1, :], mrest[:]).then_inc(neg_step, 1)
                dve.wait_ge(neg_step, 3 * n + 3)
                dve.tensor_tensor(mparts[:, :, 2, :], mrest[:], mparts[:, :, 1, :], ALU.subtract).then_inc(neg_done, 1)

            dve.wait_ge(query_done, H // 2)
            dve.wait_ge(table_copied, 1)
            dve.wait_ge(wt1_done, WT1)
            pick(0)
            experts(0, x1)
            moments_of(NS)
            normalise(NS)
            split(NS)
            for q in range(4):
                maxima(0, q)
            negate(0)

            def body1(s, first, last):
                n = 2 * (s - NS)
                if not last:
                    pick(s - NS + 1)
                add_bias(s, 0, 0)
                add_bias(s, 0, 1)
                if not first:
                    finish(1, 2 * s - 1)
                    add_out_1(s - NS - 1)
                if not last:
                    experts(s - NS + 1, x1)
                    moments_of(s + 1)
                add_bias(s, 0, 2)
                if not last:
                    normalise(s + 1)
                add_bias(s, 0, 3)
                maxima(n + 1, 0)
                if not last:
                    split(s + 1)
                for q in range(1, 4):
                    maxima(n + 1, q)
                finish(0, 2 * s)
                add_out_0(s - NS)
                negate(n + 1)
                if not last:
                    for q in range(4):
                        maxima(n + 2, q)
                    negate(n + 2)
                for q in range(4):
                    add_bias(s, 1, q)

            def add_layer1(u, at):
                dve.wait_ge(out_ps, 2 * (at + NS) + u + 1)
                dve.wait_ge(x1_kept, 16 * (at + 1))
                ps = psB if u else psA
                dst = X[:, bass.ds(ST * at + 2 * u, 2), :]
                dve.tensor_tensor(dst, dst, ps[:, 0:2 * D].rearrange("p (t d) -> p t d", t=2), ALU.add).then_inc(x_done, 1)

            def add_out_0(at):
                add_layer1(0, at)

            def add_out_1(at):
                add_layer1(1, at)

            steps(dve, body1, NS)
            finish(1, 2 * B - 1)
            add_out_1(NS - 1)

            dve.wait_ge(logits_out, 4 * NS)
            link(dve.tensor_reduce(out=rs[0][:], in_=logit0[:], axis=AX.X, op=ALU.max))
            first_of(rt[0], rs[0], logit0[:])
            link(dve.scalar_tensor_tensor(out=rt[1].rearrange("p t e -> p (t e)"), in0=rt[0].rearrange("p t e -> p (t e)"),
                                          scalar=-1e38, in1=logit0[:].rearrange("p t e -> p (t e)"), op0=ALU.mult, op1=ALU.add))
            link(dve.tensor_reduce(out=rs[1][:], in_=rt[1], axis=AX.X, op=ALU.max))
            first_of(rt[2], rs[1], rt[1])
            link(dve.tensor_tensor(rs[1][:], rs[1][:], rs[0][:], ALU.subtract))
            assert count[0] == SECOND_AT
            dve.wait_ge(route_exp, 2)
            link(dve.tensor_scalar(rs[0][:], rs[1][:], 1.0, None, ALU.add))
            link(dve.reciprocal(rs[2][:], rs[0][:]))
            link(dve.tensor_tensor(rs[1][:], rs[1][:], rs[2][:], ALU.mult))
            link(dve.tensor_tensor(rt[0], rt[0], wide3(rs[2]), ALU.mult))
            link(dve.tensor_tensor(rt[2], rt[2], wide3(rs[1]), ALU.mult))
            dve.tensor_tensor(comb[:], rt[0], rt[2], ALU.add).then_inc(comb_done, 1)
            dve.wait_ge(comb_done, 2)

            def body2(s, first, last):
                if not first:
                    dve.wait_ge(y_used, (E + 1) * s)
                dve.tensor_copy(comb_s[:], comb[:, bass.ds(s * ST, ST), :]).then_inc(comb_s_done, 1)
                dve.wait_ge(bias_ps, NS + s + 1)
                if not first:
                    dve.wait_ge(stored, 16 * s)
                dve.tensor_tensor(acc[0][:], psA[:].rearrange("p (t d) -> p t d", t=ST), X[:, bass.ds(s * ST, ST), :],
                                  ALU.add).then_inc(bias_added, 1)
                dve.wait_ge(bias_added, NS + s + 1)
                for i in range(E + 1):
                    y = y_banks[i % 3]
                    dve.wait_ge(y_ps, (E + 1) * s + i + 1)
                    if i == 0:
                        dve.tensor_tensor(acc[0][:], acc[0][:], y[:].rearrange("p (t d) -> p t d", t=ST), ALU.add).then_inc(y_used, 1)
                        dve.wait_ge(y_used, (E + 1) * s + 1)
                        continue
                    if i > 1:
                        dve.wait_ge(y_used, (E + 1) * s + i)
                    for t in range(ST):
                        last_one = dve.scalar_tensor_tensor(out=acc[0][:, t, :], in0=y[:, t * D:(t + 1) * D],
                                                            scalar=comb_s[:, t, i - 1:i], in1=acc[0][:, t, :], op0=ALU.mult, op1=ALU.add)
                    last_one.then_inc(y_used, 1)
            steps(dve, body2)

        @block.scalar
        def _(act):
            act.wait_ge(wt_ps, 1)
            act.activation(wT0[:].rearrange("p c d -> p (c d)"), psA[:], ACT.Copy).then_inc(wt_done, 1)
            act.wait_ge(wt_done, 1)
            act.wait_ge(w_in, 48)
            act.activation(wv0[:, 0:P], wT0[:, 2, :], ACT.Copy).then_inc(wt_done, 1)

            def turn(step, first):
                act.wait_ge(xn_turned, step + 1)
                if not first:
                    act.wait_ge(v_ps, 2 * step)
                    act.wait_ge(xnT_kept, 16 * step)
                act.activation(xnT[:], psA[:], ACT.Copy).then_inc(xnT_done, 1)

            def project(step, first):
                if not first:
                    act.wait_ge(scratch_in, 96 * step)
                act.wait_ge(q_ps, step + 1)
                if layer[0]:
                    act.activation(parts["q"][0][:], psA[:], ACT.Identity, bias=bqkg[:, 0:1]).then_inc(hi_done, 1)
                else:
                    act.activation(parts["q"][0][:], psA[:], ACT.Copy).then_inc(hi_done, 1)
                act.wait_ge(k_ps, step + 1)
                if layer[0]:
                    act.activation(parts["k"][0][:], psB[:], ACT.Identity, bias=bqkg[:, 1:2]).then_inc(hi_done, 1)
                else:
                    act.activation(parts["k"][0][:], psB[:], ACT.Copy).then_inc(hi_done, 1)

            def values_out(step, first):
                if not first:
                    act.wait_ge(vpad_done, 2 * step)
                for n, ps in enumerate((psB, psA) if layer[0] else (psA, psB)):
                    act.wait_ge(v_ps, 2 * step + n + 1)
                    v = ps[:, 0:2 * (P + E)].rearrange("p (t c) -> p t c", t=2)
                    act.activation(vraw[:, 2 * n:2 * n + 2, :], v[:, :, 0:P], ACT.Copy).then_inc(v_out, 1)
                    act.activation(logit0[:, bass.ds((step - NS * layer[0]) * ST + 2 * n, 2), :], v[:, :, P:P + E], ACT.Copy).then_inc(logits_out, 1)

            def exps(s, u, q, first):
                for half in range(2):
                    act.wait_ge(scored, 16 * s + 8 * u + 2 * q + half + 1)
                    if half == 0 and not (first and u == 0):
                        act.wait_ge(weighed, 8 * s + 4 * u + q - 3)
                    act.activation(probs[q][:, 2 * half:2 * half + 2, :], psS[half][:, :, 0:QW], ACT.Exp,
                                   scale=SCALE).then_inc(exp_done, 1)
            layer = [0]
            turn(0, True)
            project(0, True)
            values_out(0, True)
            act.wait_ge(wt1_ps, 1)
            act.activation(w0T[:, 0:4, :].rearrange("p c d -> p (c d)"), psA[:], ACT.Copy).then_inc(wt1_done, 1)
            act.wait_ge(wt1_ps, 2)
            act.activation(w0T[:, 4:8, :].rearrange("p c d -> p (c d)"), psB[:], ACT.Copy).then_inc(wt1_done, 1)
            act.wait_ge(wt1_ps, 3)
            act.activation(wT1[:, 0, :], psA[:, 0:P], ACT.Copy, scale=SCALE).then_inc(wt1_done, 1)
            act.activation(wT1[:, 1:4, :].rearrange("p c d -> p (c d)"), psA[:, P:4 * P], ACT.Copy).then_inc(wt1_done, 1)
            act.activation(wv1[:, 0:P], psA[:, 2 * P:3 * P], ACT.Copy).then_inc(wt1_done, 1)
            act.wait_ge(wt1_ps, 4)
            act.activation(wT1[:, 4, :], psB[:, 0:P], ACT.Copy)
            nb = E * HC + HC
            act.activation(bcol[:], psB[:, P:P + nb + 3], ACT.Copy)
            act.activation(bqkg[:, 0:1], psB[:, P + nb:P + nb + 1], ACT.Copy, scale=SCALE)
            act.activation(bqkg[:, 1:2], psB[:, P + nb + 1:P + nb + 2], ACT.Copy)
            act.activation(bqkg[:, 2:3], psB[:, P + nb + 2:P + nb + 3], ACT.Copy, scale=-1.0).then_inc(wt1_done, 1)
            for i in range(H // 2):
                act.wait_ge(key_ps, i + 1)
                act.activation(btab[:, 2 * i:2 * i + 2, P:QW], psS[0][:, i % 2, :].rearrange("p (h c) -> p h c", h=2),
                               ACT.Copy).then_inc(key_done, 1)

            def body(s, first, last):
                exps(s, 0, 0, first)
                exps(s, 0, 1, first)
                exps(s, 0, 2, first)
                if not last:
                    turn(s + 1, False)
                exps(s, 0, 3, first)
                if not last:
                    project(s + 1, False)
                exps(s, 1, 0, first)
                if not last:
                    values_out(s + 1, False)
                for q in range(1, 4):
                    exps(s, 1, q, first)
            steps(act, body)
            act.wait_ge(routing, SHIFTED_AT)
            act.activation(rt[1], rt[1], ACT.Exp).then_inc(route_exp, 1)

            layer[0] = 1

            def combT_out(n):
                act.wait_ge(combT_ps, n + 1)
                if not (isinstance(n, int) and n == 0):
                    act.wait_ge(bias_ps, n)
                act.activation(combT[0:4 * E, :], psA[0:4 * E, 0:P], ACT.Copy).then_inc(combT_done, 1)

            def gate_out(step, first):
                act.wait_ge(gate_ps, step - NS + 1)
                if not first:
                    act.wait_ge(eg_done, 2 * (step - NS))
                act.activation(egraw[:], psA[:], ACT.Exp, scale=-1.0, bias=bqkg[:, 2:3]).then_inc(eg_out, 1)

            def maxima_out(u, n, step):
                act.wait_ge(negT_ps, n + 1)
                if step is not None:
                    act.wait_ge(m_in[1 - u], 48 * (step - NS + 1))
                act.activation(mT[:], psB[0:3 * H, 0:T], ACT.Copy).then_inc(negT_done, 1)

            def exps1(s, u, q):
                act.wait_ge(biased, 16 * (s - NS) + 8 * u + 2 * q + 2)
                act.activation(probs[q][:], probs[q][:], ACT.Exp).then_inc(exp1_done, 1)

            combT_out(0)
            turn(NS, False)
            project(NS, False)
            gate_out(NS, True)
            values_out(NS, False)
            maxima_out(0, 0, None)

            def body1(s, first, last):
                exps1(s, 0, 0)
                exps1(s, 0, 1)
                if not last:
                    combT_out(s - NS + 1)
                exps1(s, 0, 2)
                if not last:
                    turn(s + 1, False)
                exps1(s, 0, 3)
                if not last:
                    project(s + 1, False)
                    gate_out(s + 1, False)
                    values_out(s + 1, False)
                maxima_out(1, 2 * (s - NS) + 1, s)
                if not last:
                    maxima_out(0, 2 * (s - NS) + 2, s)
                for q in range(4):
                    exps1(s, 1, q)
            steps(act, body1, NS)

            act.wait_ge(routing, SECOND_AT)
            act.activation(rs[1][:], rs[1][:], ACT.Exp).then_inc(route_exp, 1)

            def body2(s, first, last):
                for i in range(E + 1):
                    n = (E + 1) * s + i
                    h = wide[i % 3][:].rearrange("p (c n) -> p c n", c=HC)
                    at = E * HC if i == 0 else HC * (i - 1)
                    for c in range(HC):
                        act.wait_ge(hid_ps, HC * n + c + 1)
                        if c == 0 and not (first and i < 3):
                            act.wait_ge(y_ps, n - 2)
                        act.activation(h[:, c, :], psS[c // 2][:, c % 2, :], ACT.Gelu, bias=bcol[:, at + c:at + c + 1])\
                            .then_inc(gelu_done, 1)
                    if i == 1:
                        combT_out(NS + s)
            steps(act, body2)


        @block.tensor
        def _(pe):
            pe.wait_ge(masks_done, 4)
            pe.wait_ge(consts, 7)
            pe.wait_ge(w_in, 48)
            for c in range(4):
                last = pe.transpose(psA[:, c * P:(c + 1) * P], wraw[:, c, :], ident[:])
            last.then_inc(wt_ps, 1)

            def turn(step):
                pe.wait_ge(xn_done, step + 1)
                for t in range(ST):
                    last = pe.transpose(psA[:, t * P:(t + 1) * P], xn[:, t, :], ident[:])
                last.then_inc(xn_turned, 1)

            def project(step):
                pe.wait_ge(xnT_done, step + 1)
                w = wT1 if layer[0] else wT0
                pe.matmul(psA[:], w[:, 0, :], xnT[:], start=True, stop=True).then_inc(q_ps, 1)
                pe.matmul(psB[:], w[:, 1, :], xnT[:], start=True, stop=True).then_inc(k_ps, 1)

            def values(step):
                for n, ps in ((0, psA), (1, psB)):
                    pe.wait_ge(rest_done, 2 * step + n + 1)
                    for t in range(2):
                        last = pe.matmul(ps[:, t * (P + E):(t + 1) * (P + E)], xnT[:, (2 * n + t) * P:(2 * n + t + 1) * P],
                                         wv0[:], start=True, stop=True)
                    last.then_inc(v_ps, 1)

            def values_read(n):
                pe.wait_ge(v_out, n)
                pe.wait_ge(logits_out, n)

            def score(s, u, q, first):
                if q == 0:
                    pe.wait_ge(qk_in[u], 192 * (s + 1))
                    if layer[0]:
                        pe.wait_ge(m_in[u], 48 * (s - NS + 1))
                rows = MROWS if layer[0] else SROWS
                for half in range(2):
                    if layer[0]:
                        bank_free1(s, u, q, half, first)
                    elif not (first and u == 0 and q == 0):
                        pe.wait_ge(exp_done, 16 * s + 8 * u + 2 * q + half - 1)
                    for i in range(2):
                        h = 4 * (2 * half + i) + q
                        pe.matmul(psS[half][:, i, 0:P], ks[u][0:rows, h, P:T], qs[u][0:rows, h, P:T], start=True, stop=True)
                        last = pe.matmul(psS[half][:, i, P:QW], ks[u][0:rows, h, 0:P], qs[u][0:rows, h, :], start=True, stop=True)
                    last.then_inc(scored, 1)

            def weigh(s, u, q, first):
                if layer[0]:
                    pe.wait_ge(exp1_done, 8 * (s - NS) + 4 * u + q + 1)
                else:
                    pe.wait_ge(clipped, 2 * (8 * s + 4 * u + q + 1))
                if q == 0:
                    pe.wait_ge(vpad_done, 2 * s + u + 1)
                    if not first:
                        pe.wait_ge(heads_done, 2 * s + u - 1)
                for part, at in ((0, 0), (1, T)):
                    for kt, cols, to in ((0, (P, QW), (0, T)), (1, (0, P), (P, T))):
                        for g in range(4):
                            w = vpad[u][:, kt, 4 * g + q, :] if part == 0 else ones_pad[:, q, :]
                            last = pe.matmul(psN[u][VW * g:VW * (g + 1), at + to[0]:at + to[1]], w,
                                             probs[q][:, g, cols[0]:cols[1]],
                                             start=(q == 0 and part == 0 and kt == 0), stop=(q == 3 and kt == 1),
                                             skip_group_check=True)
                last.then_inc(weighed, 1)

            def out_project(u, n):
                pe.wait_ge(heads_done, n + 1)
                ps = psB if u else psA
                for t in range(2):
                    last = pe.matmul(ps[:, t * D:(t + 1) * D], heads[:, t * P:(t + 1) * P], (wT1 if layer[0] else wT0)[:, 3, :],
                                     start=True, stop=not layer[0])
                    if layer[0]:
                        last = pe.matmul(ps[:, t * D:(t + 1) * D], one_row[:], bias_o[:], start=False, stop=True)
                last.then_inc(out_ps, 1)

            layer = [0]
            pe.wait_ge(wt_done, 2)
            turn(0)
            project(0)
            values(0)
            pe.wait_ge(late_in, 16 * LATE)
            values_read(1)
            for e in range(4):
                last = pe.transpose(psA[:, e * P:(e + 1) * P], acc[0][:, e, :], ident[:])
            last.then_inc(wt1_ps, 1)
            values_read(2)
            for e in range(4):
                last = pe.transpose(psB[:, e * P:(e + 1) * P], acc[1][:, e, :], ident[:])
            last.then_inc(wt1_ps, 1)
            pe.wait_ge(wt1_done, 1)
            for c in range(4):
                last = pe.transpose(psA[:, c * P:(c + 1) * P], wraw1[:, c, :], ident[:])
            last.then_inc(wt1_ps, 1)
            pe.wait_ge(wt1_done, 2)
            pe.transpose(psB[:, 0:P], wraw1[:, 4, :], ident[:])
            nb = E * HC + HC + 3
            pe.transpose(psB[:, P:P + nb], brow, ident[0:nb, 0:nb]).then_inc(wt1_ps, 1)
            pe.wait_ge(tables_in, 32)
            for i in range(H // 2):
                for half, tab, sent, kept in ((0, btab[:, :, P:QW], key_ps, key_done), (1, btabq, query_ps, query_done)):
                    if i >= 2:
                        pe.wait_ge(kept, i - 1)
                    pe.matmul(psS[half][:, i % 2, :], flip[:], tab[:, 2 * i:2 * i + 2, :], start=True, stop=True).then_inc(sent, 1)
            pe.wait_ge(key_done, H // 2)
            pe.wait_ge(query_done, H // 2)
            pe.wait_ge(wt1_done, WT1)
            pe.wait_ge(ones_done, 3)

            def body(s, first, last):
                score(s, 0, 0, first)
                if not first:
                    weigh(s - 1, 1, 2, False)
                score(s, 0, 1, first)
                if not first:
                    weigh(s - 1, 1, 3, False)
                score(s, 0, 2, first)
                weigh(s, 0, 0, first)
                values_read(2 * s + 2)
                if not first:
                    out_project(1, 2 * s - 1)
                if not last:
                    if not first:
                        pe.wait_ge(x_done, 2 * s - 1)
                    turn(s + 1)
                score(s, 0, 3, first)
                weigh(s, 0, 1, first)
                if not last:
                    if not first:
                        pe.wait_ge(x_done, 2 * s)
                    project(s + 1)
                score(s, 1, 0, first)
                weigh(s, 0, 2, first)
                if not last:
                    values(s + 1)
                score(s, 1, 1, first)
                weigh(s, 0, 3, first)
                score(s, 1, 2, first)
                weigh(s, 1, 0, first)
                if not last:
                    values_read(2 * s + 3)
                out_project(0, 2 * s)
                score(s, 1, 3, first)
                weigh(s, 1, 1, first)
            steps(pe, body)
            weigh(NS - 1, 1, 2, False)
            weigh(NS - 1, 1, 3, False)
            out_project(1, B - 1)

            pe.wait_ge(routing, ONEHOT_AT)
            pe.wait_ge(x_done, B)
            flat = rt[0].rearrange("p t e -> p (t e)")
            pe.matmul(psA[:, 0:NT * E], upper[:], flat, start=True, stop=True)
            pe.matmul(psB[:, 0:NT * E], ones_sq[:], flat, start=True, stop=True).then_inc(loc_ps, 1)

            layer[0] = 1

            def bank_free1(s, u, q, half, first):
                n = 16 * (s - NS)
                if q > 0:
                    pe.wait_ge(biased, n + 8 * u + 2 * q + half - 1)
                elif u == 0 and not first:
                    pe.wait_ge(biased, n + half - 1)
                elif u == 0:
                    pe.wait_ge(maxed, 7 + half)
                else:
                    pe.wait_ge(maxed, n + 16 + (0 if last_step[0] else 8) - 1 + half)

            last_step = [False]

            def rank(n, u, q, free, first=False):
                if q == 0:
                    pe.wait_ge(qk_in[u], free[2])
                for half in range(2):
                    if q > 0:
                        pe.wait_ge(maxed, 8 * n + 2 * q + half - 1)
                    else:
                        pe.wait_ge(free[0], free[1] + half)
                    for i in range(2):
                        h = 4 * (2 * half + i) + q
                        pe.matmul(psS[half][:, i, 0:P], qs[u][0:SROWS, h, 0:P], ks[u][0:SROWS, h, 0:P], start=True, stop=True)
                        last = pe.matmul(psS[half][:, i, P:QW], qs[u][0:SROWS, h, P:T], ks[u][0:SROWS, h, :], start=True, stop=True)
                    last.then_inc(ranked, 1)

            def turn_maxima(n):
                pe.wait_ge(neg_done, n + 1)
                if isinstance(n, int) and n == 0:
                    values_read(2 * NS + 2)
                else:
                    pe.wait_ge(negT_done, n)
                for qt in range(2):
                    last = pe.matmul(psB[0:3 * H, qt * P:(qt + 1) * P],
                                     mparts[:, qt, :, :].rearrange("p a h -> p (a h)"), ident16[:], start=True, stop=True)
                last.then_inc(negT_ps, 1)

            def bias_and_comb(n, w):
                pe.wait_ge(comb_s_done, n + 1)
                pe.transpose(psA[0:4 * E, 0:P], comb_s[:].rearrange("p t e -> p (t e)"), ident[:]).then_inc(combT_ps, 1)
                pe.wait_ge(combT_done, n + 1)
                rows = 4 * E + (w is bdiag1)
                pe.matmul(psA[:], combT[0:rows, :], w[:].rearrange("k t d -> k (t d)"), start=True, stop=True).then_inc(bias_ps, 1)

            def experts(at):
                bias_and_comb(at, bdiag0)
                pe.wait_ge(stat_in, 16 * (at + 1))
                for e in range(E):
                    ps = psA if e % 2 else psB
                    if e == 1:
                        pe.wait_ge(bias_added, at + 1)
                    elif e > 1:
                        pe.wait_ge(mixed, E * at + e - 1)
                    for t in range(ST):
                        last = pe.matmul(ps[:, t * D:(t + 1) * D], xstat[:, t * P:(t + 1) * P], w0T[:, e, :], start=True, stop=True)
                    last.then_inc(mix_ps, 1)

            def gate(step):
                pe.wait_ge(rest_done, 2 * step + 1)
                pe.matmul(psA[:], wT1[:, 4, :], xnT[:], start=True, stop=True).then_inc(gate_ps, 1)

            def values1(step):
                for n, ps in ((0, psB), (1, psA)):
                    if n == 0:
                        pe.wait_ge(rest_done, 2 * step + 2)
                    else:
                        pe.wait_ge(eg_out, step - NS + 1)
                    for t in range(2):
                        o = ps[:, t * (P + E):(t + 1) * (P + E)]
                        pe.matmul(o, xnT[:, (2 * n + t) * P:(2 * n + t + 1) * P], wv1[:], start=True, stop=False)
                        last = pe.matmul(o, one_row[:], bias_v[:], start=False, stop=True)
                    last.then_inc(v_ps, 1)

            pe.wait_ge(wt1_done, WT1)
            pe.wait_ge(later_in, 16 * LATER)
            pe.wait_ge(comb_done, 1)
            experts(0)
            pe.wait_ge(mixed, E)
            turn(NS)
            project(NS)
            gate(NS)
            values1(NS)
            for q in range(4):
                rank(0, 0, q, (exp_done, 16 * NS - 1, 192 * (NS + 1)))
            turn_maxima(0)

            def body1(s, first, last):
                at, n = s - NS, 2 * (s - NS)
                last_step[0] = last
                score(s, 0, 0, first)
                if not first:
                    weigh(s - 1, 1, 2, False)
                score(s, 0, 1, first)
                if not first:
                    weigh(s - 1, 1, 3, False)
                    pe.wait_ge(negT_done, n + 1)
                    out_project(1, 2 * s - 1)
                    pe.wait_ge(x_done, 2 * s)
                if not last:
                    if not first:
                        pe.wait_ge(x_done, 2 * s - 1)
                    else:
                        pe.wait_ge(negT_done, 1)
                    experts(at + 1)
                score(s, 0, 2, first)
                weigh(s, 0, 0, False)
                if not last:
                    pe.wait_ge(mixed, E * (at + 2))
                    turn(s + 1)
                score(s, 0, 3, first)
                weigh(s, 0, 1, False)
                if not last:
                    project(s + 1)
                rank(n + 1, 1, 0, (biased, 16 * at + 7, 192 * (s + 1)))
                weigh(s, 0, 2, False)
                if not last:
                    gate(s + 1)
                    values1(s + 1)
                rank(n + 1, 1, 1, None)
                weigh(s, 0, 3, False)
                rank(n + 1, 1, 2, None)
                rank(n + 1, 1, 3, None)
                if not last:
                    values_read(2 * s + 4)
                else:
                    values_read(2 * s + 2)
                out_project(0, 2 * s)
                turn_maxima(n + 1)
                if not last:
                    for q in range(4):
                        rank(n + 2, 0, q, (maxed, 8 * n + 15, 192 * (s + 2)))
                    turn_maxima(n + 2)
                for q in range(4):
                    score(s, 1, q, first)
                    if q >= 2:
                        weigh(s, 1, q - 2, False)
            steps(pe, body1, NS)
            weigh(2 * NS - 1, 1, 2, False)
            weigh(2 * NS - 1, 1, 3, False)
            out_project(1, 2 * B - 1)

            def hidden(s, i, first):
                n = (E + 1) * s + i
                if first and i >= 1 and i % 2:
                    pe.wait_ge(w_exp_in[i // 2], 48)
                for c in range(HC):
                    if not (first and i == 0):
                        pe.wait_ge(gelu_done, HC * n + c - HC + 1)
                    else:
                        pe.wait_ge(biased, 16 * NS)
                    w = ws1_sb[:, c * P:(c + 1) * P] if i == 0 else w1_sb[:, i - 1, c * P:(c + 1) * P]
                    pe.matmul(psS[c // 2][:, c % 2, :], w, XNT[:, bass.ds(s * SC, SC)], start=True, stop=True).then_inc(hid_ps, 1)

            def outputs(s, i, first):
                n = (E + 1) * s + i
                h = wide[i % 3][:].rearrange("p (c n) -> p c n", c=HC)
                if not (first and i < 3):
                    pe.wait_ge(y_used, n - 2)
                pe.wait_ge(gelu_done, HC * (n + 1))
                for t in range(ST):
                    for c in range(HC):
                        w = ws2_sb[:, c, :] if i == 0 else w2_sb[:, i - 1, c, :]
                        last = pe.matmul(y_banks[i % 3][:, t * D:(t + 1) * D], h[:, c, t * P:(t + 1) * P], w,
                                         start=(c == 0), stop=(c == HC - 1))
                last.then_inc(y_ps, 1)

            pe.wait_ge(xnT_kept, 32 * NS)
            pe.wait_ge(heads_done, 2 * B)
            pe.wait_ge(x_done, 2 * B)

            def body2(s, first, last):
                hidden(s, 0, first)
                for i in range(1, E + 1):
                    hidden(s, i, first)
                    outputs(s, i - 1, first)
                    if i == 1:
                        pe.wait_ge(bias_added, NS + s)
                        bias_and_comb(NS + s, bdiag1)
                outputs(s, E, first)
            steps(pe, body2)


_INS = ["L0_attn_x", "L0_attn_Wqkv", "L0_attn_Wout", "L0_ffn_wg", "L0_ffn_W", "L0_ffn_b", "L1_attn_Wqkv", "L1_attn_bqkv",
        "L1_attn_Wout", "L1_attn_bout", "L1_attn_Wgate", "L1_attn_bgate", "L1_attn_pos_bias", "L1_ffn_gate_w",
        "L1_ffn_gate_b", "L1_ffn_w1", "L1_ffn_b1", "L1_ffn_w2", "L1_ffn_b2", "L1_ffn_ws1", "L1_ffn_bs1", "L1_ffn_ws2",
        "L1_ffn_bs2"]


def kernel(**inputs):
    import numpy as np
    import concourse.bacc as bacc
    from concourse.bass_utils import run_bass_kernel_spmd as run

    nc = bacc.Bacc("TRN2", target_bir_lowering=False, num_devices=1)
    arrays, args = {}, []
    for name in _INS:
        a = np.ascontiguousarray(inputs[name])
        arrays[f"in_{name}"] = a
        args.append(nc.dram_tensor(f"in_{name}", a.shape, mybir.dt.from_np(a.dtype), kind="ExternalInput").ap())
    args.append(nc.dram_tensor("out_x", (B, T, D), F32, kind="ExternalOutput").ap())
    build(nc, *args)
    r = run(nc, [arrays], core_ids=[0])
    return r.results[0]["out_x"]
```

```python
from contextlib import ExitStack

import concourse.bass as bass
from concourse import mybir

F32 = mybir.dt.float32
BF16 = mybir.dt.bfloat16
I32 = mybir.dt.int32
ALU = mybir.AluOpType
ACT = mybir.ActivationFunctionType
AX = mybir.AxisListType

P = 128
B, T, D = 16, 256, 128
H, DK = 16, 8
NT = B * T // P
ST = 4
NS = NT // ST
SC = ST * P
E = 8
CAP = B * T // E
TERMS = 6
Q_PARTS = (0, 0, 0, 1, 1, 2)
K_PARTS = (0, 1, 2, 0, 1, 0)
SROWS = 96
MROWS = 99
EPS = 1e-5
SCALE = DK ** -0.5
CLIP_HI = 22026.465794806718
CLIP_LO = 4.5399929762484854e-05
QW = 384
VW = 32


OFFSETS = tuple(range(33)) + (48, 64, 96, 128, 192)
MASKED = -1e30
LINE = 640
HID = 512
HC = HID // P
LW = 4 * P
SLOTS = 2 * P
BLOCKS = 2 * B * T // SLOTS + E
FRONT = NS // 2


def build(nc, x, wqkv0, wout0, wg0, w_exp0, b_exp0, wqkv1, bqkv1, wout1, bout1, wgate1, bgate1, pos_bias,
          gate_w, gate_b, w1, b1, w2, b2, ws1, bs1, ws2, bs2, out):
    scr_q = nc.dram_tensor("scr_q", (3, P, SC), BF16, kind="Internal").ap()
    scr_k = nc.dram_tensor("scr_k", (3, P, SC), BF16, kind="Internal").ap()
    scr_line = nc.dram_tensor("scr_line", (2, H, LINE), F32, kind="Internal").ap()
    scr_x = nc.dram_tensor("scr_x", (2 * NS, P, SC), F32, kind="Internal").ap()
    x_slots = nc.dram_tensor("x_slots", (BLOCKS * SLOTS, D), F32, kind="Internal").ap()
    y_slots = nc.dram_tensor("y_slots", (BLOCKS * SLOTS, D), F32, kind="Internal").ap()
    ctx = ExitStack()
    with ctx:
        def sb(name, shape, dt=F32):
            return ctx.enter_context(nc.sbuf_tensor(name, shape, dt))

        def sem(name):
            return ctx.enter_context(nc.semaphore(name))

        X = sb("X", [P, NT, D])
        XN = sb("XN", [P, NT, D])
        logit0 = sb("logit0", [P, NT, E])
        ident = sb("ident", [P, P])
        ident16 = sb("ident16", [P, P], BF16)
        flip = sb("flip", [P, P])
        diagcap = sb("diagcap", [P, 2 * P])
        wT1 = sb("wT1", [P, 5, P])
        wv1 = sb("wv1", [P, P + E])
        w0T = sb("w0T", [P, E, P])
        bcol = sb("bcol", [P, E * HC + HC + 3])
        bqkg = sb("bqkg", [P, 3])
        one_row = sb("one_row", [1, P])
        bias_v = sb("bias_v", [1, P + E])
        bias_o = sb("bias_o", [1, P])
        bdiag0 = sb("bdiag0", [4 * E, ST, D])
        bdiag1 = sb("bdiag1", [4 * E + 1, ST, D])
        upper = sb("upper", [P, P])
        ones_sq = sb("ones_sq", [P, P])
        rank8 = sb("rank8", [P, E])
        tables = sb("tables", [P, H * QW + H * T])
        btab = tables[:, 0:H * QW].rearrange("p (h c) -> p h c", h=H)
        btabq = tables[:, H * QW:H * (QW + T)].rearrange("p (h c) -> p h c", h=H)
        at, block_bufs = 0, {}
        for name, width in (("x", 2 * D), ("w1", HID), ("w2", HC * D), ("xT", SLOTS), ("y", 2 * D), ("b1", HC)):
            for u in range(2):
                block_bufs[name, u] = tables[:, at:at + width]
                at += width
        picked = tables[:, 0:2 * NT * D].rearrange("p (t k d) -> p t k d", k=2, d=D)
        ws1_sb = sb("ws1_sb", [P, HID])
        ws2_sb = sb("ws2_sb", [P, HC, D])
        pbT = sb("pbT", [H, len(OFFSETS)])
        lines = tables[0:H, 0:2 * LINE].rearrange("h (a c) -> h a c", a=2)
        slot0 = sb("slot0", [P, E])
        steps16 = sb("steps16", [P, B * T // SLOTS])
        numbers = sb("numbers", [P, BLOCKS])
        many = sb("many", [P, E, B * T // SLOTS])
        filled = sb("filled", [P, E])
        n_blocks = sb("n_blocks", [P, E])
        ends = [sb(f"ends{i}", [P, E]) for i in range(2)]
        passed = sb("passed", [P, BLOCKS, E])
        block_e = sb("block_e", [P, BLOCKS])
        block_at = sb("block_at", [P, BLOCKS], I32)
        slots_at = sb("slots_at", [P, 2, NT], I32)
        xstat = sb("xstat", [P, SC])
        wraw = xstat[:].rearrange("p (c n) -> p c n", c=4)
        comb = sb("comb", [P, NT, E])
        comb_s = sb("comb_s", [P, ST, E])
        combT = sb("combT", [4 * E + 1, P])
        acc = [sb(f"acc{i}", [P, ST, D]) for i in range(2)]
        x1 = acc[1]
        routes = sb("routes", [P, 3 * NT * E])
        rt = [routes[:, i * NT * E:(i + 1) * NT * E].rearrange("p (t e) -> p t e", e=E) for i in range(3)]
        rt += [xstat[:, i * NT * E:(i + 1) * NT * E].rearrange("p (t e) -> p t e", e=E) for i in range(2)]
        wraw1 = routes[:, 0:5 * P].rearrange("p (c n) -> p c n", c=5)
        rs = [sb(f"rs{i}", [P, NT]) for i in range(4)]
        egraw = sb("egraw", [P, SC])
        brow = egraw[0:E * HC + HC + 3, 0:P]
        eg = [sb(f"eg{u}", [P, T]) for u in range(2)]
        unused = sb("unused", [P, 9])
        smax = sb("smax", [P, 2, H])
        mrest = sb("mrest", [P, 2, H])
        mparts = sb("mparts", [P, 2, 3, H], BF16)
        mT = sb("mT", [3 * H, T], BF16)
        wT0 = sb("wT0", [P, 4, P])
        wv0 = sb("wv0", [P, P + E])
        stats = sb("stats", [P, ST, 6])
        moments = sb("moments", [P, ST, 2])
        var_eps = sb("var_eps", [P, ST])
        minus_half = sb("minus_half", [P, ST])
        rstd0 = sb("rstd0", [P, ST])
        newton = sb("newton", [P, ST])
        rstd = sb("rstd", [P, ST])
        xn = sb("xn", [P, ST, D])
        xnT = sb("xnT", [P, SC])
        parts = {}
        for w in "qk":
            parts[w] = [sb(f"{w}_hi", [P, SC], BF16), sb(f"{w}_mid", [P, SC], BF16), sb(f"{w}_lo", [P, SC], BF16)]
        rest = {w: sb(f"{w}_rest", [P, SC]) for w in "qk"}
        qs = [sb(f"qs{u}", [MROWS, H, T], BF16) for u in range(2)]
        ks = [sb(f"ks{u}", [MROWS, H, T], BF16) for u in range(2)]
        vraw = sb("vraw", [P, ST, D])
        vpad = [sb(f"vpad{u}", [P, 2, H, VW]) for u in range(2)]
        ones_pad = sb("ones_pad", [P, 4, VW])
        wide = [sb(f"wide{q}", [P, 4 * LW]) for q in range(4)]
        probs = [w[:, 0:4 * QW].rearrange("p (g c) -> p g c", g=4) for w in wide]
        rden = sb("rden", [P, T])
        heads = sb("heads", [P, T])

        psS = [ctx.enter_context(nc.psum_tensor(f"psS{i}", [P, 2, 512], F32)) for i in range(2)]
        psN = [ctx.enter_context(nc.psum_tensor(f"psN{i}", [P, 512], F32)) for i in range(2)]
        psA = ctx.enter_context(nc.psum_tensor("psA", [P, 512], F32))
        psB = ctx.enter_context(nc.psum_tensor("psB", [P, 512], F32))

        x_first, x_rest = sem("x_first"), sem("x_rest")
        w_in, wt_ps, wt_done, consts = sem("w_in"), sem("wt_ps"), sem("wt_done"), sem("consts")
        stat_done, mom_done, var_done, pow_done = sem("stat_done"), sem("mom_done"), sem("var_done"), sem("pow_done")
        newt, xn_done, xn_turned, xnT_done, xnT_kept = sem("newt"), sem("xn_done"), sem("xn_turned"), sem("xnT_done"), sem("xnT_kept")
        q_ps, k_ps, v_ps = sem("q_ps"), sem("k_ps"), sem("v_ps")
        hi_done, rest_done, mid_done, lo_done = sem("hi_done"), sem("rest_done"), sem("mid_done"), sem("lo_done")
        v_out, logits_out, vpad_done = sem("v_out"), sem("logits_out"), sem("vpad_done")
        scratch_in = sem("scratch_in")
        qk_in = [sem("qk_in0"), sem("qk_in1")]
        scored, exp_done, clipped, weighed = sem("scored"), sem("exp_done"), sem("clipped"), sem("weighed")
        rden_done, heads_done, out_ps, x_done = sem("rden_done"), sem("heads_done"), sem("out_ps"), sem("x_done")
        stored = sem("stored")
        masks_done, ones_done = sem("masks_done"), sem("ones_done")
        late_in, later_in, wt1_ps, wt1_done = sem("late_in"), sem("later_in"), sem("wt1_ps"), sem("wt1_done")
        lines_done, lines_in, tables_in = sem("lines_done"), sem("lines_in"), sem("tables_in")
        pos_in, key_ps, key_done = sem("pos_in"), sem("key_ps"), sem("key_done")
        query_ps, query_done, table_copied = sem("query_ps"), sem("query_done"), sem("table_copied")
        routing, loc_ps, route_exp, comb_done = sem("routing"), sem("loc_ps"), sem("route_exp"), sem("comb_done")
        stat_in, comb_s_done, combT_ps, combT_done = sem("stat_in"), sem("comb_s_done"), sem("combT_ps"), sem("combT_done")
        bias_ps, mix_ps, mixed, x1_kept = sem("bias_ps"), sem("mix_ps"), sem("mixed"), sem("x1_kept")
        gate_ps, eg_out, eg_done = sem("gate_ps"), sem("eg_out"), sem("eg_done")
        ranked, maxed, neg_done, negT_ps, negT_done = sem("ranked"), sem("maxed"), sem("neg_done"), sem("negT_ps"), sem("negT_done")
        neg_step, gated, lined, bias_added = sem("neg_step"), sem("gated"), sem("lined"), sem("bias_added")
        ONEHOT_AT, SHIFTED_AT, SECOND_AT, BOTH_AT = 5, 6, 30, 29
        WT1 = 6
        LATE, LATER = 9, 18
        m_in = [sem("m_in0"), sem("m_in1")]
        biased, exp1_done = sem("biased"), sem("exp1_done")
        xn_kept, both_ps, slots_done, table_done = sem("xn_kept"), sem("both_ps"), sem("slots_done"), sem("table_done")
        spare_in, slots_in = sem("spare_in"), sem("slots_in")
        x_in, w2_in, y_stored, picked_in = ([sem(f"{n}{u}") for u in range(2)] for n in ("x_in", "w2_in", "y_stored", "picked_in"))
        xb_turned, xb_done, b1_done, hidb_ps = sem("xb_turned"), sem("xb_done"), sem("b1_done"), sem("hidb_ps")
        gelub_done, yb_ps, yb_done, summed = sem("gelub_done"), sem("yb_ps"), sem("yb_done"), sem("summed")
        first_added = sem("first_added")
        hid_ps, gelu_done, y_ps, y_used = sem("hid_ps"), sem("gelu_done"), sem("y_ps"), sem("y_used")

        block = ctx.enter_context(nc.Block())

        def steps(engine, body, base=0):
            body(base, True, False)
            with engine.Fori(base + 1, base + NS - 1) as s:
                body(s, False, False)
            body(base + NS - 1, False, True)

        def spread_over(t, pattern):
            return bass.AP(tensor=t[:].tensor, offset=t[:].offset, ap=pattern)

        x_tiles = x.rearrange("b (t p) d -> p (b t) d", p=P)

        @block.sync
        def _(sp):
            sp.dma_start(X[:, 0:ST, :], x_tiles[:, 0:ST, :]).then_inc(x_first, 16)
            sp.dma_start(pbT[:], pos_bias.rearrange("o h -> h o"), allow_slow_non_contiguous=True).then_inc(pos_in, 16)
            sp.dma_start(wraw[:, 0:3, :], wqkv0.rearrange("(c p) d -> p c d", p=P)).then_inc(w_in, 16)
            sp.dma_start(wraw[:, 3, :], wout0).then_inc(w_in, 16)
            sp.dma_start(wv0[:, P:P + E], wg0).then_inc(w_in, 16)
            sp.dma_start(X[:, ST:NT, :], x_tiles[:, ST:NT, :]).then_inc(x_rest, 16)

            layer = [0]

            def late(dst, src):
                sp.dma_start(dst, src).then_inc(late_in, 16)

            def later(dst, src):
                sp.dma_start(dst, src).then_inc(later_in, 16)

            late(wraw1[:, 0:3, :], wqkv1.rearrange("(c p) d -> p c d", p=P))
            late(wraw1[:, 3, :], wout1)
            late(wraw1[:, 4, :], wgate1)
            for i in range(2):
                late(acc[i][:], w_exp0[4 * i:4 * i + 4].rearrange("e f h -> f e h"))
            late(brow[0:E * HC, :], b1.rearrange("e (c p) -> (e c) p", p=P))
            late(brow[E * HC:E * HC + HC, :], bs1.rearrange("(c p) -> c p", p=P))
            late(brow[E * HC + HC:E * HC + HC + 2, :], bqkv1[0:2 * P].rearrange("(c p) -> c p", p=P))
            late(brow[E * HC + HC + 2:E * HC + HC + 3, :], bgate1.rearrange("(c p) -> c p", p=P))

            def spread(step):
                sp.wait_ge(hi_done, 2 * (step + 1))
                sp.wait_ge(mid_done, 2 * (step + 1))
                sp.wait_ge(lo_done, 2 * (step + 1))
                for scr, w in ((scr_q, "q"), (scr_k, "k")):
                    for i in range(3):
                        sp.dma_start(scr[i], parts[w][i][:]).then_inc(scratch_in, 16)
                sp.dma_start(scr_x[bass.ds(step, 1)].rearrange("a p n -> (a p) n"), xnT[:]).then_inc(xnT_kept, 16)
                if layer[0]:
                    sp.dma_start(XN[:, bass.ds((step - NS) * ST, ST), :], xn[:]).then_inc(xn_kept, 16)
                sp.wait_ge(scratch_in, 96 * (step + 1))

            def load(u):
                for scr, to, which in ((scr_q, qs, Q_PARTS), (scr_k, ks, K_PARTS)):
                    for r, i in enumerate(which):
                        sp.dma_start(to[u][DK * r:DK * (r + 1), :, :],
                                     scr[i][:, u * T:(u + 1) * T].rearrange("(h d) t -> d h t", d=DK))\
                          .then_inc(qk_in[u], 16)

            sp.wait_ge(lines_done, 1)
            sp.dma_start(scr_line.rearrange("a h c -> h a c"), lines).then_inc(lines_in, 16)
            sp.wait_ge(lines_in, 16)
            by_key = bass.AP(tensor=scr_line.tensor, offset=scr_line.offset + T - (P - 1), ap=[[1, P], [LINE, H], [1, T]])
            sp.dma_start(btab[:, :, P:QW], by_key).then_inc(tables_in, 16)
            by_query = bass.AP(tensor=scr_line.tensor, offset=scr_line.offset + H * LINE + LINE - 2 * T,
                               ap=[[1, P], [LINE, H], [1, T]])
            sp.dma_start(btabq, by_query).then_inc(tables_in, 16)

            sp.wait_ge(consts, 7)
            spread(0)
            load(0)
            load(1)
            sp.dma_start(x_slots.rearrange("(a p) d -> p a d", p=P),
                         spread_over(ones_sq, [[P, P], [0, BLOCKS * SLOTS // P], [1, D]])).then_inc(spare_in, 16)
            later(bias_v[:, 0:P], bqkv1[2 * P:3 * P].rearrange("(a n) -> a n", a=1))
            later(bias_v[:, P:P + E], gate_b.rearrange("(a n) -> a n", a=1))
            later(bias_o[:], bout1.rearrange("(a n) -> a n", a=1))
            later(wv1[:, P:P + E], gate_w)
            later(ws1_sb[:], ws1)
            later(ws2_sb[:], ws2.rearrange("(c p) n -> p c n", p=P))
            for t in range(ST):
                later(bdiag0[E * t:E * (t + 1), t, :], b_exp0)
                later(bdiag1[E * t:E * (t + 1), t, :], b2)
                later(bdiag1[4 * E:4 * E + 1, t, :], bs2.rearrange("(a n) -> a n", a=1))

            def body(s, first, last):
                if last:
                    return
                sp.wait_ge(qk_in[1], 192 * (s + 1))
                spread(s + 1)
                sp.wait_ge(scored, 16 * s + 8)
                load(0)
                sp.wait_ge(scored, 16 * s + 16)
                load(1)
            steps(sp, body)

            def fetch(at):
                sp.dma_start(xstat[:], scr_x[bass.ds(at, 1)].rearrange("a p n -> (a p) n")).then_inc(stat_in, 16)

            def keep(at):
                sp.wait_ge(mixed, E * (at + 1))
                sp.dma_start(X[:, bass.ds(at * ST, ST), :], x1[:]).then_inc(x1_kept, 16)

            def load_maxima(u, n):
                sp.wait_ge(negT_done, n + 1)
                for i in range(3):
                    sp.dma_start(qs[u][SROWS + i:SROWS + i + 1, :, :], mT[H * i:H * (i + 1), :]).then_inc(m_in[u], 16)

            layer[0] = 1
            sp.wait_ge(xnT_kept, 16 * NS)
            fetch(0)
            keep(0)
            sp.wait_ge(qk_in[1], 192 * NS)
            spread(NS)
            sp.wait_ge(scored, 16 * NS)
            load(0)
            load(1)
            load_maxima(0, 0)

            def body1(s, first, last):
                if not last:
                    sp.wait_ge(mix_ps, E * (s - NS + 1))
                    fetch(s - NS + 1)
                    keep(s - NS + 1)
                    sp.wait_ge(qk_in[1], 192 * (s + 1))
                    spread(s + 1)
                    sp.wait_ge(scored, 16 * s + 8)
                    load(0)
                load_maxima(1, 2 * (s - NS) + 1)
                if not last:
                    load_maxima(0, 2 * (s - NS) + 2)
                    sp.wait_ge(scored, 16 * s + 16)
                    load(1)
            steps(sp, body1, NS)

            def fetch_shared(step):
                sp.wait_ge(hid_ps, HC * step)
                fetch(NS + step)

            def load_block(j, u):
                e = sp.value_load(block_at[0:1, bass.ds(j, 1)], min_val=0, max_val=E - 1)
                if not (isinstance(j, int) and j < 2):
                    sp.wait_ge(hidb_ps, HC * (j - 1))
                sp.dma_start(block_bufs["x", u].rearrange("p (a d) -> p a d", a=2),
                             x_slots[bass.ds(j * SLOTS, SLOTS), :].rearrange("(a p) d -> p a d", p=P)).then_inc(x_in[u], 16)
                sp.dma_start(block_bufs["w1", u], w1[bass.ds(e, 1)].rearrange("a p n -> (a p) n")).then_inc(x_in[u], 16)

            def load_second(j, u):
                e = sp.value_load(block_at[0:1, bass.ds(j, 1)], min_val=0, max_val=E - 1)
                if not (isinstance(j, int) and j < 2):
                    sp.wait_ge(yb_ps, j - 1)
                sp.dma_start(block_bufs["w2", u].rearrange("p (c n) -> p c n", c=HC),
                             w2[bass.ds(e, 1)].rearrange("a (c p) n -> p (a c) n", p=P)).then_inc(w2_in[u], 16)

            def store_block(j, u):
                sp.wait_ge(yb_done, j + 1)
                sp.dma_start(y_slots[bass.ds(j * SLOTS, SLOTS), :].rearrange("(a p) d -> p a d", p=P),
                             block_bufs["y", u].rearrange("p (a d) -> p a d", a=2)).then_inc(y_stored[u], 16)

            sp.wait_ge(xnT_kept, 32 * NS)
            sp.wait_ge(table_done, 1)
            fetch(NS)
            with sp.Fori(1, FRONT) as s:
                fetch_shared(s)
            sp.wait_ge(maxed, 16 * NS)
            sp.wait_ge(biased, 16 * NS)
            sp.wait_ge(slots_in, 32 * NT)
            for j in range(2):
                load_block(j, j)
                load_second(j, j)
            load_block(2, 0)
            with sp.Fori(0, BLOCKS // 2 - 2) as i:
                for u in range(2):
                    load_block(2 * i + u + 3, 1 - u)
                    load_second(2 * i + u + 2, u)
                    store_block(2 * i + u, u)
            load_block(BLOCKS - 1, 1)
            load_second(BLOCKS - 2, 0)
            store_block(BLOCKS - 4, 0)
            load_second(BLOCKS - 1, 1)
            for j in range(BLOCKS - 3, BLOCKS):
                store_block(j, j % 2)
            fetch_shared(FRONT)
            out_tiles = out.rearrange("b (t p) d -> p (b t) d", p=P)

            def store(s):
                sp.wait_ge(summed, s + 1)
                sp.dma_start(out_tiles[:, bass.ds(s * ST, ST), :], acc[0][:]).then_inc(stored, 16)
            with sp.Fori(0, NS - FRONT - 1) as s:
                fetch_shared(FRONT + s + 1)
                store(s)
            with sp.Fori(NS - FRONT - 1, NS) as s:
                store(s)
            sp.wait_ge(stored, 16 * NS)

        @block.gpsimd
        def _(pool):
            pool.memset(ident[:], 0.0).then_inc(consts, 1)
            pool.memset(diagcap[:], CLIP_HI).then_inc(consts, 1)
            pool.memset(flip[:], 0.0).then_inc(consts, 1)
            pool.memset(ones_sq[:], 1.0).then_inc(consts, 1)
            pool.wait_ge(consts, 4)
            pool.affine_select(out=ident[:], in_=ident[:], compare_op=ALU.not_equal, fill=1.0, base=0,
                               pattern=[[-1, P]], channel_multiplier=1).then_inc(masks_done, 1)
            pool.affine_select(out=upper[:], in_=ones_sq[:], compare_op=ALU.is_gt, fill=0.0, base=0,
                               pattern=[[1, P]], channel_multiplier=-1).then_inc(masks_done, 1)
            pool.affine_select(out=flip[:], in_=flip[:], compare_op=ALU.not_equal, fill=1.0, base=-(P - 1),
                               pattern=[[1, P]], channel_multiplier=1).then_inc(masks_done, 1)
            both = diagcap[:].rearrange("p (a n) -> p a n", a=2)
            pool.affine_select(out=both, in_=both, compare_op=ALU.is_ge, fill=0.0, base=0,
                               pattern=[[0, 2], [1, P]], channel_multiplier=-1).then_inc(masks_done, 1)
            pool.wait_ge(masks_done, 1)
            pool.tensor_copy(ident16[:], ident[:]).then_inc(consts, 1)
            pool.memset(minus_half[:], -0.5).then_inc(consts, 1)
            pool.iota(steps16[:], pattern=[[SLOTS, B * T // SLOTS]], base=0, channel_multiplier=0,
                      allow_small_or_imprecise_dtypes=True)
            pool.iota(numbers[:], pattern=[[1, BLOCKS]], base=0, channel_multiplier=0, allow_small_or_imprecise_dtypes=True)
            pool.memset(bdiag0[:], 0.0)
            pool.memset(bdiag1[:], 0.0)
            for u in range(2):
                pool.memset(qs[u][:].bitcast(F32)[0:SROWS], 0.0)
                pool.memset(ks[u][:].bitcast(F32)[0:SROWS], 0.0)
                last = pool.memset(vpad[u][:], 0.0)
            last.then_inc(consts, 1)

            def power(step):
                pool.wait_ge(var_done, step + 1)
                pool.tensor_tensor(rstd0[:], var_eps[:], minus_half[:], ALU.pow).then_inc(pow_done, 1)

            def low(step):
                for n, w in enumerate("qk"):
                    pool.wait_ge(mid_done, 2 * step + n + 1)
                    pool.tensor_tensor(parts[w][2][:], rest[w][:], parts[w][1][:], ALU.subtract).then_inc(lo_done, 1)

            def pad(step, u, wait_batch):
                pool.wait_ge(v_out, 2 * (step + 1))
                if wait_batch is not None:
                    pool.wait_ge(weighed, wait_batch)
                pool.tensor_tensor(spread_over(vpad[u], [[2 * H * VW, P], [4 * VW, 8], [VW + DK, 4], [1, DK]]),
                                   vraw[:, 2 * u:2 * u + 2, :].rearrange("p t (g j d) -> p (t g) j d", g=4, j=4),
                                   spread_over(ones_sq, [[P, P], [0, 8], [0, 4], [1, DK]]), ALU.mult).then_inc(vpad_done, 1)

            def gates(step, u, read):
                pool.wait_ge(eg_out, step - NS + 1)
                if read is not None:
                    pool.wait_ge(heads_done, read)
                pool.tensor_tensor(eg[u][:], egraw[:, u * T:(u + 1) * T], spread_over(ones_sq, [[P, P], [0, 2], [1, P]]),
                                   ALU.add).then_inc(eg_done, 1)

            pool.wait_ge(consts, 7)
            power(0)
            low(0)
            pad(0, 0, None)
            pad(0, 1, None)
            pool.wait_ge(key_done, H // 2)
            pool.tensor_tensor(btab[:, :, 0:P], btab[:, :, P:2 * P], spread_over(ones_sq, [[P, P], [0, H], [1, P]]),
                               ALU.mult).then_inc(table_copied, 1)

            def body(s, first, last):
                if last:
                    return
                power(s + 1)
                low(s + 1)
                pad(s + 1, 0, 8 * s + 4)
                pad(s + 1, 1, 8 * s + 8)
            steps(pool, body)

            power(NS)
            low(NS)
            pad(NS, 0, 8 * NS - 4)
            pad(NS, 1, 8 * NS)
            gates(NS, 0, None)
            gates(NS, 1, None)

            def body1(s, first, last):
                if last:
                    return
                power(s + 1)
                low(s + 1)
                pad(s + 1, 0, 8 * s + 4)
                gates(s + 1, 0, 2 * s + 1)
                pad(s + 1, 1, 8 * s + 8)
                gates(s + 1, 1, 2 * s + 2)
            steps(pool, body1, NS)

            pool.wait_ge(xn_kept, 16 * NS)
            pool.wait_ge(slots_done, 1)
            pool.wait_ge(spare_in, 16)
            for t in range(NT):
                for k in range(2):
                    pool.indirect_dma_start(x_slots, bass.IndirectOffsetOnAxis(ap=slots_at[:, k, t:t + 1], axis=0),
                                            XN[:, t, :], None).then_inc(slots_in, 16)
            for u in range(2):
                pool.wait_ge(y_stored[u], 8 * BLOCKS)
            for t in range(NT):
                u, before = t // ST % 2, t // (2 * ST)
                if t % ST == 0 and before:
                    pool.wait_ge(picked_in[u], 32 * ST * before)
                for k in range(2):
                    pool.indirect_dma_start(picked[:, t, k, :], None, y_slots,
                                            bass.IndirectOffsetOnAxis(ap=slots_at[:, k, t:t + 1], axis=0))\
                        .then_inc(picked_in[u], 16)

        @block.vector
        def _(dve):
            def tokens(step, t):
                if layer[0]:
                    return x1[:, t, :]
                return X[:, bass.ds(step * ST + t, 1), :].rearrange("p a d -> p (a d)")

            layer = [0]

            def moments_of(step):
                for t in range(ST):
                    dve.bn_stats(stats[:, t, :], tokens(step, t)).then_inc(stat_done, 1)
                dve.wait_ge(stat_done, (step + 1) * ST)
                dve.memset(unused[:, 8:9], 0.0)
                for t in range(ST):
                    dve.bn_aggr(moments[:, t, :], stats[:, t, :]).then_inc(mom_done, 1)
                dve.wait_ge(mom_done, (step + 1) * ST)
                dve.tensor_scalar(var_eps[:], moments[:, :, 1], EPS, None, ALU.add).then_inc(var_done, 1)

            def normalise(step):
                dve.wait_ge(pow_done, step + 1)
                dve.tensor_tensor(newton[:], rstd0[:], rstd0[:], ALU.mult).then_inc(newt, 1)
                dve.wait_ge(newt, 4 * step + 1)
                dve.tensor_tensor(newton[:], newton[:], var_eps[:], ALU.mult).then_inc(newt, 1)
                dve.wait_ge(newt, 4 * step + 2)
                dve.tensor_scalar(newton[:], newton[:], -0.5, 1.5, ALU.mult, ALU.add).then_inc(newt, 1)
                dve.wait_ge(newt, 4 * step + 3)
                dve.tensor_tensor(rstd[:], rstd0[:], newton[:], ALU.mult).then_inc(newt, 1)
                dve.wait_ge(newt, 4 * step + 4)
                if layer[0] and not (isinstance(step, int) and step == NS):
                    dve.wait_ge(xn_kept, 16 * (step - NS))
                for t in range(ST):
                    last = dve.tensor_scalar(xn[:, t, :], tokens(step, t),
                                             moments[:, t, 0:1], rstd[:, t:t + 1], ALU.subtract, ALU.mult)
                last.then_inc(xn_done, 1)

            def split(step):
                for n, (w, ps) in enumerate((("q", psA), ("k", psB))):
                    dve.wait_ge(hi_done, 2 * step + n + 1)
                    if layer[0]:
                        dve.scalar_tensor_tensor(out=rest[w][:], in0=ps[:], scalar=bqkg[:, n:n + 1], in1=parts[w][0][:],
                                                 op0=ALU.add, op1=ALU.subtract).then_inc(rest_done, 1)
                    else:
                        dve.tensor_tensor(rest[w][:], ps[:], parts[w][0][:], ALU.subtract).then_inc(rest_done, 1)
                    dve.wait_ge(rest_done, 2 * step + n + 1)
                    dve.tensor_copy(parts[w][1][:], rest[w][:]).then_inc(mid_done, 1)

            def clip(s, u, q):
                dve.wait_ge(exp_done, 16 * s + 8 * u + 2 * q + 2)
                dve.scalar_tensor_tensor(out=probs[q][:, :, 0:2 * P], in0=probs[q][:, :, 0:2 * P], scalar=CLIP_LO,
                                         in1=bass.AP(tensor=diagcap[:].tensor, offset=diagcap[:].offset,
                                                     ap=[[2 * P, P], [0, 4], [1, 2 * P]]),
                                         op0=ALU.max, op1=ALU.min).then_inc(clipped, 1)
                dve.tensor_scalar(probs[q][:, :, 2 * P:QW], probs[q][:, :, 2 * P:QW], CLIP_LO, CLIP_HI,
                                  ALU.max, ALU.min).then_inc(clipped, 1)

            def finish(u, n):
                dve.wait_ge(weighed, 4 * n + 4)
                if layer[0]:
                    dve.wait_ge(eg_done, n - B + 1)
                    dve.tensor_tensor(rden[:], psN[u][:, T:2 * T], eg[u][:], ALU.mult).then_inc(gated, 1)
                    dve.wait_ge(gated, n - B + 1)
                    dve.reciprocal(rden[:], rden[:]).then_inc(rden_done, 1)
                else:
                    dve.reciprocal(rden[:], psN[u][:, T:2 * T]).then_inc(rden_done, 1)
                dve.wait_ge(rden_done, n + 1)
                if not (isinstance(n, int) and n == 0):
                    dve.wait_ge(out_ps, n)
                dve.tensor_tensor(heads[:], psN[u][:, 0:T], rden[:], ALU.mult).then_inc(heads_done, 1)

            def add_out(u, n):
                dve.wait_ge(out_ps, n + 1)
                ps = psB if u else psA
                dst = X[:, bass.ds(2 * n, 2), :]
                dve.tensor_tensor(dst, dst, ps[:, 0:2 * D].rearrange("p (t d) -> p t d", t=2), ALU.add).then_inc(x_done, 1)

            dve.memset(ones_pad[:], 0.0).then_inc(ones_done, 1)
            dve.wait_ge(ones_done, 1)
            for j in range(4):
                last = dve.memset(ones_pad[:, j, DK * j:DK * (j + 1)], 1.0)
            last.then_inc(ones_done, 1)
            for e in range(E):
                last = dve.memset(rank8[:, e:e + 1], float(E - e))
            dve.memset(one_row[:], 1.0)
            dve.memset(combT[4 * E:4 * E + 1, :], 1.0)
            for u in range(2):
                last = dve.memset(ks[u][SROWS:MROWS, :, :], 1.0)
            last.then_inc(ones_done, 1)
            dve.memset(lines, MASKED).then_inc(lined, 1)
            dve.wait_ge(lined, 1)
            dve.wait_ge(pos_in, 16)
            run = 33
            dve.tensor_copy(lines[:, 0, T:T + run], pbT[:, 0:run])
            back = LINE - 1 - T
            dve.tensor_copy(lines[:, 1, back - run + 1:back + 1],
                            bass.AP(tensor=pbT[:].tensor, offset=pbT[:].offset + run - 1, ap=[[len(OFFSETS), H], [-1, run]]))
            for n in range(run, len(OFFSETS)):
                dve.tensor_copy(lines[:, 0, T + OFFSETS[n]:T + OFFSETS[n] + 1], pbT[:, n:n + 1])
                last = dve.tensor_copy(lines[:, 1, back - OFFSETS[n]:back - OFFSETS[n] + 1], pbT[:, n:n + 1])
            last.then_inc(lines_done, 1)
            dve.wait_ge(x_first, 16)
            moments_of(0)
            normalise(0)
            dve.wait_ge(masks_done, 4)
            split(0)
            for i in range(H // 2):
                dve.wait_ge(query_ps, i + 1)
                dve.tensor_copy(btabq[:, 2 * i:2 * i + 2, :], psS[1][:, i % 2, :].rearrange("p (h c) -> p h c", h=2)).then_inc(query_done, 1)

            def body(s, first, last):
                if not last:
                    if first:
                        dve.wait_ge(x_rest, 16)
                    moments_of(s + 1)
                clip(s, 0, 0)
                clip(s, 0, 1)
                if not first:
                    finish(1, 2 * s - 1)
                if not last:
                    normalise(s + 1)
                clip(s, 0, 2)
                if not first:
                    add_out(1, 2 * s - 1)
                clip(s, 0, 3)
                if not last:
                    split(s + 1)
                clip(s, 1, 0)
                clip(s, 1, 1)
                finish(0, 2 * s)
                clip(s, 1, 2)
                add_out(0, 2 * s)
                clip(s, 1, 3)
            steps(dve, body)

            count = [0]

            def link(instruction):
                count[0] += 1
                instruction.then_inc(routing, 1)
                dve.wait_ge(routing, count[0])

            def wide3(t):
                return spread_over(t, [[NT, P], [1, NT], [0, E]])

            def first_of(onehot, top, logits):
                ranks = spread_over(rank8, [[E, P], [0, NT], [1, E]])
                link(dve.tensor_tensor(onehot, logits, wide3(top), ALU.is_equal))
                link(dve.tensor_tensor(onehot, onehot, ranks, ALU.mult))
                link(dve.tensor_reduce(out=rs[3][:], in_=onehot, axis=AX.X, op=ALU.max))
                link(dve.tensor_tensor(onehot, onehot, wide3(rs[3]), ALU.is_equal))

            dve.wait_ge(logits_out, 2 * NS)
            link(dve.tensor_reduce(out=rs[0][:], in_=logit0[:], axis=AX.X, op=ALU.max))
            first_of(rt[0], rs[0], logit0[:])
            onehot_done_at = count[0]
            assert onehot_done_at == ONEHOT_AT
            link(dve.tensor_tensor(rt[1], logit0[:], wide3(rs[0]), ALU.subtract))
            dve.wait_ge(route_exp, 1)
            link(dve.tensor_reduce(out=rs[1][:], in_=rt[1], axis=AX.X, op=ALU.add))
            link(dve.reciprocal(rs[2][:], rs[1][:]))
            finish(1, B - 1)
            add_out(1, B - 1)

            def places(a, b, n_loc):
                dve.wait_ge(loc_ps, n_loc)
                dve.memset(rt[a][:, 0, :], 0.0)
                link(dve.tensor_copy(rt[a][:, 1:NT, :], totals[:, 0:NT - 1, :]))
                k = 1
                while k < NT:
                    dve.tensor_copy(rt[b][:, 0:k, :], rt[a][:, 0:k, :])
                    link(dve.tensor_tensor(rt[b][:, k:NT, :], rt[a][:, k:NT, :], rt[a][:, 0:NT - k, :], ALU.add))
                    a, b, k = b, a, 2 * k
                link(dve.tensor_tensor(rt[b], psA[:, 0:NT * E].rearrange("p (t e) -> p t e", e=E), rt[a], ALU.add))
                return a, b

            totals = psB[:, 0:NT * E].rearrange("p (t e) -> p t e", e=E)
            a, b = places(1, 2, 1)
            link(dve.tensor_scalar(rt[b], rt[b], float(CAP), None, ALU.is_lt))
            link(dve.tensor_tensor(rt[b], rt[b], rt[0], ALU.mult))
            dve.tensor_tensor(comb[:], rt[b], wide3(rs[2]), ALU.mult).then_inc(comb_done, 1)
            dve.wait_ge(comb_done, 1)

            layer[0] = 1

            def pick(at):
                dve.tensor_copy(comb_s[:], comb[:, bass.ds(at * ST, ST), :]).then_inc(comb_s_done, 1)

            def experts(at, dst):
                dve.wait_ge(bias_ps, at + 1)
                if not (isinstance(at, int) and at == 0):
                    dve.wait_ge(x1_kept, 16 * at)
                dve.tensor_tensor(dst[:], psA[:].rearrange("p (t d) -> p t d", t=ST), X[:, bass.ds(at * ST, ST), :],
                                  ALU.add).then_inc(bias_added, 1)
                dve.wait_ge(bias_added, at + 1)
                for e in range(E):
                    ps = psA if e % 2 else psB
                    dve.wait_ge(mix_ps, E * at + e + 1)
                    if e > 0:
                        dve.wait_ge(mixed, E * at + e)
                    for t in range(ST):
                        last = dve.scalar_tensor_tensor(out=dst[:, t, :], in0=ps[:, t * D:(t + 1) * D],
                                                        scalar=comb_s[:, t, e:e + 1], in1=dst[:, t, :], op0=ALU.mult, op1=ALU.add)
                    last.then_inc(mixed, 1)
                dve.wait_ge(mixed, E * (at + 1))

            def add_bias(s, u, q):
                for half in range(2):
                    dve.wait_ge(scored, 16 * s + 8 * u + 2 * q + half + 1)
                    if half == 0:
                        dve.wait_ge(weighed, 8 * s + 4 * u + q - 3)
                    h = 8 * half + q
                    dve.tensor_tensor(probs[q][:, 2 * half:2 * half + 2, :], psS[half][:, :, 0:QW], btab[:, h:h + 5:4, :],
                                      ALU.add).then_inc(biased, 1)

            def maxima(n, q):
                for half in range(2):
                    dve.wait_ge(ranked, 8 * n + 2 * q + half + 1)
                    at = 2 * q + half
                    dve.memset(unused[:, at:at + 1], 0.0)
                    for i in range(2):
                        h = 4 * (2 * half + i) + q
                        dve.tensor_tensor_reduce(out=psS[half][:, i, 0:P], in0=psS[half][:, i, 0:P], in1=btabq[:, h, P:T], scale=1.0,
                                                 scalar=-3e38, op0=ALU.add, op1=ALU.max, accum_out=smax[:, 0, h:h + 1])
                        last = dve.tensor_tensor_reduce(out=psS[half][:, i, P:QW], in0=psS[half][:, i, P:QW], in1=btabq[:, h, :], scale=1.0,
                                                        scalar=-3e38, op0=ALU.add, op1=ALU.max, accum_out=smax[:, 1, h:h + 1])
                    last.then_inc(maxed, 1)

            def negate(n):
                dve.wait_ge(maxed, 8 * n + 8)
                if not (isinstance(n, int) and n == 0):
                    dve.wait_ge(negT_ps, n)
                dve.tensor_scalar(mparts[:, :, 0, :], smax[:], -1.0, None, ALU.mult).then_inc(neg_step, 1)
                dve.wait_ge(neg_step, 3 * n + 1)
                dve.scalar_tensor_tensor(out=mrest[:], in0=smax[:], scalar=-1.0, in1=mparts[:, :, 0, :], op0=ALU.mult,
                                         op1=ALU.subtract).then_inc(neg_step, 1)
                dve.wait_ge(neg_step, 3 * n + 2)
                dve.tensor_copy(mparts[:, :, 1, :], mrest[:]).then_inc(neg_step, 1)
                dve.wait_ge(neg_step, 3 * n + 3)
                dve.tensor_tensor(mparts[:, :, 2, :], mrest[:], mparts[:, :, 1, :], ALU.subtract).then_inc(neg_done, 1)

            dve.wait_ge(query_done, H // 2)
            dve.wait_ge(table_copied, 1)
            dve.wait_ge(wt1_done, WT1)
            pick(0)
            experts(0, x1)
            moments_of(NS)
            normalise(NS)
            split(NS)
            for q in range(4):
                maxima(0, q)
            negate(0)

            def choose():
                dve.wait_ge(logits_out, 4 * NS)
                link(dve.tensor_reduce(out=rs[0][:], in_=logit0[:], axis=AX.X, op=ALU.max))
                first_of(rt[0], rs[0], logit0[:])
                link(dve.scalar_tensor_tensor(out=rt[1].rearrange("p t e -> p (t e)"), in0=rt[0].rearrange("p t e -> p (t e)"),
                                              scalar=-1e38, in1=logit0[:].rearrange("p t e -> p (t e)"), op0=ALU.mult, op1=ALU.add))
                link(dve.tensor_reduce(out=rs[1][:], in_=rt[1], axis=AX.X, op=ALU.max))
                first_of(rt[2], rs[1], rt[1])
                link(dve.tensor_tensor(rt[1], rt[0], rt[2], ALU.add))
                assert count[0] == BOTH_AT, count[0]
                link(dve.tensor_tensor(rs[1][:], rs[1][:], rs[0][:], ALU.subtract))
                assert count[0] == SECOND_AT

            def weights_and_slots():
                a, b = places(3, 4, 2)
                link(dve.tensor_tensor(filled[:], rt[a][:, NT - 1, :], totals[:, NT - 1, :], ALU.add))
                M = B * T // SLOTS
                link(dve.tensor_tensor(many[:], spread_over(filled, [[E, P], [1, E], [0, M]]),
                                       spread_over(steps16, [[M, P], [0, E], [1, M]]), ALU.is_gt))
                link(dve.tensor_reduce(out=n_blocks[:], in_=many[:], axis=AX.X, op=ALU.add))
                link(dve.tensor_copy(ends[0][:], n_blocks[:]))
                c, d, k = 0, 1, 1
                while k < E:
                    dve.tensor_copy(ends[d][:, 0:k], ends[c][:, 0:k])
                    link(dve.tensor_tensor(ends[d][:, k:E], ends[c][:, k:E], ends[c][:, 0:E - k], ALU.add))
                    c, d, k = d, c, 2 * k
                link(dve.tensor_tensor(slot0[:], ends[c][:], n_blocks[:], ALU.subtract))
                link(dve.tensor_scalar(slot0[:], slot0[:], float(SLOTS), None, ALU.mult))
                link(dve.tensor_tensor(rt[b], rt[b], spread_over(slot0, [[E, P], [0, NT], [1, E]]), ALU.add))
                for k, (onehot, at) in enumerate(((rt[0], rs[0]), (rt[2], rs[3]))):
                    link(dve.tensor_tensor(rt[a], rt[b], onehot, ALU.mult))
                    link(dve.tensor_reduce(out=at[:], in_=rt[a], axis=AX.X, op=ALU.add))
                    last = dve.tensor_copy(slots_at[:, k, :], at[:])
                last.then_inc(slots_done, 1)
                link(dve.tensor_tensor(passed[:], spread_over(numbers, [[BLOCKS, P], [1, BLOCKS], [0, E]]),
                                       spread_over(ends[c], [[E, P], [0, BLOCKS], [1, E]]), ALU.is_ge))
                link(dve.tensor_reduce(out=block_e[:], in_=passed[:], axis=AX.X, op=ALU.add))
                link(dve.tensor_scalar(block_e[:], block_e[:], float(E - 1), None, ALU.min))
                dve.tensor_copy(block_at[:], block_e[:]).then_inc(table_done, 1)
                dve.wait_ge(route_exp, 2)
                link(dve.tensor_scalar(rs[0][:], rs[1][:], 1.0, None, ALU.add))
                link(dve.reciprocal(rs[2][:], rs[0][:]))
                link(dve.tensor_tensor(rs[1][:], rs[1][:], rs[2][:], ALU.mult))
                link(dve.tensor_tensor(rt[0], rt[0], wide3(rs[2]), ALU.mult))
                link(dve.tensor_tensor(rt[2], rt[2], wide3(rs[1]), ALU.mult))
                dve.tensor_tensor(comb[:], rt[0], rt[2], ALU.add).then_inc(comb_done, 1)

            def body1(s, first, last):
                n = 2 * (s - NS)
                if not last:
                    pick(s - NS + 1)
                add_bias(s, 0, 0)
                add_bias(s, 0, 1)
                if not first:
                    finish(1, 2 * s - 1)
                    add_out_1(s - NS - 1)
                if not last:
                    experts(s - NS + 1, x1)
                    moments_of(s + 1)
                else:
                    choose()
                add_bias(s, 0, 2)
                if not last:
                    normalise(s + 1)
                else:
                    weights_and_slots()
                add_bias(s, 0, 3)
                maxima(n + 1, 0)
                if not last:
                    split(s + 1)
                for q in range(1, 4):
                    maxima(n + 1, q)
                finish(0, 2 * s)
                add_out_0(s - NS)
                negate(n + 1)
                if not last:
                    for q in range(4):
                        maxima(n + 2, q)
                    negate(n + 2)
                for q in range(4):
                    add_bias(s, 1, q)

            def add_layer1(u, at):
                dve.wait_ge(out_ps, 2 * (at + NS) + u + 1)
                dve.wait_ge(x1_kept, 16 * (at + 1))
                ps = psB if u else psA
                dst = X[:, bass.ds(ST * at + 2 * u, 2), :]
                dve.tensor_tensor(dst, dst, ps[:, 0:2 * D].rearrange("p (t d) -> p t d", t=2), ALU.add).then_inc(x_done, 1)

            def add_out_0(at):
                add_layer1(0, at)

            def add_out_1(at):
                add_layer1(1, at)

            steps(dve, body1, NS)
            finish(1, 2 * B - 1)
            add_out_1(NS - 1)

            def shared(s):
                if not (isinstance(s, int) and s == 0):
                    dve.wait_ge(y_used, s)
                dve.tensor_copy(comb_s[:], comb[:, bass.ds(s * ST, ST), :]).then_inc(comb_s_done, 1)
                stream = X[:, bass.ds(s * ST, ST), :]
                dve.wait_ge(bias_ps, NS + s + 1)
                dve.tensor_tensor(stream, psA[:].rearrange("p (t d) -> p t d", t=ST), stream, ALU.add).then_inc(bias_added, 1)
                dve.wait_ge(bias_added, NS + s + 1)
                dve.wait_ge(y_ps, s + 1)
                dve.tensor_tensor(stream, psN[0][:].rearrange("p (t d) -> p t d", t=ST), stream, ALU.add).then_inc(y_used, 1)

            def take_tokens(j, u):
                dve.wait_ge(xb_turned, j + 1)
                dve.tensor_copy(block_bufs["xT", u], (psB if u else psA)[:, 0:SLOTS]).then_inc(xb_done, 1)

            def take_bias(j, u):
                e = dve.value_load(block_at[0:1, bass.ds(j, 1)], min_val=0, max_val=E - 1)
                if not (isinstance(j, int) and j < 2):
                    dve.wait_ge(gelub_done, HC * (j - 1))
                dve.tensor_tensor(block_bufs["b1", u], bcol[:, bass.ds(e * HC, HC)], ones_sq[:, 0:HC], ALU.mult).then_inc(b1_done, 1)

            def take_result(j, u):
                dve.wait_ge(yb_ps, j + 1)
                if not (isinstance(j, int) and j < 2):
                    dve.wait_ge(y_stored[u], 16 * ((j - u) // 2) if isinstance(j, int) else 16 * half_of[0])
                dve.tensor_copy(block_bufs["y", u], psN[u][:, 0:2 * D]).then_inc(yb_done, 1)

            shared(0)
            with dve.Fori(1, FRONT) as s:
                shared(s)
            half_of = [None]
            for j in range(2):
                take_bias(j, j)
            for j in range(2):
                take_tokens(j, j)
            for j in range(2):
                take_tokens(j + 2, j)
                take_result(j, j)
                take_bias(j + 2, j)
            with dve.Fori(1, BLOCKS // 2 - 1) as i:
                half_of[0] = i
                for u in range(2):
                    take_tokens(2 * i + u + 2, u)
                    take_result(2 * i + u, u)
                    take_bias(2 * i + u + 2, u)
            for u in range(2):
                take_result(BLOCKS - 2 + u, u)

            def combine(s, pair, u):
                dve.wait_ge(picked_in[u], 32 * ST * (pair + 1))
                if not (isinstance(s, int) and s == 0):
                    dve.wait_ge(stored, 16 * s)
                for k in range(2):
                    for t in range(ST):
                        if k == 0:
                            before = X[:, bass.ds(s * ST + t, 1), :].rearrange("p a d -> p (a d)")
                        else:
                            before = acc[0][:, t, :]
                        done = dve.scalar_tensor_tensor(out=acc[0][:, t, :],
                                                        in0=picked[:, bass.ds(s * ST + t, 1), k, :].rearrange("p a d -> p (a d)"),
                                                        scalar=rs[2 - k][:, bass.ds(s * ST + t, 1)], in1=before,
                                                        op0=ALU.mult, op1=ALU.add)
                    done.then_inc(summed if k else first_added, 1)
                    if k == 0:
                        dve.wait_ge(first_added, s + 1)

            dve.wait_ge(y_used, FRONT)
            for s in range(2):
                shared(FRONT + s)
                combine(s, 0, s)
            with dve.Fori(1, NS // 4) as i:
                for u in range(2):
                    shared(FRONT + 2 * i + u)
                    combine(2 * i + u, i, u)
            with dve.Fori(NS // 4, NS // 2) as i:
                for u in range(2):
                    combine(2 * i + u, i, u)

        @block.scalar
        def _(act):
            act.wait_ge(wt_ps, 1)
            act.activation(wT0[:].rearrange("p c d -> p (c d)"), psA[:], ACT.Copy).then_inc(wt_done, 1)
            act.wait_ge(wt_done, 1)
            act.wait_ge(w_in, 48)
            act.activation(wv0[:, 0:P], wT0[:, 2, :], ACT.Copy).then_inc(wt_done, 1)

            def turn(step, first):
                act.wait_ge(xn_turned, step + 1)
                if not first:
                    act.wait_ge(v_ps, 2 * step)
                    act.wait_ge(xnT_kept, 16 * step)
                act.activation(xnT[:], psA[:], ACT.Copy).then_inc(xnT_done, 1)

            def project(step, first):
                if not first:
                    act.wait_ge(scratch_in, 96 * step)
                act.wait_ge(q_ps, step + 1)
                if layer[0]:
                    act.activation(parts["q"][0][:], psA[:], ACT.Identity, bias=bqkg[:, 0:1]).then_inc(hi_done, 1)
                else:
                    act.activation(parts["q"][0][:], psA[:], ACT.Copy).then_inc(hi_done, 1)
                act.wait_ge(k_ps, step + 1)
                if layer[0]:
                    act.activation(parts["k"][0][:], psB[:], ACT.Identity, bias=bqkg[:, 1:2]).then_inc(hi_done, 1)
                else:
                    act.activation(parts["k"][0][:], psB[:], ACT.Copy).then_inc(hi_done, 1)

            def values_out(step, first):
                if not first:
                    act.wait_ge(vpad_done, 2 * step)
                for n, ps in enumerate((psB, psA) if layer[0] else (psA, psB)):
                    act.wait_ge(v_ps, 2 * step + n + 1)
                    v = ps[:, 0:2 * (P + E)].rearrange("p (t c) -> p t c", t=2)
                    act.activation(vraw[:, 2 * n:2 * n + 2, :], v[:, :, 0:P], ACT.Copy).then_inc(v_out, 1)
                    act.activation(logit0[:, bass.ds((step - NS * layer[0]) * ST + 2 * n, 2), :], v[:, :, P:P + E], ACT.Copy).then_inc(logits_out, 1)

            def exps(s, u, q, first):
                for half in range(2):
                    act.wait_ge(scored, 16 * s + 8 * u + 2 * q + half + 1)
                    if half == 0 and not (first and u == 0):
                        act.wait_ge(weighed, 8 * s + 4 * u + q - 3)
                    act.activation(probs[q][:, 2 * half:2 * half + 2, :], psS[half][:, :, 0:QW], ACT.Exp,
                                   scale=SCALE).then_inc(exp_done, 1)
            layer = [0]
            turn(0, True)
            project(0, True)
            values_out(0, True)
            act.wait_ge(wt1_ps, 1)
            act.activation(w0T[:, 0:4, :].rearrange("p c d -> p (c d)"), psA[:], ACT.Copy).then_inc(wt1_done, 1)
            act.wait_ge(wt1_ps, 2)
            act.activation(w0T[:, 4:8, :].rearrange("p c d -> p (c d)"), psB[:], ACT.Copy).then_inc(wt1_done, 1)
            act.wait_ge(wt1_ps, 3)
            act.activation(wT1[:, 0, :], psA[:, 0:P], ACT.Copy, scale=SCALE).then_inc(wt1_done, 1)
            act.activation(wT1[:, 1:4, :].rearrange("p c d -> p (c d)"), psA[:, P:4 * P], ACT.Copy).then_inc(wt1_done, 1)
            act.activation(wv1[:, 0:P], psA[:, 2 * P:3 * P], ACT.Copy).then_inc(wt1_done, 1)
            act.wait_ge(wt1_ps, 4)
            act.activation(wT1[:, 4, :], psB[:, 0:P], ACT.Copy)
            nb = E * HC + HC
            act.activation(bcol[:], psB[:, P:P + nb + 3], ACT.Copy)
            act.activation(bqkg[:, 0:1], psB[:, P + nb:P + nb + 1], ACT.Copy, scale=SCALE)
            act.activation(bqkg[:, 1:2], psB[:, P + nb + 1:P + nb + 2], ACT.Copy)
            act.activation(bqkg[:, 2:3], psB[:, P + nb + 2:P + nb + 3], ACT.Copy, scale=-1.0).then_inc(wt1_done, 1)
            for i in range(H // 2):
                act.wait_ge(key_ps, i + 1)
                act.activation(btab[:, 2 * i:2 * i + 2, P:QW], psS[0][:, i % 2, :].rearrange("p (h c) -> p h c", h=2),
                               ACT.Copy).then_inc(key_done, 1)

            def body(s, first, last):
                exps(s, 0, 0, first)
                exps(s, 0, 1, first)
                exps(s, 0, 2, first)
                if not last:
                    turn(s + 1, False)
                exps(s, 0, 3, first)
                if not last:
                    project(s + 1, False)
                exps(s, 1, 0, first)
                if not last:
                    values_out(s + 1, False)
                for q in range(1, 4):
                    exps(s, 1, q, first)
            steps(act, body)
            act.wait_ge(routing, SHIFTED_AT)
            act.activation(rt[1], rt[1], ACT.Exp).then_inc(route_exp, 1)

            layer[0] = 1

            def combT_out(n):
                act.wait_ge(combT_ps, n + 1)
                if not (isinstance(n, int) and n == 0):
                    act.wait_ge(bias_ps, n)
                act.activation(combT[0:4 * E, :], psA[0:4 * E, 0:P], ACT.Copy).then_inc(combT_done, 1)

            def gate_out(step, first):
                act.wait_ge(gate_ps, step - NS + 1)
                if not first:
                    act.wait_ge(eg_done, 2 * (step - NS))
                act.activation(egraw[:], psA[:], ACT.Exp, scale=-1.0, bias=bqkg[:, 2:3]).then_inc(eg_out, 1)

            def maxima_out(u, n, step):
                act.wait_ge(negT_ps, n + 1)
                if step is not None:
                    act.wait_ge(m_in[1 - u], 48 * (step - NS + 1))
                act.activation(mT[:], psB[0:3 * H, 0:T], ACT.Copy).then_inc(negT_done, 1)

            def exps1(s, u, q):
                act.wait_ge(biased, 16 * (s - NS) + 8 * u + 2 * q + 2)
                act.activation(probs[q][:], probs[q][:], ACT.Exp).then_inc(exp1_done, 1)

            combT_out(0)
            turn(NS, False)
            project(NS, False)
            gate_out(NS, True)
            values_out(NS, False)
            maxima_out(0, 0, None)

            def body1(s, first, last):
                exps1(s, 0, 0)
                exps1(s, 0, 1)
                if not last:
                    combT_out(s - NS + 1)
                else:
                    act.wait_ge(routing, SECOND_AT)
                    act.activation(rs[1][:], rs[1][:], ACT.Exp).then_inc(route_exp, 1)
                exps1(s, 0, 2)
                if not last:
                    turn(s + 1, False)
                exps1(s, 0, 3)
                if not last:
                    project(s + 1, False)
                    gate_out(s + 1, False)
                    values_out(s + 1, False)
                maxima_out(1, 2 * (s - NS) + 1, s)
                if not last:
                    maxima_out(0, 2 * (s - NS) + 2, s)
                for q in range(4):
                    exps1(s, 1, q)
            steps(act, body1, NS)

            def shared(s):
                combT_out(NS + s)
                if not (isinstance(s, int) and s == 0):
                    act.wait_ge(y_ps, s)
                for c in range(HC):
                    act.wait_ge(hid_ps, HC * s + c + 1)
                    act.activation(wide[2][:, c * SC:(c + 1) * SC], psS[c // 2][:, c % 2, :], ACT.Gelu,
                                   bias=bcol[:, E * HC + c:E * HC + c + 1]).then_inc(gelu_done, 1)

            def blocks(j, u):
                act.wait_ge(b1_done, j + 1)
                if not (isinstance(j, int) and j < 2):
                    act.wait_ge(yb_ps, j - 1)
                for c in range(HC):
                    act.wait_ge(hidb_ps, HC * j + 2 * (c // 2) + 2)
                    act.activation(wide[u][:, c * SLOTS:(c + 1) * SLOTS], psS[u][:, c // 2, c % 2 * SLOTS:(c % 2 + 1) * SLOTS],
                                   ACT.Gelu, bias=block_bufs["b1", u][:, c:c + 1]).then_inc(gelub_done, 1)

            shared(0)
            with act.Fori(1, FRONT) as s:
                shared(s)
            for j in range(2):
                blocks(j, j)
            with act.Fori(1, BLOCKS // 2) as i:
                for u in range(2):
                    blocks(2 * i + u, u)
            with act.Fori(FRONT, NS) as s:
                shared(s)

        @block.tensor
        def _(pe):
            pe.wait_ge(masks_done, 4)
            pe.wait_ge(consts, 7)
            pe.wait_ge(w_in, 48)
            for c in range(4):
                last = pe.transpose(psA[:, c * P:(c + 1) * P], wraw[:, c, :], ident[:])
            last.then_inc(wt_ps, 1)

            def turn(step):
                pe.wait_ge(xn_done, step + 1)
                for t in range(ST):
                    last = pe.transpose(psA[:, t * P:(t + 1) * P], xn[:, t, :], ident[:])
                last.then_inc(xn_turned, 1)

            def project(step):
                pe.wait_ge(xnT_done, step + 1)
                w = wT1 if layer[0] else wT0
                pe.matmul(psA[:], w[:, 0, :], xnT[:], start=True, stop=True).then_inc(q_ps, 1)
                pe.matmul(psB[:], w[:, 1, :], xnT[:], start=True, stop=True).then_inc(k_ps, 1)

            def values(step):
                for n, ps in ((0, psA), (1, psB)):
                    pe.wait_ge(rest_done, 2 * step + n + 1)
                    for t in range(2):
                        last = pe.matmul(ps[:, t * (P + E):(t + 1) * (P + E)], xnT[:, (2 * n + t) * P:(2 * n + t + 1) * P],
                                         wv0[:], start=True, stop=True)
                    last.then_inc(v_ps, 1)

            def values_read(n):
                pe.wait_ge(v_out, n)
                pe.wait_ge(logits_out, n)

            def score(s, u, q, first):
                if q == 0:
                    pe.wait_ge(qk_in[u], 192 * (s + 1))
                    if layer[0]:
                        pe.wait_ge(m_in[u], 48 * (s - NS + 1))
                rows = MROWS if layer[0] else SROWS
                for half in range(2):
                    if layer[0]:
                        bank_free1(s, u, q, half, first)
                    elif not (first and u == 0 and q == 0):
                        pe.wait_ge(exp_done, 16 * s + 8 * u + 2 * q + half - 1)
                    for i in range(2):
                        h = 4 * (2 * half + i) + q
                        pe.matmul(psS[half][:, i, 0:P], ks[u][0:rows, h, P:T], qs[u][0:rows, h, P:T], start=True, stop=True)
                        last = pe.matmul(psS[half][:, i, P:QW], ks[u][0:rows, h, 0:P], qs[u][0:rows, h, :], start=True, stop=True)
                    last.then_inc(scored, 1)

            def weigh(s, u, q, first):
                if layer[0]:
                    pe.wait_ge(exp1_done, 8 * (s - NS) + 4 * u + q + 1)
                else:
                    pe.wait_ge(clipped, 2 * (8 * s + 4 * u + q + 1))
                if q == 0:
                    pe.wait_ge(vpad_done, 2 * s + u + 1)
                    if not first:
                        pe.wait_ge(heads_done, 2 * s + u - 1)
                for part, at in ((0, 0), (1, T)):
                    for kt, cols, to in ((0, (P, QW), (0, T)), (1, (0, P), (P, T))):
                        for g in range(4):
                            w = vpad[u][:, kt, 4 * g + q, :] if part == 0 else ones_pad[:, q, :]
                            last = pe.matmul(psN[u][VW * g:VW * (g + 1), at + to[0]:at + to[1]], w,
                                             probs[q][:, g, cols[0]:cols[1]],
                                             start=(q == 0 and part == 0 and kt == 0), stop=(q == 3 and kt == 1),
                                             skip_group_check=True)
                last.then_inc(weighed, 1)

            def out_project(u, n):
                pe.wait_ge(heads_done, n + 1)
                ps = psB if u else psA
                for t in range(2):
                    last = pe.matmul(ps[:, t * D:(t + 1) * D], heads[:, t * P:(t + 1) * P], (wT1 if layer[0] else wT0)[:, 3, :],
                                     start=True, stop=not layer[0])
                    if layer[0]:
                        last = pe.matmul(ps[:, t * D:(t + 1) * D], one_row[:], bias_o[:], start=False, stop=True)
                last.then_inc(out_ps, 1)

            layer = [0]
            pe.wait_ge(wt_done, 2)
            turn(0)
            project(0)
            values(0)
            pe.wait_ge(late_in, 16 * LATE)
            values_read(1)
            for e in range(4):
                last = pe.transpose(psA[:, e * P:(e + 1) * P], acc[0][:, e, :], ident[:])
            last.then_inc(wt1_ps, 1)
            values_read(2)
            for e in range(4):
                last = pe.transpose(psB[:, e * P:(e + 1) * P], acc[1][:, e, :], ident[:])
            last.then_inc(wt1_ps, 1)
            pe.wait_ge(wt1_done, 1)
            for c in range(4):
                last = pe.transpose(psA[:, c * P:(c + 1) * P], wraw1[:, c, :], ident[:])
            last.then_inc(wt1_ps, 1)
            pe.wait_ge(wt1_done, 2)
            pe.transpose(psB[:, 0:P], wraw1[:, 4, :], ident[:])
            nb = E * HC + HC + 3
            pe.transpose(psB[:, P:P + nb], brow, ident[0:nb, 0:nb]).then_inc(wt1_ps, 1)
            pe.wait_ge(tables_in, 32)
            for i in range(H // 2):
                for half, tab, sent, kept in ((0, btab[:, :, P:QW], key_ps, key_done), (1, btabq, query_ps, query_done)):
                    if i >= 2:
                        pe.wait_ge(kept, i - 1)
                    pe.matmul(psS[half][:, i % 2, :], flip[:], tab[:, 2 * i:2 * i + 2, :], start=True, stop=True).then_inc(sent, 1)
            pe.wait_ge(key_done, H // 2)
            pe.wait_ge(query_done, H // 2)
            pe.wait_ge(wt1_done, WT1)
            pe.wait_ge(ones_done, 3)

            def body(s, first, last):
                score(s, 0, 0, first)
                if not first:
                    weigh(s - 1, 1, 2, False)
                score(s, 0, 1, first)
                if not first:
                    weigh(s - 1, 1, 3, False)
                score(s, 0, 2, first)
                weigh(s, 0, 0, first)
                values_read(2 * s + 2)
                if not first:
                    out_project(1, 2 * s - 1)
                if not last:
                    if not first:
                        pe.wait_ge(x_done, 2 * s - 1)
                    turn(s + 1)
                score(s, 0, 3, first)
                weigh(s, 0, 1, first)
                if not last:
                    if not first:
                        pe.wait_ge(x_done, 2 * s)
                    project(s + 1)
                score(s, 1, 0, first)
                weigh(s, 0, 2, first)
                if not last:
                    values(s + 1)
                score(s, 1, 1, first)
                weigh(s, 0, 3, first)
                score(s, 1, 2, first)
                weigh(s, 1, 0, first)
                if not last:
                    values_read(2 * s + 3)
                out_project(0, 2 * s)
                score(s, 1, 3, first)
                weigh(s, 1, 1, first)
            steps(pe, body)
            weigh(NS - 1, 1, 2, False)
            weigh(NS - 1, 1, 3, False)
            out_project(1, B - 1)

            pe.wait_ge(routing, ONEHOT_AT)
            pe.wait_ge(x_done, B)

            def count_tokens(chosen):
                flat = chosen.rearrange("p t e -> p (t e)")
                pe.matmul(psA[:, 0:NT * E], upper[:], flat, start=True, stop=True)
                pe.matmul(psB[:, 0:NT * E], ones_sq[:], flat, start=True, stop=True).then_inc(loc_ps, 1)

            count_tokens(rt[0])

            layer[0] = 1

            def bank_free1(s, u, q, half, first):
                n = 16 * (s - NS)
                if q > 0:
                    pe.wait_ge(biased, n + 8 * u + 2 * q + half - 1)
                elif u == 0 and not first:
                    pe.wait_ge(biased, n + half - 1)
                elif u == 0:
                    pe.wait_ge(maxed, 7 + half)
                else:
                    pe.wait_ge(maxed, n + 16 + (0 if last_step[0] else 8) - 1 + half)

            last_step = [False]

            def rank(n, u, q, free, first=False):
                if q == 0:
                    pe.wait_ge(qk_in[u], free[2])
                for half in range(2):
                    if q > 0:
                        pe.wait_ge(maxed, 8 * n + 2 * q + half - 1)
                    else:
                        pe.wait_ge(free[0], free[1] + half)
                    for i in range(2):
                        h = 4 * (2 * half + i) + q
                        pe.matmul(psS[half][:, i, 0:P], qs[u][0:SROWS, h, 0:P], ks[u][0:SROWS, h, 0:P], start=True, stop=True)
                        last = pe.matmul(psS[half][:, i, P:QW], qs[u][0:SROWS, h, P:T], ks[u][0:SROWS, h, :], start=True, stop=True)
                    last.then_inc(ranked, 1)

            def turn_maxima(n):
                pe.wait_ge(neg_done, n + 1)
                if isinstance(n, int) and n == 0:
                    values_read(2 * NS + 2)
                else:
                    pe.wait_ge(negT_done, n)
                for qt in range(2):
                    last = pe.matmul(psB[0:3 * H, qt * P:(qt + 1) * P],
                                     mparts[:, qt, :, :].rearrange("p a h -> p (a h)"), ident16[:], start=True, stop=True)
                last.then_inc(negT_ps, 1)

            def bias_and_comb(n, w=None):
                pe.wait_ge(comb_s_done, n + 1)
                pe.transpose(psA[0:4 * E, 0:P], comb_s[:].rearrange("p t e -> p (t e)"), ident[:]).then_inc(combT_ps, 1)
                if w is not None:
                    bias_product(n, w)

            def bias_product(n, w):
                pe.wait_ge(combT_done, n + 1)
                rows = 4 * E + (w is bdiag1)
                pe.matmul(psA[:], combT[0:rows, :], w[:].rearrange("k t d -> k (t d)"), start=True, stop=True).then_inc(bias_ps, 1)

            def experts(at):
                bias_and_comb(at, bdiag0)
                pe.wait_ge(stat_in, 16 * (at + 1))
                for e in range(E):
                    ps = psA if e % 2 else psB
                    if e == 1:
                        pe.wait_ge(bias_added, at + 1)
                    elif e > 1:
                        pe.wait_ge(mixed, E * at + e - 1)
                    for t in range(ST):
                        last = pe.matmul(ps[:, t * D:(t + 1) * D], xstat[:, t * P:(t + 1) * P], w0T[:, e, :], start=True, stop=True)
                    last.then_inc(mix_ps, 1)

            def gate(step):
                pe.wait_ge(rest_done, 2 * step + 1)
                pe.matmul(psA[:], wT1[:, 4, :], xnT[:], start=True, stop=True).then_inc(gate_ps, 1)

            def values1(step):
                for n, ps in ((0, psB), (1, psA)):
                    if n == 0:
                        pe.wait_ge(rest_done, 2 * step + 2)
                    else:
                        pe.wait_ge(eg_out, step - NS + 1)
                    for t in range(2):
                        o = ps[:, t * (P + E):(t + 1) * (P + E)]
                        pe.matmul(o, xnT[:, (2 * n + t) * P:(2 * n + t + 1) * P], wv1[:], start=True, stop=False)
                        last = pe.matmul(o, one_row[:], bias_v[:], start=False, stop=True)
                    last.then_inc(v_ps, 1)

            pe.wait_ge(wt1_done, WT1)
            pe.wait_ge(later_in, 16 * LATER)
            pe.wait_ge(comb_done, 1)
            experts(0)
            pe.wait_ge(mixed, E)
            turn(NS)
            project(NS)
            gate(NS)
            values1(NS)
            for q in range(4):
                rank(0, 0, q, (exp_done, 16 * NS - 1, 192 * (NS + 1)))
            turn_maxima(0)

            def body1(s, first, last):
                at, n = s - NS, 2 * (s - NS)
                last_step[0] = last
                score(s, 0, 0, first)
                if not first:
                    weigh(s - 1, 1, 2, False)
                score(s, 0, 1, first)
                if not first:
                    weigh(s - 1, 1, 3, False)
                    pe.wait_ge(negT_done, n + 1)
                    out_project(1, 2 * s - 1)
                    pe.wait_ge(x_done, 2 * s)
                if not last:
                    if not first:
                        pe.wait_ge(x_done, 2 * s - 1)
                    else:
                        pe.wait_ge(negT_done, 1)
                    experts(at + 1)
                else:
                    pe.wait_ge(routing, BOTH_AT)
                    count_tokens(rt[1])
                score(s, 0, 2, first)
                weigh(s, 0, 0, False)
                if not last:
                    pe.wait_ge(mixed, E * (at + 2))
                    turn(s + 1)
                score(s, 0, 3, first)
                weigh(s, 0, 1, False)
                if not last:
                    project(s + 1)
                rank(n + 1, 1, 0, (biased, 16 * at + 7, 192 * (s + 1)))
                weigh(s, 0, 2, False)
                if not last:
                    gate(s + 1)
                    values1(s + 1)
                rank(n + 1, 1, 1, None)
                weigh(s, 0, 3, False)
                rank(n + 1, 1, 2, None)
                rank(n + 1, 1, 3, None)
                if not last:
                    values_read(2 * s + 4)
                else:
                    values_read(2 * s + 2)
                out_project(0, 2 * s)
                turn_maxima(n + 1)
                if not last:
                    for q in range(4):
                        rank(n + 2, 0, q, (maxed, 8 * n + 15, 192 * (s + 2)))
                    turn_maxima(n + 2)
                for q in range(4):
                    score(s, 1, q, first)
                    if q >= 2:
                        weigh(s, 1, q - 2, False)
            steps(pe, body1, NS)
            weigh(2 * NS - 1, 1, 2, False)
            weigh(2 * NS - 1, 1, 3, False)
            out_project(1, 2 * B - 1)

            def shared(s):
                bias_and_comb(NS + s)
                pe.wait_ge(stat_in, 16 * (NS + s + 1))
                if not (isinstance(s, int) and s == 0):
                    pe.wait_ge(gelu_done, HC * s)
                for c in range(HC):
                    pe.matmul(psS[c // 2][:, c % 2, :], ws1_sb[:, c * P:(c + 1) * P], xstat[:], start=True, stop=True).then_inc(hid_ps, 1)
                bias_product(NS + s, bdiag1)
                pe.wait_ge(gelu_done, HC * (s + 1))
                if not (isinstance(s, int) and s == 0):
                    pe.wait_ge(y_used, s)
                for t in range(ST):
                    for c in range(HC):
                        last = pe.matmul(psN[0][:, t * D:(t + 1) * D], wide[2][:, c * SC + t * P:c * SC + (t + 1) * P],
                                         ws2_sb[:, c, :], start=(c == 0), stop=(c == HC - 1))
                last.then_inc(y_ps, 1)

            def turn_block(j, u, pair):
                pe.wait_ge(x_in[u], 32 * (pair + 1))
                ps = psB if u else psA
                for t in range(2):
                    last = pe.transpose(ps[:, t * P:(t + 1) * P], block_bufs["x", u][:, t * D:(t + 1) * D], ident[:])
                last.then_inc(xb_turned, 1)

            def hidden(j, u):
                pe.wait_ge(xb_done, j + 1)
                for c in range(HC):
                    pe.matmul(psS[u][:, c // 2, c % 2 * SLOTS:(c % 2 + 1) * SLOTS], block_bufs["w1", u][:, c * P:(c + 1) * P],
                              block_bufs["xT", u], start=True, stop=True).then_inc(hidb_ps, 1)

            def results(j, u, pair):
                pe.wait_ge(w2_in[u], 16 * (pair + 1))
                pe.wait_ge(gelub_done, HC * (j + 1))
                if not (isinstance(j, int) and j < 2):
                    pe.wait_ge(yb_done, j - 1)
                for t in range(2):
                    for c in range(HC):
                        last = pe.matmul(psN[u][:, t * D:(t + 1) * D], wide[u][:, c * SLOTS + t * P:c * SLOTS + (t + 1) * P],
                                         block_bufs["w2", u][:, c * D:(c + 1) * D], start=(c == 0), stop=(c == HC - 1))
                last.then_inc(yb_ps, 1)

            pe.wait_ge(heads_done, 2 * B)
            pe.wait_ge(x_done, 2 * B)
            pe.wait_ge(biased, 16 * NS)
            shared(0)
            with pe.Fori(1, FRONT) as s:
                shared(s)
            pe.wait_ge(y_used, FRONT)
            pe.wait_ge(bias_added, NS + FRONT)
            turn_block(0, 0, 0)
            turn_block(1, 1, 0)
            hidden(0, 0)
            for j in range(2):
                hidden(j + 1, 1 - j)
                turn_block(j + 2, j, 1)
                results(j, j, 0)
            with pe.Fori(1, BLOCKS // 2 - 1) as i:
                for u in range(2):
                    hidden(2 * i + u + 1, 1 - u)
                    turn_block(2 * i + u + 2, u, i + 1)
                    results(2 * i + u, u, i)
            hidden(BLOCKS - 1, 1)
            results(BLOCKS - 2, 0, BLOCKS // 2 - 1)
            results(BLOCKS - 1, 1, BLOCKS // 2 - 1)
            pe.wait_ge(yb_done, BLOCKS)
            with pe.Fori(FRONT, NS) as s:
                shared(s)


_INS = ["L0_attn_x", "L0_attn_Wqkv", "L0_attn_Wout", "L0_ffn_wg", "L0_ffn_W", "L0_ffn_b", "L1_attn_Wqkv", "L1_attn_bqkv",
        "L1_attn_Wout", "L1_attn_bout", "L1_attn_Wgate", "L1_attn_bgate", "L1_attn_pos_bias", "L1_ffn_gate_w",
        "L1_ffn_gate_b", "L1_ffn_w1", "L1_ffn_b1", "L1_ffn_w2", "L1_ffn_b2", "L1_ffn_ws1", "L1_ffn_bs1", "L1_ffn_ws2",
        "L1_ffn_bs2"]


def kernel(**inputs):
    import numpy as np
    import concourse.bacc as bacc
    from concourse.bass_utils import run_bass_kernel_spmd as run

    nc = bacc.Bacc("TRN2", target_bir_lowering=False, num_devices=1)
    arrays, args = {}, []
    for name in _INS:
        a = np.ascontiguousarray(inputs[name])
        arrays[f"in_{name}"] = a
        args.append(nc.dram_tensor(f"in_{name}", a.shape, mybir.dt.from_np(a.dtype), kind="ExternalInput").ap())
    args.append(nc.dram_tensor("out_x", (B, T, D), F32, kind="ExternalOutput").ap())
    build(nc, *args)
    r = run(nc, [arrays], core_ids=[0])
    return r.results[0]["out_x"]
```

```python
from contextlib import ExitStack

import concourse.bass as bass
from concourse import mybir

F32 = mybir.dt.float32
BF16 = mybir.dt.bfloat16
I32 = mybir.dt.int32
ALU = mybir.AluOpType
ACT = mybir.ActivationFunctionType
AX = mybir.AxisListType

P = 128
B, T, D = 16, 256, 128
H, DK = 16, 8
NT = B * T // P
ST = 4
NS = NT // ST
SC = ST * P
E = 8
CAP = B * T // E
TERMS = 6
GROUPS = (((0, 0, 0), (0, 1, 2)), ((1, 1), (0, 1)), ((2,), (0,)))
SROWS = 96
EPS = 1e-5
SCALE = DK ** -0.5
CLIP_HI = 22026.465794806718
CLIP_LO = 4.5399929762484854e-05
QW = 384
VW = 32


OFFSETS = tuple(range(33)) + (48, 64, 96, 128, 192)
MASKED = -1e30
LINE = 640
HID = 512
HC = HID // P
LW = 4 * P
SLOTS = 2 * P
BLOCKS = 2 * B * T // SLOTS + E
EARLY, EARLY1 = 12, 8
FRONT = 1


def build(nc, x, wqkv0, wout0, wg0, w_exp0, b_exp0, wqkv1, bqkv1, wout1, bout1, wgate1, bgate1, pos_bias,
          gate_w, gate_b, w1, b1, w2, b2, ws1, bs1, ws2, bs2, out):
    scr_q = nc.dram_tensor("scr_q", (2, 3, P, T), BF16, kind="Internal").ap()
    scr_k = nc.dram_tensor("scr_k", (2, 3, P, T), BF16, kind="Internal").ap()
    scr_line = nc.dram_tensor("scr_line", (2, H, LINE), F32, kind="Internal").ap()
    scr_x = nc.dram_tensor("scr_x", (NS, P, SC), F32, kind="Internal").ap()
    x_slots = nc.dram_tensor("x_slots", (BLOCKS * SLOTS, D), F32, kind="Internal").ap()
    y_slots0 = nc.dram_tensor("y_slots0", (2 * B * T, D), F32, kind="Internal").ap()
    y_slots = nc.dram_tensor("y_slots", (BLOCKS * SLOTS, D), F32, kind="Internal").ap()
    ctx = ExitStack()
    with ctx:
        def sb(name, shape, dt=F32):
            return ctx.enter_context(nc.sbuf_tensor(name, shape, dt))

        def sem(name):
            return ctx.enter_context(nc.semaphore(name))

        X = sb("X", [P, NT, D])
        XN = sb("XN", [P, NT, D])
        logit0 = sb("logit0", [P, NT, E])
        ident = sb("ident", [P, P])
        ident16 = sb("ident16", [P, P], BF16)
        flip = sb("flip", [P, P])
        flip16 = sb("flip16", [P, P], BF16)
        diagcap = sb("diagcap", [P, 2 * P])
        wT1 = sb("wT1", [P, 5, P])
        wv1 = sb("wv1", [P, P + E])
        w0T = sb("w0T", [P, E, P])
        bcol = sb("bcol", [P, E * HC + HC + 3])
        bqkg = sb("bqkg", [P, 3])
        one_row = sb("one_row", [1, P])
        bias_v = sb("bias_v", [1, P + E])
        bias_o = sb("bias_o", [1, P])
        bdiag1 = sb("bdiag1", [4 * E + 1, ST, D])
        upper = sb("upper", [P, P])
        ones_sq = sb("ones_sq", [P, P])
        rank8 = sb("rank8", [P, E])
        tables = sb("tables", [P, H * QW + H * T])
        btab = tables[:, 0:H * QW].rearrange("p (h c) -> p h c", h=H)
        bparts = tables[:, 0:H * QW].bitcast(BF16).rearrange("p (h k c) -> p h k c", h=H, k=3)
        btabq = tables[:, H * QW:H * (QW + T)].rearrange("p (h c) -> p h c", h=H)
        at, block_bufs = 0, {}
        for name, width in (("x", 2 * D), ("w1", HID), ("w2", HC * D), ("xT", SLOTS), ("y", 2 * D), ("b1", HC)):
            for u in range(2):
                block_bufs[name, u] = tables[:, at:at + width]
                at += width
        picked = tables[:, 0:2 * NT * D].rearrange("p (t k d) -> p t k d", k=2, d=D)
        ws1_sb = sb("ws1_sb", [P, HID])
        ws2_sb = sb("ws2_sb", [P, HC, D])
        pbT = sb("pbT", [H, len(OFFSETS)])
        lines = tables[0:H, 0:2 * LINE].rearrange("h (a c) -> h a c", a=2)
        slot0 = sb("slot0", [P, E])
        steps16 = sb("steps16", [P, B * T // SLOTS])
        numbers = sb("numbers", [P, BLOCKS])
        filled = sb("filled", [P, E])
        n_blocks = sb("n_blocks", [P, E])
        ends = [sb(f"ends{i}", [P, E]) for i in range(2)]
        block_e = sb("block_e", [P, BLOCKS])
        block_at = sb("block_at", [P, BLOCKS], I32)
        slots_at = sb("slots_at", [P, 2, NT], I32)
        slot0_of = sb("slot0_of", [P, E])
        token = sb("token", [P, NT])
        kept = sb("kept", [P, NT])
        gate0 = sb("gate0", [P, NT])
        slots0_at = sb("slots0_at", [P, NT + ST], I32)
        slots0_s = sb("slots0_s", [P, ST], I32)
        pool_unused = sb("pool_unused", [P, 1])
        xstat = sb("xstat", [P, SC])
        wraw = xstat[:].rearrange("p (c n) -> p c n", c=4)
        comb = sb("comb", [P, NT + ST, E])
        comb_s = sb("comb_s", [P, ST, E])
        combT = sb("combT", [4 * E + 1, P])
        acc = [sb(f"acc{i}", [P, ST, D]) for i in range(2)]
        spare = acc[0][:].rearrange("p t d -> p (t d)")
        passed = spare[:, 0:BLOCKS * E].rearrange("p (b e) -> p b e", e=E)
        many = spare[:, BLOCKS * E:BLOCKS * E + E * (B * T // SLOTS)].rearrange("p (e n) -> p e n", e=E)
        yg = acc[1]
        routes = sb("routes", [P, 3 * NT * E])
        rt = [routes[:, i * NT * E:(i + 1) * NT * E].rearrange("p (t e) -> p t e", e=E) for i in range(3)]
        rt += [xstat[:, i * NT * E:(i + 1) * NT * E].rearrange("p (t e) -> p t e", e=E) for i in range(2)]
        wraw1 = routes[:, 0:5 * P].rearrange("p (c n) -> p c n", c=5)
        rs = [sb(f"rs{i}", [P, NT]) for i in range(4)]
        egraw = sb("egraw", [P, SC])
        brow = egraw[0:E * HC + HC + 3, 0:P]
        eg = [sb(f"eg{u}", [P, T]) for u in range(2)]
        unused = sb("unused", [P, 9])
        smax = sb("smax", [P, 2, H])
        mrest = sb("mrest", [P, 2, H])
        mparts = sb("mparts", [P, 2, 3, H], BF16)
        mT = sb("mT", [P, T], BF16)
        pick_head = sb("pick_head", [P, H, P], BF16)
        wT0 = sb("wT0", [P, 4, P])
        wv0 = sb("wv0", [P, P + E])
        stats = sb("stats", [P, ST, 6])
        moments = sb("moments", [P, ST, 2])
        var_eps = sb("var_eps", [P, ST])
        minus_half = sb("minus_half", [P, ST])
        rstd0 = sb("rstd0", [P, ST])
        newton = sb("newton", [P, ST])
        rstd = sb("rstd", [P, ST])
        xn = sb("xn", [P, ST, D])
        xnT = sb("xnT", [P, SC])
        parts = {}
        for w in "qk":
            parts[w] = sb(f"{w}_parts", [P, 3, SC], BF16)
        rest = {w: sb(f"{w}_rest", [P, SC]) for w in "qk"}
        qs = [sb(f"qs{u}", [SROWS, H, T], BF16) for u in range(2)]
        ks = [sb(f"ks{u}", [SROWS, H, T], BF16) for u in range(2)]
        vraw = sb("vraw", [P, ST, D])
        vpad = [sb(f"vpad{u}", [P, 2, H, VW]) for u in range(2)]
        ones_pad = sb("ones_pad", [P, 4, VW])
        wide_all = sb("wide_all", [P, 16 * LW])
        wide = [wide_all[:, q * 4 * LW:(q + 1) * 4 * LW] for q in range(4)]
        probs = [w[:, 0:4 * QW].rearrange("p (g c) -> p g c", g=4) for w in wide]
        rden = sb("rden", [P, T])
        heads = sb("heads", [P, T])

        psS = [ctx.enter_context(nc.psum_tensor(f"psS{i}", [P, 2, 512], F32)) for i in range(2)]
        psN = [ctx.enter_context(nc.psum_tensor(f"psN{i}", [P, 512], F32)) for i in range(2)]
        psA = ctx.enter_context(nc.psum_tensor("psA", [P, 512], F32))
        psB = ctx.enter_context(nc.psum_tensor("psB", [P, 512], F32))

        x_first, x_rest = sem("x_first"), sem("x_rest")
        w_in, wt_ps, wt_done, consts = sem("w_in"), sem("wt_ps"), sem("wt_done"), sem("consts")
        stat_done, mom_done, var_done, pow_done = sem("stat_done"), sem("mom_done"), sem("var_done"), sem("pow_done")
        newt, xn_done, xn_turned, xnT_done, xnT_kept = sem("newt"), sem("xn_done"), sem("xn_turned"), sem("xnT_done"), sem("xnT_kept")
        q_ps, k_ps, v_ps = sem("q_ps"), sem("k_ps"), sem("v_ps")
        hi_done, rest_done, mid_done, lo_done = sem("hi_done"), sem("rest_done"), sem("mid_done"), sem("lo_done")
        v_out, logits_out, vpad_done = sem("v_out"), sem("logits_out"), sem("vpad_done")
        scratch_in = sem("scratch_in")
        qk_in = [sem("qk_in0"), sem("qk_in1")]
        scored, exp_done, clipped, weighed = sem("scored"), sem("exp_done"), sem("clipped"), sem("weighed")
        rden_done, heads_done, out_ps, x_done = sem("rden_done"), sem("heads_done"), sem("out_ps"), sem("x_done")
        stored = [sem("stored0"), sem("stored1")]
        masks_done, ones_done = sem("masks_done"), sem("ones_done")
        late_in, later_in, wt1_ps, wt1_done = sem("late_in"), sem("later_in"), sem("wt1_ps"), sem("wt1_done")
        lines_done, lines_in = sem("lines_done"), sem("lines_in")
        key_table_in, query_table_in, key_high = sem("key_table_in"), sem("query_table_in"), sem("key_high")
        pos_in, key_ps, key_done = sem("pos_in"), sem("key_ps"), sem("key_done")
        key_rest, key_mid, key_lo = sem("key_rest"), sem("key_mid"), sem("key_lo")
        query_ps, query_done, table_copied = sem("query_ps"), sem("query_done"), sem("table_copied")
        routing, loc_ps, route_exp, comb_done = sem("routing"), sem("loc_ps"), sem("route_exp"), sem("comb_done")
        stat_in, comb_s_done, combT_ps, combT_done = sem("stat_in"), sem("comb_s_done"), sem("combT_ps"), sem("combT_done")
        bias_ps = sem("bias_ps")
        gate_ps, eg_out, eg_done = sem("gate_ps"), sem("eg_out"), sem("eg_done")
        ranked, maxed, neg_done, negT_ps, negT_done = sem("ranked"), sem("maxed"), sem("neg_done"), sem("negT_ps"), sem("negT_done")
        neg_step, gated, lined, bias_added = sem("neg_step"), sem("gated"), sem("lined"), sem("bias_added")
        ONEHOT_AT, SHIFTED_AT, SECOND_AT, BOTH_AT = 5, 6, 37, 36
        WT1 = 5
        LATE, LATER = 10, 14
        heads_masked = sem("heads_masked")
        biased, exp1_done = sem("biased"), sem("exp1_done")
        xn_kept, slots_done, table_done = sem("xn_kept"), sem("slots_done"), sem("table_done")
        spare_in, slots_in = sem("spare_in"), sem("slots_in")
        x_in, w2_in, y_stored, picked_in = ([sem(f"{n}{u}") for u in range(2)] for n in ("x_in", "w2_in", "y_stored", "picked_in"))
        xb_turned, xb_done, b1_done, hidb_ps = sem("xb_turned"), sem("xb_done"), sem("b1_done"), sem("hidb_ps")
        gelub_done, yb_ps, yb_done, summed = sem("gelub_done"), sem("yb_ps"), sem("yb_done"), sem("summed")
        first_added = sem("first_added")
        slots0_done, slots0_in, spare0_in, b0_in = sem("slots0_done"), sem("slots0_in"), sem("spare0_in"), sem("b0_in")
        x0_in = [sem(f"x0_in{i}") for i in range(4)]
        y0_stored = sem("y0_stored")
        x0_turned, x0_done, y0_ps, y0_done = sem("x0_turned"), sem("x0_done"), sem("y0_ps"), sem("y0_done")
        pool_seen = sem("pool_seen")
        slots0_picked, yg_in, streamed = sem("slots0_picked"), sem("yg_in"), sem("streamed")
        hid_ps, gelu_done, y_ps, y_used = sem("hid_ps"), sem("gelu_done"), sem("y_ps"), sem("y_used")

        block = ctx.enter_context(nc.Block())

        def steps(engine, body, base=0):
            body(base, True, False)
            with engine.Fori(base + 1, base + NS - 2) as s:
                body(s, False, False)
            body(base + NS - 2, False, False)
            body(base + NS - 1, False, True)

        def routes_now(s):
            return isinstance(s, int) and s % NS == NS - 2

        def spread_over(t, pattern):
            return bass.AP(tensor=t[:].tensor, offset=t[:].offset, ap=pattern)

        x0_all = wide_all[:, 0:E * CAP]
        x0T = [wide_all[:, E * CAP + u * CAP:E * CAP + (u + 1) * CAP] for u in range(2)]
        b0_all = wide_all[:, E * CAP + 2 * CAP:E * CAP + 2 * CAP + E * D]

        PE_PAIRS = [i for i in range(H // 2) if 2 * i // 4 % 2 == 0]
        DVE_PAIRS = [i for i in range(H // 2) if i not in PE_PAIRS]
        remainders = [xstat[:], acc[0][:].rearrange("p t d -> p (t d)"), acc[1][:].rearrange("p t d -> p (t d)"), egraw[:]]

        x_tiles = x.rearrange("b (t p) d -> p (b t) d", p=P)

        @block.sync
        def _(sp):
            sp.dma_start(X[:, 0:ST, :], x_tiles[:, 0:ST, :]).then_inc(x_first, 16)
            sp.dma_start(pbT[:], pos_bias.rearrange("o h -> h o"), allow_slow_non_contiguous=True).then_inc(pos_in, 16)
            sp.dma_start(wraw[:, 0:3, :], wqkv0.rearrange("(c p) d -> p c d", p=P)).then_inc(w_in, 16)
            sp.dma_start(wraw[:, 3, :], wout0).then_inc(w_in, 16)
            sp.dma_start(wv0[:, P:P + E], wg0).then_inc(w_in, 16)
            sp.dma_start(X[:, ST:2 * ST, :], x_tiles[:, ST:2 * ST, :]).then_inc(x_rest, 16)
            sp.wait_ge(lines_done, 1)
            sp.dma_start(scr_line.rearrange("a h c -> h a c"), lines).then_inc(lines_in, 16)

            layer = [0]

            def late(dst, src):
                sp.dma_start(dst, src).then_inc(late_in, 16)

            def later(dst, src):
                sp.dma_start(dst, src).then_inc(later_in, 16)

            late(wraw1[:, 0:3, :], wqkv1.rearrange("(c p) d -> p c d", p=P))
            late(wraw1[:, 3, :], wout1)
            late(wraw1[:, 4, :], wgate1)
            for i in range(2):
                late(acc[i][:], w_exp0[4 * i:4 * i + 4].rearrange("e f h -> f e h"))
            late(brow[0:E * HC, :], b1.rearrange("e (c p) -> (e c) p", p=P))
            late(brow[E * HC:E * HC + HC, :], bs1.rearrange("(c p) -> c p", p=P))
            for c in range(2):
                sp.dma_start(brow[E * HC + HC + c:E * HC + HC + c + 1, :].rearrange("c (d h) -> c d h", h=H),
                             bqkv1[c * P:(c + 1) * P].rearrange("(c h d) -> c d h", c=1, h=H),
                             allow_slow_non_contiguous=True).then_inc(late_in, 16)
            late(brow[E * HC + HC + 2:E * HC + HC + 3, :], bgate1.rearrange("(c p) -> c p", p=P))

            def spread(step):
                for n, (scr, w) in enumerate(((scr_q, "q"), (scr_k, "k"))):
                    sp.wait_ge(lo_done, 2 * step + n + 1)
                    for u in range(2):
                        sp.dma_start(scr[u].rearrange("i p t -> p i t"), parts[w][:, :, u * T:(u + 1) * T]).then_inc(scratch_in, 16)
                at = step - NS * layer[0]
                sp.dma_start(XN[:, bass.ds(at * ST, ST), :], xn[:]).then_inc(xn_kept, 16)
                if layer[0]:
                    sp.dma_start(scr_x[bass.ds(at, 1)].rearrange("a p n -> (a p) n"), xnT[:]).then_inc(xnT_kept, 16)
                sp.wait_ge(scratch_in, 64 * (step + 1))

            def load(u):
                for n, (scr, to) in enumerate(((scr_q, qs), (scr_k, ks))):
                    row = 0
                    for group in GROUPS:
                        which = group[n]
                        step_of_parts = P * T * (which[1] - which[0] if len(which) > 1 else 0)
                        rows = DK * len(which)
                        sp.dma_start(to[u][row:row + rows, :, :].rearrange("r h t -> r (h t)"),
                                     bass.AP(tensor=scr.tensor, offset=scr.offset + (3 * u + which[0]) * P * T,
                                             ap=[[H * T, DK], [step_of_parts, len(which)], [1, H * T]]))\
                          .then_inc(qk_in[u], 16)
                        row += rows

            sp.wait_ge(lines_in, 16)
            by_key = bass.AP(tensor=scr_line.tensor, offset=scr_line.offset + T - (P - 1), ap=[[1, P], [LINE, H], [1, T]])
            sp.dma_start(btab[:, :, P:QW], by_key).then_inc(key_table_in, 16)
            by_query = bass.AP(tensor=scr_line.tensor, offset=scr_line.offset + H * LINE + LINE - 2 * T,
                               ap=[[1, P], [LINE, H], [1, T]])
            sp.dma_start(btabq, by_query).then_inc(query_table_in, 16)

            sp.wait_ge(consts, 7)
            spread(0)
            load(0)
            load(1)
            sp.dma_start(X[:, 2 * ST:NT, :], x_tiles[:, 2 * ST:NT, :]).then_inc(x_rest, 16)

            def fill_slots(s):
                for dst, rows, done in ((x_slots, BLOCKS * SLOTS // NS, spare_in), (y_slots0[B * T:, :], B * T // NS, spare0_in)):
                    sp.dma_start(dst[bass.ds(s * rows, rows), :].rearrange("(a p) d -> p a d", p=P),
                                 spread_over(ones_sq, [[P, P], [0, rows // P], [1, D]])).then_inc(done, 16)

            fill_slots(0)
            later(bias_v[:, 0:P], bqkv1[2 * P:3 * P].rearrange("(a n) -> a n", a=1))
            later(bias_v[:, P:P + E], gate_b.rearrange("(a n) -> a n", a=1))
            later(bias_o[:], bout1.rearrange("(a n) -> a n", a=1))
            later(wv1[:, P:P + E], gate_w)
            later(ws1_sb[:], ws1)
            later(ws2_sb[:], ws2.rearrange("(c p) n -> p c n", p=P))
            for t in range(ST):
                later(bdiag1[E * t:E * (t + 1), t, :], b2)
                later(bdiag1[4 * E:4 * E + 1, t, :], bs2.rearrange("(a n) -> a n", a=1))

            def body(s, first, last):
                if last:
                    return
                sp.wait_ge(qk_in[1], 96 * (s + 1))
                spread(s + 1)
                sp.wait_ge(scored, 16 * s + 8)
                load(0)
                fill_slots(s + 1)
                sp.wait_ge(scored, 16 * s + 16)
                load(1)
            steps(sp, body)

            def fetch(at):
                sp.dma_start(xstat[:], scr_x[bass.ds(at, 1)].rearrange("a p n -> (a p) n")).then_inc(stat_in, 16)

            layer[0] = 1
            sp.wait_ge(weighed, 8 * NS)
            sp.dma_start(b0_all, b_exp0.rearrange("(a e) d -> a (e d)", a=1).to_broadcast([P, E * D])).then_inc(b0_in, 16)
            sp.wait_ge(slots0_in, 16 * NT)
            quarter = E * CAP // 4
            for i in range(4):
                sp.dma_start(x0_all[:, i * quarter:(i + 1) * quarter].rearrange("p (a d) -> p a d", d=D),
                             x_slots[i * quarter:(i + 1) * quarter, :].rearrange("(a p) d -> p a d", p=P)).then_inc(x0_in[i], 16)
            for i in range(4):
                sp.wait_ge(y0_done, 2 * (i + 1))
                sp.dma_start(y_slots0[i * quarter:(i + 1) * quarter, :].rearrange("(a p) d -> p a d", p=P),
                             x0_all[:, i * quarter:(i + 1) * quarter].rearrange("p (a d) -> p a d", d=D)).then_inc(y0_stored, 16)
            sp.wait_ge(qk_in[1], 96 * NS)
            spread(NS)
            sp.wait_ge(scored, 16 * NS)
            load(0)
            load(1)

            def body1(s, first, last):
                if not last:
                    sp.wait_ge(qk_in[1], 96 * (s + 1))
                    spread(s + 1)
                    sp.wait_ge(scored, 16 * s + 8)
                    load(0)
                if not last:
                    sp.wait_ge(scored, 16 * s + 16)
                    load(1)
            steps(sp, body1, NS)

            def fetch_shared(step):
                sp.wait_ge(hid_ps, HC * step)
                fetch(step)

            def load_block(j, u):
                e = sp.value_load(block_at[0:1, bass.ds(j, 1)], min_val=0, max_val=E - 1)
                if not (isinstance(j, int) and j < 2):
                    sp.wait_ge(hidb_ps, HC * (j - 1))
                sp.dma_start(block_bufs["x", u].rearrange("p (a d) -> p a d", a=2),
                             x_slots[bass.ds(j * SLOTS, SLOTS), :].rearrange("(a p) d -> p a d", p=P)).then_inc(x_in[u], 16)
                sp.dma_start(block_bufs["w1", u], w1[bass.ds(e, 1)].rearrange("a p n -> (a p) n")).then_inc(x_in[u], 16)

            def load_second(j, u):
                e = sp.value_load(block_at[0:1, bass.ds(j, 1)], min_val=0, max_val=E - 1)
                if not (isinstance(j, int) and j < 2):
                    sp.wait_ge(yb_ps, j - 1)
                sp.dma_start(block_bufs["w2", u].rearrange("p (c n) -> p c n", c=HC),
                             w2[bass.ds(e, 1)].rearrange("a (c p) n -> p (a c) n", p=P)).then_inc(w2_in[u], 16)

            def store_block(j, u):
                sp.wait_ge(yb_done, j + 1)
                sp.dma_start(y_slots[bass.ds(j * SLOTS, SLOTS), :].rearrange("(a p) d -> p a d", p=P),
                             block_bufs["y", u].rearrange("p (a d) -> p a d", a=2)).then_inc(y_stored[u], 16)

            sp.wait_ge(xnT_kept, 16 * NS)
            sp.wait_ge(table_done, 1)
            fetch(0)
            sp.wait_ge(maxed, 16 * NS)
            sp.wait_ge(biased, 16 * NS)
            sp.wait_ge(scored, 32 * NS)
            sp.wait_ge(slots_in, 32 * NT)
            for j in range(2):
                load_block(j, j)
                load_second(j, j)
            load_block(2, 0)
            fetch_shared(FRONT)
            with sp.Fori(0, BLOCKS // 2 - 2) as i:
                for u in range(2):
                    load_block(2 * i + u + 3, 1 - u)
                    load_second(2 * i + u + 2, u)
                    store_block(2 * i + u, u)
            load_block(BLOCKS - 1, 1)
            load_second(BLOCKS - 2, 0)
            store_block(BLOCKS - 4, 0)
            load_second(BLOCKS - 1, 1)
            for j in range(BLOCKS - 3, BLOCKS):
                store_block(j, j % 2)
            fetch_shared(FRONT + 1)
            out_tiles = out.rearrange("b (t p) d -> p (b t) d", p=P)

            def store(s, u):
                sp.wait_ge(summed, s + 1)
                sp.dma_start(out_tiles[:, bass.ds(s * ST, ST), :], acc[u][:]).then_inc(stored[u], 16)
            with sp.Fori(0, (NS - FRONT - 1) // 2 - 1) as i:
                for u in range(2):
                    fetch_shared(FRONT + 2 * i + u + 2)
                    store(2 * i + u, u)
            fetch_shared(NS - 1)
            with sp.Fori((NS - FRONT - 1) // 2 - 1, NS // 2) as i:
                for u in range(2):
                    store(2 * i + u, u)
            for u in range(2):
                sp.wait_ge(stored[u], 8 * NS)

        @block.gpsimd
        def _(pool):
            pool.memset(ident[:], 0.0).then_inc(consts, 1)
            pool.memset(diagcap[:], CLIP_HI).then_inc(consts, 1)
            pool.memset(flip[:], 0.0).then_inc(consts, 1)
            pool.memset(ones_sq[:], 1.0).then_inc(consts, 1)
            pool.wait_ge(consts, 4)
            pool.affine_select(out=ident[:], in_=ident[:], compare_op=ALU.not_equal, fill=1.0, base=0,
                               pattern=[[-1, P]], channel_multiplier=1).then_inc(masks_done, 1)
            pool.affine_select(out=upper[:], in_=ones_sq[:], compare_op=ALU.is_gt, fill=0.0, base=0,
                               pattern=[[1, P]], channel_multiplier=-1).then_inc(masks_done, 1)
            pool.affine_select(out=flip[:], in_=flip[:], compare_op=ALU.not_equal, fill=1.0, base=-(P - 1),
                               pattern=[[1, P]], channel_multiplier=1).then_inc(masks_done, 1)
            both = diagcap[:].rearrange("p (a n) -> p a n", a=2)
            pool.affine_select(out=both, in_=both, compare_op=ALU.is_ge, fill=0.0, base=0,
                               pattern=[[0, 2], [1, P]], channel_multiplier=-1).then_inc(masks_done, 1)
            pool.wait_ge(masks_done, 4)
            pool.tensor_copy(ident16[:], ident[:]).then_inc(consts, 1)
            pool.tensor_copy(flip16[:], flip[:])
            pool.memset(minus_half[:], -0.5).then_inc(consts, 1)
            pool.iota(slot0_of[:], pattern=[[CAP, E]], base=0, channel_multiplier=0, allow_small_or_imprecise_dtypes=True)
            pool.iota(token[:], pattern=[[P, NT]], base=B * T, channel_multiplier=1, allow_small_or_imprecise_dtypes=True)
            pool.iota(steps16[:], pattern=[[SLOTS, B * T // SLOTS]], base=0, channel_multiplier=0,
                      allow_small_or_imprecise_dtypes=True)
            pool.iota(numbers[:], pattern=[[1, BLOCKS]], base=0, channel_multiplier=0, allow_small_or_imprecise_dtypes=True)
            pool.memset(bdiag1[:], 0.0)

            def power(step):
                pool.wait_ge(var_done, step + 1)
                pool.tensor_tensor(rstd0[:], var_eps[:], minus_half[:], ALU.pow).then_inc(pow_done, 1)

            pool.wait_ge(consts, 6)
            power(0)
            for u in range(2):
                pool.memset(qs[u][:].bitcast(F32)[0:SROWS], 0.0)
                pool.memset(ks[u][:].bitcast(F32)[0:SROWS], 0.0)
                last = pool.memset(vpad[u][:], 0.0)
            last.then_inc(consts, 1)

            def low(step):
                for n, w in enumerate("qk"):
                    pool.wait_ge(mid_done, 2 * step + n + 1)
                    pool.tensor_tensor(parts[w][:, 2, :], rest[w][:], parts[w][:, 1, :], ALU.subtract).then_inc(lo_done, 1)

            def pad(step, u, wait_batch):
                pool.wait_ge(v_out, 2 * (step + 1))
                if wait_batch is not None:
                    pool.wait_ge(weighed, wait_batch)
                pool.tensor_tensor(spread_over(vpad[u], [[2 * H * VW, P], [4 * VW, 8], [VW + DK, 4], [1, DK]]),
                                   vraw[:, 2 * u:2 * u + 2, :].rearrange("p t (g j d) -> p (t g) j d", g=4, j=4),
                                   spread_over(ones_sq, [[P, P], [0, 8], [0, 4], [1, DK]]), ALU.mult).then_inc(vpad_done, 1)

            def gates(step, u, read):
                pool.wait_ge(eg_out, step - NS + 1)
                if read is not None:
                    pool.wait_ge(heads_done, read)
                pool.tensor_tensor(eg[u][:], egraw[:, u * T:(u + 1) * T], spread_over(ones_sq, [[P, P], [0, 2], [1, P]]),
                                   ALU.add).then_inc(eg_done, 1)

            pool.wait_ge(consts, 7)
            low(0)
            pad(0, 0, None)
            pad(0, 1, None)
            for n, i in enumerate(PE_PAIRS):
                part = bparts[:, 2 * i:2 * i + 2]
                left = remainders[n].rearrange("p (h c) -> p h c", h=2)
                pool.wait_ge(key_rest, n + 1)
                pool.tensor_copy(part[:, :, 1, :], left).then_inc(key_mid, 1)
                pool.wait_ge(key_mid, n + 1)
                pool.tensor_tensor(part[:, :, 2, :], left, part[:, :, 1, :], ALU.subtract).then_inc(key_lo, 1)
            def scatter0(start, end):
                for t in range(start, end):
                    pool.indirect_dma_start(x_slots, bass.IndirectOffsetOnAxis(ap=slots0_at[:, t:t + 1], axis=0),
                                            XN[:, t, :], None).then_inc(slots0_in, 16)

            def for_layer_1():
                pool.memset(pick_head[:], 0.0).then_inc(heads_masked, 1)
                for k in range(3):
                    pool.wait_ge(heads_masked, k + 1)
                    pool.affine_select(out=pick_head[:], in_=pick_head[:], compare_op=ALU.not_equal, fill=1.0, base=-H * k,
                                       pattern=[[-1, H], [0, P]], channel_multiplier=1).then_inc(heads_masked, 1)
                pool.wait_ge(key_done, len(DVE_PAIRS))
                for a in range(2):
                    rows = btab[:, 8 * a + 4:8 * a + 8, :]
                    last = pool.tensor_tensor(rows[:, :, 0:P], rows[:, :, P:2 * P], spread_over(ones_sq, [[P, P], [0, 4], [1, P]]),
                                              ALU.mult)
                last.then_inc(table_copied, 1)

            def body(s, first, last):
                if last:
                    return
                power(s + 1)
                low(s + 1)
                pad(s + 1, 0, 8 * s + 4)
                if routes_now(s):
                    pool.wait_ge(xn_kept, 16 * NS)
                    pool.wait_ge(slots0_done, 1)
                    pool.wait_ge(spare_in, 16 * NS)
                    scatter0(0, EARLY)
                pad(s + 1, 1, 8 * s + 8)
            steps(pool, body)

            scatter0(EARLY, NT)
            for_layer_1()

            def gather0(at):
                pool.wait_ge(slots0_picked, at + 1)
                if not (isinstance(at, int) and at == 0):
                    pool.wait_ge(pool_seen, at)
                pool.tensor_tensor(pool_unused[:], ones_sq[:, 0:1], ones_sq[:, 0:1], ALU.mult).then_inc(pool_seen, 1)
                for t in range(ST):
                    pool.indirect_dma_start(yg[:, t, :], None, y_slots0,
                                            bass.IndirectOffsetOnAxis(ap=slots0_s[:, t:t + 1], axis=0)).then_inc(yg_in, 16)

            pool.wait_ge(spare0_in, 16 * NS)
            pool.wait_ge(y0_stored, 64)
            gather0(0)

            power(NS)
            gather0(1)
            low(NS)
            pad(NS, 0, 8 * NS - 4)
            pad(NS, 1, 8 * NS)
            gates(NS, 0, None)
            gates(NS, 1, None)

            def scatter1(start, end):
                if start == 0:
                    pool.wait_ge(xn_kept, 32 * NS)
                    pool.wait_ge(slots_done, 1)
                for t in range(start, end):
                    for k in range(2):
                        pool.indirect_dma_start(x_slots, bass.IndirectOffsetOnAxis(ap=slots_at[:, k, t:t + 1], axis=0),
                                                XN[:, t, :], None).then_inc(slots_in, 16)

            def body1(s, first, last):
                if not last:
                    power(s + 1)
                    gather0(s - NS + 2)
                if last:
                    scatter1(0, EARLY1)
                if not first:
                    pad(s, 1, 8 * s)
                    gates(s, 1, 2 * s)
                if last:
                    return
                low(s + 1)
                pad(s + 1, 0, 8 * s + 4)
                gates(s + 1, 0, 2 * s + 1)
            steps(pool, body1, NS)

            scatter1(EARLY1, NT)
            for u in range(2):
                pool.wait_ge(y_stored[u], 8 * BLOCKS)
            for t in range(NT):
                u, before = t // ST % 2, t // (2 * ST)
                if t % ST == 0 and before:
                    pool.wait_ge(picked_in[u], 32 * ST * before)
                for k in range(2):
                    pool.indirect_dma_start(picked[:, t, k, :], None, y_slots,
                                            bass.IndirectOffsetOnAxis(ap=slots_at[:, k, t:t + 1], axis=0))\
                        .then_inc(picked_in[u], 16)

        @block.vector
        def _(dve):
            def tokens(step, t):
                return X[:, bass.ds((step - NS * layer[0]) * ST + t, 1), :].rearrange("p a d -> p (a d)")

            layer = [0]

            def moments_of(step):
                for t in range(ST):
                    dve.bn_stats(stats[:, t, :], tokens(step, t)).then_inc(stat_done, 1)
                dve.wait_ge(stat_done, (step + 1) * ST)
                dve.memset(unused[:, 8:9], 0.0)
                for t in range(ST):
                    dve.bn_aggr(moments[:, t, :], stats[:, t, :]).then_inc(mom_done, 1)
                dve.wait_ge(mom_done, (step + 1) * ST)
                dve.tensor_scalar(var_eps[:], moments[:, :, 1], EPS, None, ALU.add).then_inc(var_done, 1)

            def normalise(step):
                dve.wait_ge(pow_done, step + 1)
                dve.tensor_tensor(newton[:], rstd0[:], rstd0[:], ALU.mult).then_inc(newt, 1)
                dve.wait_ge(newt, 4 * step + 1)
                dve.tensor_tensor(newton[:], newton[:], var_eps[:], ALU.mult).then_inc(newt, 1)
                dve.wait_ge(newt, 4 * step + 2)
                dve.tensor_scalar(newton[:], newton[:], -0.5, 1.5, ALU.mult, ALU.add).then_inc(newt, 1)
                dve.wait_ge(newt, 4 * step + 3)
                dve.tensor_tensor(rstd[:], rstd0[:], newton[:], ALU.mult).then_inc(newt, 1)
                dve.wait_ge(newt, 4 * step + 4)
                if not (isinstance(step, int) and step == 0):
                    dve.wait_ge(xn_kept, 16 * step)
                for t in range(ST):
                    last = dve.tensor_scalar(xn[:, t, :], tokens(step, t),
                                             moments[:, t, 0:1], rstd[:, t:t + 1], ALU.subtract, ALU.mult)
                last.then_inc(xn_done, 1)

            def split(step):
                for n, (w, ps) in enumerate((("q", psA), ("k", psB))):
                    dve.wait_ge(hi_done, 2 * step + n + 1)
                    if layer[0]:
                        dve.scalar_tensor_tensor(out=rest[w][:], in0=ps[:], scalar=bqkg[:, n:n + 1], in1=parts[w][:, 0, :],
                                                 op0=ALU.add, op1=ALU.subtract).then_inc(rest_done, 1)
                    else:
                        dve.tensor_tensor(rest[w][:], ps[:], parts[w][:, 0, :], ALU.subtract).then_inc(rest_done, 1)
                    dve.wait_ge(rest_done, 2 * step + n + 1)
                    dve.tensor_copy(parts[w][:, 1, :], rest[w][:]).then_inc(mid_done, 1)

            def clip(s, u, q):
                dve.wait_ge(exp_done, 16 * s + 8 * u + 2 * q + 2)
                dve.scalar_tensor_tensor(out=probs[q][:, :, 0:2 * P], in0=probs[q][:, :, 0:2 * P], scalar=CLIP_LO,
                                         in1=bass.AP(tensor=diagcap[:].tensor, offset=diagcap[:].offset,
                                                     ap=[[2 * P, P], [0, 4], [1, 2 * P]]),
                                         op0=ALU.max, op1=ALU.min).then_inc(clipped, 1)
                dve.tensor_scalar(probs[q][:, :, 2 * P:QW], probs[q][:, :, 2 * P:QW], CLIP_LO, CLIP_HI,
                                  ALU.max, ALU.min).then_inc(clipped, 1)

            def finish(u, n):
                dve.wait_ge(weighed, 4 * n + 4)
                if layer[0]:
                    dve.wait_ge(eg_done, n - B + 1)
                    dve.tensor_tensor(rden[:], psN[u][:, T:2 * T], eg[u][:], ALU.mult).then_inc(gated, 1)
                    dve.wait_ge(gated, n - B + 1)
                    dve.reciprocal(rden[:], rden[:]).then_inc(rden_done, 1)
                else:
                    dve.reciprocal(rden[:], psN[u][:, T:2 * T]).then_inc(rden_done, 1)
                dve.wait_ge(rden_done, n + 1)
                if not (isinstance(n, int) and n == 0):
                    dve.wait_ge(out_ps, n)
                dve.tensor_tensor(heads[:], psN[u][:, 0:T], rden[:], ALU.mult).then_inc(heads_done, 1)

            def add_out(u, n):
                dve.wait_ge(out_ps, n + 1)
                ps = psB if u else psA
                dst = X[:, bass.ds(2 * n, 2), :]
                dve.tensor_tensor(dst, dst, ps[:, 0:2 * D].rearrange("p (t d) -> p t d", t=2), ALU.add).then_inc(x_done, 1)

            dve.memset(ones_pad[:], 0.0).then_inc(ones_done, 1)
            dve.wait_ge(ones_done, 1)
            for j in range(4):
                last = dve.memset(ones_pad[:, j, DK * j:DK * (j + 1)], 1.0)
            last.then_inc(ones_done, 1)
            for e in range(E):
                last = dve.memset(rank8[:, e:e + 1], float(E - e))
            dve.memset(one_row[:], 1.0)
            dve.memset(combT[4 * E:4 * E + 1, :], 1.0)
            dve.memset(slots0_at[:, NT:], 0)
            dve.memset(comb[:, NT:, :], 0.0)
            dve.memset(mT[:], 0.0).then_inc(ones_done, 1)
            dve.memset(lines, MASKED).then_inc(lined, 1)
            dve.wait_ge(lined, 1)
            dve.wait_ge(pos_in, 16)
            run = 33
            dve.tensor_copy(lines[:, 0, T:T + run], pbT[:, 0:run])
            back = LINE - 1 - T
            dve.tensor_copy(lines[:, 1, back - run + 1:back + 1],
                            bass.AP(tensor=pbT[:].tensor, offset=pbT[:].offset + run - 1, ap=[[len(OFFSETS), H], [-1, run]]))
            for n in range(run, len(OFFSETS)):
                dve.tensor_copy(lines[:, 0, T + OFFSETS[n]:T + OFFSETS[n] + 1], pbT[:, n:n + 1])
                last = dve.tensor_copy(lines[:, 1, back - OFFSETS[n]:back - OFFSETS[n] + 1], pbT[:, n:n + 1])
            last.then_inc(lines_done, 1)
            dve.wait_ge(x_first, 16)
            moments_of(0)
            normalise(0)
            dve.wait_ge(masks_done, 4)
            split(0)
            dve.wait_ge(wt1_ps, 4)
            for i in range(H // 2):
                if i % 2 == 0:
                    n = i // 2
                    dve.wait_ge(key_high, n + 1)
                    pair = 2 * PE_PAIRS[n]
                    dve.tensor_tensor(remainders[n].rearrange("p (h c) -> p h c", h=2), btab[:, pair:pair + 2, P:QW],
                                      bparts[:, pair:pair + 2, 0, :], ALU.subtract).then_inc(key_rest, 1)
                dve.wait_ge(query_ps, i + 1)
                dve.tensor_copy(btabq[:, 2 * i:2 * i + 2, :], psS[1][:, i % 2, :].rearrange("p (h c) -> p h c", h=2)).then_inc(query_done, 1)

            count = [0]

            def link(instruction):
                count[0] += 1
                instruction.then_inc(routing, 1)
                dve.wait_ge(routing, count[0])

            def wide3(t):
                return spread_over(t, [[NT, P], [1, NT], [0, E]])

            def first_of(onehot, top, logits):
                ranks = spread_over(rank8, [[E, P], [0, NT], [1, E]])
                link(dve.tensor_tensor(onehot, logits, wide3(top), ALU.is_equal))
                link(dve.tensor_tensor(onehot, onehot, ranks, ALU.mult))
                link(dve.tensor_reduce(out=rs[3][:], in_=onehot, axis=AX.X, op=ALU.max))
                link(dve.tensor_tensor(onehot, onehot, wide3(rs[3]), ALU.is_equal))

            def places(a, b, n_loc):
                dve.wait_ge(loc_ps, n_loc)
                dve.memset(rt[a][:, 0, :], 0.0)
                link(dve.tensor_copy(rt[a][:, 1:NT, :], totals[:, 0:NT - 1, :]))
                k = 1
                while k < NT:
                    dve.tensor_copy(rt[b][:, 0:k, :], rt[a][:, 0:k, :])
                    link(dve.tensor_tensor(rt[b][:, k:NT, :], rt[a][:, k:NT, :], rt[a][:, 0:NT - k, :], ALU.add))
                    a, b, k = b, a, 2 * k
                link(dve.tensor_tensor(rt[b], psA[:, 0:NT * E].rearrange("p (t e) -> p t e", e=E), rt[a], ALU.add))
                return a, b

            totals = psA[:, NT * E:2 * NT * E].rearrange("p (t e) -> p t e", e=E)
            def choose0():
                dve.wait_ge(logits_out, 2 * NS)
                link(dve.tensor_reduce(out=rs[0][:], in_=logit0[:], axis=AX.X, op=ALU.max))
                first_of(rt[0], rs[0], logit0[:])
                assert count[0] == ONEHOT_AT
                link(dve.tensor_tensor(rt[1], logit0[:], wide3(rs[0]), ALU.subtract))
                assert count[0] == SHIFTED_AT
                dve.wait_ge(route_exp, 1)
                link(dve.tensor_reduce(out=rs[1][:], in_=rt[1], axis=AX.X, op=ALU.add))
                link(dve.reciprocal(rs[2][:], rs[1][:]))

            def slots0():
                a, b = places(1, 2, 1)
                link(dve.tensor_scalar(rt[a], rt[b], float(CAP), None, ALU.is_lt))
                link(dve.tensor_tensor(rt[0], rt[a], rt[0], ALU.mult))
                link(dve.tensor_reduce(out=kept[:], in_=rt[0], axis=AX.X, op=ALU.add))
                link(dve.tensor_tensor(rt[b], rt[b], spread_over(slot0_of, [[E, P], [0, NT], [1, E]]), ALU.add))
                link(dve.tensor_tensor(rt[b], rt[b], rt[0], ALU.mult))
                link(dve.tensor_reduce(out=rs[0][:], in_=rt[b], axis=AX.X, op=ALU.add))
                dve.tensor_tensor(gate0[:], kept[:], rs[2][:], ALU.mult)
                link(dve.tensor_scalar(rs[1][:], kept[:], -1.0, 1.0, ALU.mult, ALU.add))
                link(dve.tensor_tensor(rs[1][:], rs[1][:], token[:], ALU.mult))
                link(dve.tensor_tensor(rs[0][:], rs[0][:], rs[1][:], ALU.add))
                dve.tensor_copy(slots0_at[:, 0:NT], rs[0][:]).then_inc(slots0_done, 1)

            def body(s, first, last):
                if not last:
                    dve.wait_ge(x_rest, 16 if first else 32)
                    moments_of(s + 1)
                clip(s, 0, 0)
                clip(s, 0, 1)
                if not first:
                    finish(1, 2 * s - 1)
                if not last:
                    normalise(s + 1)
                clip(s, 0, 2)
                if not first:
                    add_out(1, 2 * s - 1)
                clip(s, 0, 3)
                if not last:
                    split(s + 1)
                clip(s, 1, 0)
                if routes_now(s):
                    choose0()
                clip(s, 1, 1)
                if routes_now(s):
                    slots0()
                finish(0, 2 * s)
                clip(s, 1, 2)
                add_out(0, 2 * s)
                clip(s, 1, 3)
            steps(dve, body)

            finish(1, B - 1)
            add_out(1, B - 1)

            dve.wait_ge(b0_in, 16)
            for e in range(E):
                dve.wait_ge(y0_ps, e + 1)
                dve.tensor_tensor(x0_all[:, e * CAP:(e + 1) * CAP].rearrange("p (t d) -> p t d", d=D),
                                  psN[e % 2][:].rearrange("p (t d) -> p t d", d=D),
                                  bass.AP(tensor=b0_all.tensor, offset=b0_all.offset + e * D, ap=[b0_all.ap[0], [0, ST], [1, D]]),
                                  ALU.add).then_inc(y0_done, 1)

            layer[0] = 1

            def pick(at):
                dve.tensor_copy(slots0_s[:], slots0_at[:, bass.ds(at * ST, ST)]).then_inc(slots0_picked, 1)

            def stream(at):
                dve.wait_ge(yg_in, 64 * (at + 1))
                for t in range(ST):
                    tile = X[:, bass.ds(at * ST + t, 1), :].rearrange("p a d -> p (a d)")
                    last = dve.scalar_tensor_tensor(out=tile, in0=yg[:, t, :], scalar=gate0[:, bass.ds(at * ST + t, 1)],
                                                    in1=tile, op0=ALU.mult, op1=ALU.add)
                last.then_inc(streamed, 1)
                dve.wait_ge(streamed, at + 1)
                pick(at + 1)

            def add_bias(s, u, q):
                for half in range(2):
                    dve.wait_ge(scored, 16 * s + 8 * u + 2 * q + half + 1)
                    if half == 0:
                        dve.wait_ge(weighed, 8 * s + 4 * u + q - 3)
                    dve.tensor_tensor(probs[q][:, 2 * half + 1, :], psS[half][:, 1, 0:QW], btab[:, 8 * half + 4 + q, :],
                                      ALU.add).then_inc(biased, 1)

            def maxima(n, q):
                for half in range(2):
                    dve.wait_ge(ranked, 8 * n + 2 * q + half + 1)
                    at = 2 * q + half
                    dve.memset(unused[:, at:at + 1], 0.0)
                    for i in range(2):
                        h = 4 * (2 * half + i) + q
                        dve.tensor_tensor_reduce(out=psS[half][:, i, 0:P], in0=psS[half][:, i, 0:P], in1=btabq[:, h, P:T], scale=1.0,
                                                 scalar=-3e38, op0=ALU.add, op1=ALU.max, accum_out=smax[:, 0, h:h + 1])
                        last = dve.tensor_tensor_reduce(out=psS[half][:, i, P:QW], in0=psS[half][:, i, P:QW], in1=btabq[:, h, :], scale=1.0,
                                                        scalar=-3e38, op0=ALU.add, op1=ALU.max, accum_out=smax[:, 1, h:h + 1])
                    last.then_inc(maxed, 1)

            def negate(n):
                dve.wait_ge(maxed, 8 * n + 8)
                if not (isinstance(n, int) and n == 0):
                    dve.wait_ge(negT_ps, n)
                dve.tensor_scalar(mparts[:, :, 0, :], smax[:], -1.0, None, ALU.mult).then_inc(neg_step, 1)
                dve.wait_ge(neg_step, 3 * n + 1)
                dve.scalar_tensor_tensor(out=mrest[:], in0=smax[:], scalar=-1.0, in1=mparts[:, :, 0, :], op0=ALU.mult,
                                         op1=ALU.subtract).then_inc(neg_step, 1)
                dve.wait_ge(neg_step, 3 * n + 2)
                dve.tensor_copy(mparts[:, :, 1, :], mrest[:]).then_inc(neg_step, 1)
                dve.wait_ge(neg_step, 3 * n + 3)
                dve.tensor_tensor(mparts[:, :, 2, :], mrest[:], mparts[:, :, 1, :], ALU.subtract).then_inc(neg_done, 1)

            dve.wait_ge(query_done, H // 2)
            dve.wait_ge(table_copied, 1)
            dve.wait_ge(wt1_done, WT1)
            pick(0)
            stream(0)
            moments_of(NS)
            normalise(NS)
            split(NS)
            for q in range(4):
                maxima(0, q)
            negate(0)

            def choose():
                dve.wait_ge(logits_out, 4 * NS)
                link(dve.tensor_reduce(out=rs[0][:], in_=logit0[:], axis=AX.X, op=ALU.max))
                first_of(rt[0], rs[0], logit0[:])
                link(dve.scalar_tensor_tensor(out=rt[1].rearrange("p t e -> p (t e)"), in0=rt[0].rearrange("p t e -> p (t e)"),
                                              scalar=-1e38, in1=logit0[:].rearrange("p t e -> p (t e)"), op0=ALU.mult, op1=ALU.add))
                link(dve.tensor_reduce(out=rs[1][:], in_=rt[1], axis=AX.X, op=ALU.max))
                first_of(rt[2], rs[1], rt[1])
                link(dve.tensor_tensor(rt[1], rt[0], rt[2], ALU.add))
                assert count[0] == BOTH_AT
                link(dve.tensor_tensor(rs[1][:], rs[1][:], rs[0][:], ALU.subtract))
                assert count[0] == SECOND_AT

            def slots1():
                a, b = places(3, 4, 2)
                link(dve.tensor_tensor(filled[:], rt[a][:, NT - 1, :], totals[:, NT - 1, :], ALU.add))
                M = B * T // SLOTS
                link(dve.tensor_tensor(many, spread_over(filled, [[E, P], [1, E], [0, M]]),
                                       spread_over(steps16, [[M, P], [0, E], [1, M]]), ALU.is_gt))
                link(dve.tensor_reduce(out=n_blocks[:], in_=many, axis=AX.X, op=ALU.add))
                link(dve.tensor_copy(ends[1][:], n_blocks[:]))
                c, d, k = 1, 0, 1
                while k < E:
                    dve.tensor_copy(ends[d][:, 0:k], ends[c][:, 0:k])
                    link(dve.tensor_tensor(ends[d][:, k:E], ends[c][:, k:E], ends[c][:, 0:E - k], ALU.add))
                    c, d, k = d, c, 2 * k
                assert c == 0
                link(dve.tensor_tensor(slot0[:], ends[c][:], n_blocks[:], ALU.subtract))
                link(dve.tensor_scalar(slot0[:], slot0[:], float(SLOTS), None, ALU.mult))
                link(dve.tensor_tensor(rt[b], rt[b], spread_over(slot0, [[E, P], [0, NT], [1, E]]), ALU.add))
                for k, (onehot, at) in enumerate(((rt[0], rs[0]), (rt[2], rs[3]))):
                    link(dve.tensor_tensor(rt[a], rt[b], onehot, ALU.mult))
                    link(dve.tensor_reduce(out=at[:], in_=rt[a], axis=AX.X, op=ALU.add))
                    last = dve.tensor_copy(slots_at[:, k, :], at[:])
                last.then_inc(slots_done, 1)

            def blocks_and_weights():
                link(dve.tensor_tensor(passed, spread_over(numbers, [[BLOCKS, P], [1, BLOCKS], [0, E]]),
                                       spread_over(ends[0], [[E, P], [0, BLOCKS], [1, E]]), ALU.is_ge))
                link(dve.tensor_reduce(out=block_e[:], in_=passed, axis=AX.X, op=ALU.add))
                link(dve.tensor_scalar(block_e[:], block_e[:], float(E - 1), None, ALU.min))
                dve.tensor_copy(block_at[:], block_e[:]).then_inc(table_done, 1)
                dve.wait_ge(route_exp, 2)
                link(dve.tensor_scalar(rs[0][:], rs[1][:], 1.0, None, ALU.add))
                link(dve.reciprocal(rs[2][:], rs[0][:]))
                link(dve.tensor_tensor(rs[1][:], rs[1][:], rs[2][:], ALU.mult))
                link(dve.tensor_tensor(rt[0], rt[0], wide3(rs[2]), ALU.mult))
                link(dve.tensor_tensor(rt[2], rt[2], wide3(rs[1]), ALU.mult))
                dve.tensor_tensor(comb[:, 0:NT, :], rt[0], rt[2], ALU.add).then_inc(comb_done, 1)

            def body1(s, first, last):
                n = 2 * (s - NS)
                if not first:
                    finish(1, 2 * s - 1)
                add_bias(s, 0, 0)
                if not last:
                    stream(s - NS + 1)
                    moments_of(s + 1)
                add_bias(s, 0, 1)
                if not last:
                    normalise(s + 1)
                if not first:
                    add_out_1(s - NS - 1)
                maxima(n + 1, 0)
                add_bias(s, 0, 2)
                maxima(n + 1, 1)
                if not last:
                    split(s + 1)
                add_bias(s, 0, 3)
                maxima(n + 1, 2)
                maxima(n + 1, 3)
                negate(n + 1)
                finish(0, 2 * s)
                add_bias(s, 1, 0)
                add_bias(s, 1, 1)
                add_out_0(s - NS)
                if last:
                    blocks_and_weights()
                if routes_now(s):
                    choose()
                if not last:
                    maxima(n + 2, 0)
                if routes_now(s):
                    slots1()
                add_bias(s, 1, 2)
                if not last:
                    maxima(n + 2, 1)
                add_bias(s, 1, 3)
                if not last:
                    maxima(n + 2, 2)
                    maxima(n + 2, 3)
                    negate(n + 2)

            def add_layer1(u, at):
                dve.wait_ge(out_ps, 2 * (at + NS) + u + 1)
                ps = psB if u else psA
                dst = X[:, bass.ds(ST * at + 2 * u, 2), :]
                dve.tensor_tensor(dst, dst, ps[:, 0:2 * D].rearrange("p (t d) -> p t d", t=2), ALU.add).then_inc(x_done, 1)

            def add_out_0(at):
                add_layer1(0, at)

            def add_out_1(at):
                add_layer1(1, at)

            steps(dve, body1, NS)
            finish(1, 2 * B - 1)
            add_out_1(NS - 1)

            def weights_of(s):
                dve.tensor_copy(comb_s[:], comb[:, bass.ds(s * ST, ST), :]).then_inc(comb_s_done, 1)

            def shared(s):
                stream = X[:, bass.ds(s * ST, ST), :]
                dve.wait_ge(bias_ps, s + 1)
                dve.tensor_tensor(stream, psA[:].rearrange("p (t d) -> p t d", t=ST), stream, ALU.add).then_inc(bias_added, 1)
                weights_of(s + 1)
                dve.wait_ge(bias_added, s + 1)
                dve.wait_ge(y_ps, s + 1)
                dve.tensor_tensor(stream, psN[0][:].rearrange("p (t d) -> p t d", t=ST), stream, ALU.add).then_inc(y_used, 1)

            def take_tokens(j, u):
                dve.wait_ge(xb_turned, j + 1)
                dve.tensor_copy(block_bufs["xT", u], (psB if u else psA)[:, 0:SLOTS]).then_inc(xb_done, 1)

            def take_bias(j, u):
                e = dve.value_load(block_at[0:1, bass.ds(j, 1)], min_val=0, max_val=E - 1)
                if not (isinstance(j, int) and j < 2):
                    dve.wait_ge(gelub_done, HC * (j - 1))
                dve.tensor_tensor(block_bufs["b1", u], bcol[:, bass.ds(e * HC, HC)], ones_sq[:, 0:HC], ALU.mult).then_inc(b1_done, 1)

            def take_result(j, u):
                dve.wait_ge(yb_ps, j + 1)
                if not (isinstance(j, int) and j < 2):
                    dve.wait_ge(y_stored[u], 16 * ((j - u) // 2) if isinstance(j, int) else 16 * half_of[0])
                dve.tensor_copy(block_bufs["y", u], psN[u][:, 0:2 * D]).then_inc(yb_done, 1)

            dve.wait_ge(comb_done, 1)
            weights_of(0)
            shared(0)
            half_of = [None]
            for j in range(2):
                take_bias(j, j)
            for j in range(2):
                take_tokens(j, j)
            for j in range(2):
                take_tokens(j + 2, j)
                take_result(j, j)
                take_bias(j + 2, j)
            with dve.Fori(1, BLOCKS // 2 - 1) as i:
                half_of[0] = i
                for u in range(2):
                    take_tokens(2 * i + u + 2, u)
                    take_result(2 * i + u, u)
                    take_bias(2 * i + u + 2, u)
            for u in range(2):
                take_result(BLOCKS - 2 + u, u)

            def combine(s, pair, u):
                dve.wait_ge(picked_in[u], 32 * ST * (pair + 1))
                if not (isinstance(s, int) and s < 2):
                    dve.wait_ge(stored[u], 16 * pair)
                for k in range(2):
                    for t in range(ST):
                        if k == 0:
                            before = X[:, bass.ds(s * ST + t, 1), :].rearrange("p a d -> p (a d)")
                        else:
                            before = acc[u][:, t, :]
                        done = dve.scalar_tensor_tensor(out=acc[u][:, t, :],
                                                        in0=picked[:, bass.ds(s * ST + t, 1), k, :].rearrange("p a d -> p (a d)"),
                                                        scalar=rs[2 - k][:, bass.ds(s * ST + t, 1)], in1=before,
                                                        op0=ALU.mult, op1=ALU.add)
                    done.then_inc(summed if k else first_added, 1)
                    if k == 0:
                        dve.wait_ge(first_added, s + 1)

            dve.wait_ge(y_used, FRONT)
            shared(FRONT)
            for s in range(2):
                shared(FRONT + 1 + s)
                combine(s, 0, s)
            with dve.Fori(1, (NS - FRONT - 1) // 2) as i:
                for u in range(2):
                    shared(FRONT + 1 + 2 * i + u)
                    combine(2 * i + u, i, u)
            with dve.Fori((NS - FRONT - 1) // 2, NS // 2) as i:
                for u in range(2):
                    combine(2 * i + u, i, u)

        @block.scalar
        def _(act):
            act.wait_ge(wt_ps, 1)
            for c in range(2):
                act.activation(wT0[:, c, :].rearrange("p (d h) -> p d h", h=H),
                               psA[:, c * P:(c + 1) * P].rearrange("p (h d) -> p d h", h=H), ACT.Copy)
            act.activation(wT0[:, 2:4, :].rearrange("p c d -> p (c d)"), psA[:, 2 * P:4 * P], ACT.Copy).then_inc(wt_done, 1)
            act.wait_ge(wt_done, 1)
            act.wait_ge(w_in, 48)
            act.activation(wv0[:, 0:P], wT0[:, 2, :], ACT.Copy).then_inc(wt_done, 1)

            def turn(step, first):
                act.wait_ge(xn_turned, step + 1)
                if not first:
                    act.wait_ge(v_ps, 2 * step)
                    if layer[0] and not (isinstance(step, int) and step == NS):
                        act.wait_ge(xnT_kept, 16 * (step - NS))
                act.activation(xnT[:], psA[:], ACT.Copy).then_inc(xnT_done, 1)

            def project(step, first):
                if not first:
                    act.wait_ge(scratch_in, 64 * step)
                act.wait_ge(q_ps, step + 1)
                if layer[0]:
                    act.activation(parts["q"][:, 0, :], psA[:], ACT.Identity, bias=bqkg[:, 0:1]).then_inc(hi_done, 1)
                else:
                    act.activation(parts["q"][:, 0, :], psA[:], ACT.Copy).then_inc(hi_done, 1)
                act.wait_ge(k_ps, step + 1)
                if layer[0]:
                    act.activation(parts["k"][:, 0, :], psB[:], ACT.Identity, bias=bqkg[:, 1:2]).then_inc(hi_done, 1)
                else:
                    act.activation(parts["k"][:, 0, :], psB[:], ACT.Copy).then_inc(hi_done, 1)

            def values_out(step, first):
                if not first:
                    act.wait_ge(vpad_done, 2 * step)
                for n, ps in enumerate((psB, psA) if layer[0] else (psA, psB)):
                    act.wait_ge(v_ps, 2 * step + n + 1)
                    v = ps[:, 0:2 * (P + E)].rearrange("p (t c) -> p t c", t=2)
                    act.activation(vraw[:, 2 * n:2 * n + 2, :], v[:, :, 0:P], ACT.Copy).then_inc(v_out, 1)
                    act.activation(logit0[:, bass.ds((step - NS * layer[0]) * ST + 2 * n, 2), :], v[:, :, P:P + E], ACT.Copy).then_inc(logits_out, 1)

            def exps(s, u, q, first):
                for half in range(2):
                    act.wait_ge(scored, 16 * s + 8 * u + 2 * q + half + 1)
                    if half == 0 and not (first and u == 0):
                        act.wait_ge(weighed, 8 * s + 4 * u + q - 3)
                    act.activation(probs[q][:, 2 * half:2 * half + 2, :], psS[half][:, :, 0:QW], ACT.Exp,
                                   scale=SCALE).then_inc(exp_done, 1)
            layer = [0]
            turn(0, True)
            project(0, True)
            values_out(0, True)
            act.wait_ge(wt1_ps, 1)
            act.activation(w0T[:, 0:4, :].rearrange("p c d -> p (c d)"), psA[:], ACT.Copy).then_inc(wt1_done, 1)
            act.wait_ge(wt1_ps, 2)
            act.activation(w0T[:, 4:8, :].rearrange("p c d -> p (c d)"), psB[:], ACT.Copy).then_inc(wt1_done, 1)
            act.wait_ge(wt1_ps, 3)
            for c in range(2):
                act.activation(wT1[:, c, :].rearrange("p (d h) -> p d h", h=H),
                               psA[:, c * P:(c + 1) * P].rearrange("p (h d) -> p d h", h=H), ACT.Copy,
                               scale=1.0 if c else SCALE)
            act.activation(wT1[:, 2:4, :].rearrange("p c d -> p (c d)"), psA[:, 2 * P:4 * P], ACT.Copy).then_inc(wt1_done, 1)
            act.activation(wv1[:, 0:P], psA[:, 2 * P:3 * P], ACT.Copy).then_inc(wt1_done, 1)
            act.wait_ge(wt1_ps, 4)
            act.activation(wT1[:, 4, :], psB[:, 0:P], ACT.Copy)
            nb = E * HC + HC
            act.activation(bcol[:], psB[:, P:P + nb + 3], ACT.Copy)
            act.activation(bqkg[:, 0:1], psB[:, P + nb:P + nb + 1], ACT.Copy, scale=SCALE)
            act.activation(bqkg[:, 1:2], psB[:, P + nb + 1:P + nb + 2], ACT.Copy)
            act.activation(bqkg[:, 2:3], psB[:, P + nb + 2:P + nb + 3], ACT.Copy, scale=-1.0).then_inc(wt1_done, 1)
            act.wait_ge(key_table_in, 16)
            for n, i in enumerate(DVE_PAIRS):
                act.wait_ge(key_ps, n + 1)
                act.activation(btab[:, 2 * i:2 * i + 2, P:QW], psS[0][:, n % 2, :].rearrange("p (h c) -> p h c", h=2),
                               ACT.Copy).then_inc(key_done, 1)
            for i in PE_PAIRS:
                act.activation(bparts[:, 2 * i:2 * i + 2, 0, :], btab[:, 2 * i:2 * i + 2, P:QW], ACT.Copy).then_inc(key_high, 1)

            def body(s, first, last):
                exps(s, 0, 0, first)
                exps(s, 0, 1, first)
                exps(s, 0, 2, first)
                if not last:
                    turn(s + 1, False)
                exps(s, 0, 3, first)
                if not last:
                    project(s + 1, False)
                exps(s, 1, 0, first)
                if not last:
                    values_out(s + 1, False)
                exps(s, 1, 1, first)
                if routes_now(s):
                    act.wait_ge(routing, SHIFTED_AT)
                    act.activation(rt[1], rt[1], ACT.Exp).then_inc(route_exp, 1)
                exps(s, 1, 2, first)
                exps(s, 1, 3, first)
            steps(act, body)

            for e in range(E):
                act.wait_ge(x0_turned, e + 1)
                if e >= 2:
                    act.wait_ge(y0_ps, e - 1)
                act.activation(x0T[e % 2], (psB if e % 2 else psA)[:], ACT.Copy).then_inc(x0_done, 1)

            layer[0] = 1

            def combT_out(n):
                act.wait_ge(combT_ps, n + 1)
                if not (isinstance(n, int) and n == 0):
                    act.wait_ge(bias_ps, n)
                act.activation(combT[0:4 * E, :], psA[0:4 * E, 0:P], ACT.Copy).then_inc(combT_done, 1)

            def gate_out(step, first):
                act.wait_ge(gate_ps, step - NS + 1)
                if not first:
                    act.wait_ge(eg_done, 2 * (step - NS))
                act.activation(egraw[:], psA[:], ACT.Exp, scale=-1.0, bias=bqkg[:, 2:3]).then_inc(eg_out, 1)

            def maxima_out(n):
                act.wait_ge(negT_ps, n + 1)
                act.activation(mT[0:3 * H, :], psB[0:3 * H, 0:T], ACT.Copy).then_inc(negT_done, 1)

            def exps1(s, u, q):
                for half in range(2):
                    act.wait_ge(scored, 16 * s + 8 * u + 2 * q + half + 1)
                    if half == 0:
                        act.wait_ge(weighed, 8 * s + 4 * u + q - 3)
                    act.activation(probs[q][:, 2 * half, :], psS[half][:, 0, 0:QW], ACT.Exp).then_inc(exp1_done, 1)
                act.wait_ge(biased, 16 * (s - NS) + 8 * u + 2 * q + 2)
                act.activation(probs[q][:, 1:4:2, :], probs[q][:, 1:4:2, :], ACT.Exp).then_inc(exp1_done, 1)

            turn(NS, False)
            project(NS, False)
            gate_out(NS, True)
            values_out(NS, False)
            maxima_out(0)

            def body1(s, first, last):
                exps1(s, 0, 0)
                exps1(s, 0, 1)
                if not last:
                    turn(s + 1, False)
                exps1(s, 0, 2)
                if not last:
                    project(s + 1, False)
                exps1(s, 0, 3)
                if not last:
                    gate_out(s + 1, False)
                    values_out(s + 1, False)
                maxima_out(2 * (s - NS) + 1)
                for q in range(4):
                    exps1(s, 1, q)
                    if q == 1 and routes_now(s):
                        act.wait_ge(routing, SECOND_AT)
                        act.activation(rs[1][:], rs[1][:], ACT.Exp).then_inc(route_exp, 1)
                if not last:
                    maxima_out(2 * (s - NS) + 2)
            steps(act, body1, NS)

            def shared(s):
                if not (isinstance(s, int) and s == 0):
                    act.wait_ge(y_ps, s)
                for c in range(HC):
                    act.wait_ge(hid_ps, HC * s + c + 1)
                    act.activation(wide[2][:, c * SC:(c + 1) * SC], psS[c // 2][:, c % 2, :], ACT.Gelu,
                                   bias=bcol[:, E * HC + c:E * HC + c + 1]).then_inc(gelu_done, 1)
                    if c == 1:
                        combT_out(s)

            def blocks(j, u):
                act.wait_ge(b1_done, j + 1)
                if not (isinstance(j, int) and j < 2):
                    act.wait_ge(yb_ps, j - 1)
                for c in range(HC):
                    act.wait_ge(hidb_ps, HC * j + 2 * (c // 2) + 2)
                    act.activation(wide[u][:, c * SLOTS:(c + 1) * SLOTS], psS[u][:, c // 2, c % 2 * SLOTS:(c % 2 + 1) * SLOTS],
                                   ACT.Gelu, bias=block_bufs["b1", u][:, c:c + 1]).then_inc(gelub_done, 1)

            shared(0)
            for j in range(2):
                blocks(j, j)
            with act.Fori(1, BLOCKS // 2) as i:
                for u in range(2):
                    blocks(2 * i + u, u)
            with act.Fori(FRONT, NS) as s:
                shared(s)

        @block.tensor
        def _(pe):
            pe.wait_ge(masks_done, 4)
            pe.wait_ge(w_in, 48)
            for c in range(4):
                last = pe.transpose(psA[:, c * P:(c + 1) * P], wraw[:, c, :], ident[:])
            last.then_inc(wt_ps, 1)

            def turn(step):
                pe.wait_ge(xn_done, step + 1)
                for t in range(ST):
                    last = pe.transpose(psA[:, t * P:(t + 1) * P], xn[:, t, :], ident[:])
                last.then_inc(xn_turned, 1)

            def project(step):
                pe.wait_ge(xnT_done, step + 1)
                w = wT1 if layer[0] else wT0
                pe.matmul(psA[:], w[:, 0, :], xnT[:], start=True, stop=True).then_inc(q_ps, 1)
                pe.matmul(psB[:], w[:, 1, :], xnT[:], start=True, stop=True).then_inc(k_ps, 1)

            def values(step):
                for n, ps in ((0, psA), (1, psB)):
                    pe.wait_ge(rest_done, 2 * step + n + 1)
                    for t in range(2):
                        last = pe.matmul(ps[:, t * (P + E):(t + 1) * (P + E)], xnT[:, (2 * n + t) * P:(2 * n + t + 1) * P],
                                         wv0[:], start=True, stop=True)
                    last.then_inc(v_ps, 1)

            def values_read(n):
                pe.wait_ge(v_out, n)
                pe.wait_ge(logits_out, n)

            def score(s, u, q, first):
                if q == 0:
                    pe.wait_ge(qk_in[u], 96 * (s + 1))
                rows = SROWS
                for half in range(2):
                    if not (first and u == 0 and q == 0):
                        pe.wait_ge(exp_done, 16 * s + 8 * u + 2 * q + half - 1)
                    for i in range(2):
                        h = 4 * (2 * half + i) + q
                        pe.matmul(psS[half][:, i, 0:P], ks[u][0:rows, h, P:T], qs[u][0:rows, h, P:T], start=True, stop=True)
                        last = pe.matmul(psS[half][:, i, P:QW], ks[u][0:rows, h, 0:P], qs[u][0:rows, h, :], start=True, stop=True)
                    last.then_inc(scored, 1)

            def weigh(s, u, q, first, parts=(0, 1)):
                if parts[0] == 0:
                    if layer[0]:
                        pe.wait_ge(exp1_done, 24 * (s - NS) + 12 * u + 3 * q + 3)
                    else:
                        pe.wait_ge(clipped, 2 * (8 * s + 4 * u + q + 1))
                    if q == 0:
                        pe.wait_ge(vpad_done, 2 * s + u + 1)
                        if not first:
                            pe.wait_ge(heads_done, 2 * s + u - 1)
                for part in parts:
                    at = part * T
                    for kt, cols, to in ((0, (P, QW), (0, T)), (1, (0, P), (P, T))):
                        for g in range(4):
                            w = vpad[u][:, kt, 4 * g + q, :] if part == 0 else ones_pad[:, q, :]
                            last = pe.matmul(psN[u][VW * g:VW * (g + 1), at + to[0]:at + to[1]], w,
                                             probs[q][:, g, cols[0]:cols[1]],
                                             start=(q == 0 and part == 0 and kt == 0), stop=(q == 3 and kt == 1),
                                             skip_group_check=True)
                if 1 in parts:
                    last.then_inc(weighed, 1)

            def out_project(u, n):
                pe.wait_ge(heads_done, n + 1)
                ps = psB if u else psA
                for t in range(2):
                    last = pe.matmul(ps[:, t * D:(t + 1) * D], heads[:, t * P:(t + 1) * P], (wT1 if layer[0] else wT0)[:, 3, :],
                                     start=True, stop=not layer[0])
                    if layer[0]:
                        last = pe.matmul(ps[:, t * D:(t + 1) * D], one_row[:], bias_o[:], start=False, stop=True)
                last.then_inc(out_ps, 1)

            layer = [0]
            pe.wait_ge(wt_done, 2)
            turn(0)
            project(0)
            values(0)
            pe.wait_ge(late_in, 16 * LATE)
            values_read(1)
            for e in range(4):
                last = pe.transpose(psA[:, e * P:(e + 1) * P], acc[0][:, e, :], ident[:])
            last.then_inc(wt1_ps, 1)
            values_read(2)
            for e in range(4):
                last = pe.transpose(psB[:, e * P:(e + 1) * P], acc[1][:, e, :], ident[:])
            last.then_inc(wt1_ps, 1)
            pe.wait_ge(wt1_done, 1)
            for c in range(4):
                last = pe.transpose(psA[:, c * P:(c + 1) * P], wraw1[:, c, :], ident[:])
            last.then_inc(wt1_ps, 1)
            pe.wait_ge(wt1_done, 2)
            pe.transpose(psB[:, 0:P], wraw1[:, 4, :], ident[:])
            nb = E * HC + HC + 3
            pe.transpose(psB[:, P:P + nb], brow, ident[0:nb, 0:nb]).then_inc(wt1_ps, 1)
            pe.wait_ge(key_table_in, 16)
            for n, i in enumerate(DVE_PAIRS):
                if n >= 2:
                    pe.wait_ge(key_done, n - 1)
                pe.matmul(psS[0][:, n % 2, :], flip[:], btab[:, 2 * i:2 * i + 2, P:QW], start=True, stop=True).then_inc(key_ps, 1)
            pe.wait_ge(query_table_in, 16)
            for i in range(H // 2):
                if i >= 2:
                    pe.wait_ge(query_done, i - 1)
                pe.matmul(psS[1][:, i % 2, :], flip[:], btabq[:, 2 * i:2 * i + 2, :], start=True, stop=True).then_inc(query_ps, 1)
            pe.wait_ge(key_done, len(DVE_PAIRS))
            pe.wait_ge(query_done, H // 2)
            pe.wait_ge(wt1_done, WT1)
            pe.wait_ge(ones_done, 3)

            def count_tokens(chosen):
                flat = chosen.rearrange("p t e -> p (t e)")
                pe.matmul(psA[:, 0:NT * E], upper[:], flat, start=True, stop=True)
                pe.matmul(psA[:, NT * E:2 * NT * E], ones_sq[:], flat, start=True, stop=True).then_inc(loc_ps, 1)

            def body(s, first, last):
                score(s, 0, 0, first)
                if not first:
                    weigh(s - 1, 1, 2, False)
                score(s, 0, 1, first)
                if not first:
                    weigh(s - 1, 1, 3, False)
                score(s, 0, 2, first)
                weigh(s, 0, 0, first)
                values_read(2 * s + 2)
                if not first:
                    out_project(1, 2 * s - 1)
                if not last:
                    if not first:
                        pe.wait_ge(x_done, 2 * s - 1)
                    turn(s + 1)
                score(s, 0, 3, first)
                weigh(s, 0, 1, first)
                if not last:
                    if not first:
                        pe.wait_ge(x_done, 2 * s)
                    project(s + 1)
                score(s, 1, 0, first)
                weigh(s, 0, 2, first)
                if not last:
                    values(s + 1)
                score(s, 1, 1, first)
                weigh(s, 0, 3, first)
                score(s, 1, 2, first)
                weigh(s, 1, 0, first)
                if not last:
                    values_read(2 * s + 3)
                if routes_now(s):
                    pe.wait_ge(routing, ONEHOT_AT)
                    count_tokens(rt[0])
                out_project(0, 2 * s)
                score(s, 1, 3, first)
                weigh(s, 1, 1, first)
            steps(pe, body)
            weigh(NS - 1, 1, 2, False)
            weigh(NS - 1, 1, 3, False)
            out_project(1, B - 1)

            def turn0(e):
                pe.wait_ge(x0_in[e // 2], 16)
                for t in range(ST):
                    last = pe.transpose((psB if e % 2 else psA)[:, t * P:(t + 1) * P],
                                        x0_all[:, e * CAP + t * D:e * CAP + (t + 1) * D], ident[:])
                last.then_inc(x0_turned, 1)

            pe.wait_ge(x_done, B)
            pe.wait_ge(wt1_done, WT1)
            turn0(0)
            for e in range(E):
                if e + 1 < E:
                    turn0(e + 1)
                pe.wait_ge(x0_done, e + 1)
                if e >= 2:
                    pe.wait_ge(y0_done, e - 1)
                for t in range(ST):
                    last = pe.matmul(psN[e % 2][:, t * D:(t + 1) * D], x0T[e % 2][:, t * P:(t + 1) * P], w0T[:, e, :],
                                     start=True, stop=True)
                last.then_inc(y0_ps, 1)
            pe.wait_ge(y0_done, E)

            layer[0] = 1

            def emptied(unit, half):
                kind, n, q = unit
                if kind == "scores":
                    pe.wait_ge(exp1_done, 12 * n + 3 * q + half + 1)
                    pe.wait_ge(biased, 8 * n + 2 * q + half + 1)
                elif kind == "ranks":
                    pe.wait_ge(maxed, 8 * n + 2 * q + half + 1)
                else:
                    pe.wait_ge(exp_done, 16 * NS - 1 + half)

            def score1(s, u, q, before):
                if q == 0:
                    pe.wait_ge(qk_in[u], 96 * (s + 1))

                def less_maxima(half):
                    for i in range(2):
                        h = 4 * (2 * half + i) + q
                        pe.matmul(psS[half][:, i, 0:P], pick_head[:, h, :], mT[:, P:T], start=False, stop=True,
                                  skip_group_check=True)
                        last_one = pe.matmul(psS[half][:, i, P:QW], pick_head[:, h, :], mT[:], start=False, stop=True,
                                             skip_group_check=True)
                    last_one.then_inc(scored, 1)

                for half in range(2):
                    emptied(before, half)
                    for i in range(2):
                        h = 4 * (2 * half + i) + q
                        for cols, keys, queries, width in (((0, P), (P, T), (P, T), P), ((P, QW), (0, P), (0, T), T)):
                            o = psS[half][:, i, cols[0]:cols[1]]
                            pe.matmul(o, ks[u][:, h, keys[0]:keys[1]], qs[u][:, h, queries[0]:queries[1]],
                                      start=cols[0] == 0, stop=False, skip_group_check=True)
                            for k in range(0 if i else 3):
                                pe.matmul(o, flip16[:], bparts[:, h, k, 0:width], start=False, stop=False, skip_group_check=True)
                    if q:
                        less_maxima(half)
                if q == 0:
                    pe.wait_ge(negT_done, 2 * (s - NS) + u + 1)
                    less_maxima(0)
                    less_maxima(1)

            def rank(n, u, q, before):
                for half in range(2):
                    emptied(before, half)
                    for i in range(2):
                        h = 4 * (2 * half + i) + q
                        pe.matmul(psS[half][:, i, 0:P], qs[u][0:SROWS, h, 0:P], ks[u][0:SROWS, h, 0:P], start=True, stop=True)
                        last = pe.matmul(psS[half][:, i, P:QW], qs[u][0:SROWS, h, P:T], ks[u][0:SROWS, h, :], start=True, stop=True)
                    last.then_inc(ranked, 1)

            def turn_maxima(n):
                pe.wait_ge(neg_done, n + 1)
                if isinstance(n, int) and n == 0:
                    values_read(2 * NS + 2)
                else:
                    pe.wait_ge(negT_done, n)
                for qt in range(2):
                    last = pe.matmul(psB[0:3 * H, qt * P:(qt + 1) * P],
                                     mparts[:, qt, :, :].rearrange("p a h -> p (a h)"), ident16[:], start=True, stop=True)
                last.then_inc(negT_ps, 1)

            def turn_weights(n):
                pe.wait_ge(comb_s_done, n + 1)
                pe.transpose(psA[0:4 * E, 0:P], comb_s[:].rearrange("p t e -> p (t e)"), ident[:]).then_inc(combT_ps, 1)

            def bias_product(n):
                pe.wait_ge(combT_done, n + 1)
                pe.matmul(psA[:], combT[:], bdiag1[:].rearrange("k t d -> k (t d)"), start=True, stop=True).then_inc(bias_ps, 1)

            def gate(step):
                pe.wait_ge(rest_done, 2 * step + 1)
                pe.matmul(psA[:], wT1[:, 4, :], xnT[:], start=True, stop=True).then_inc(gate_ps, 1)

            def values1(step):
                for n, ps in ((0, psB), (1, psA)):
                    if n == 0:
                        pe.wait_ge(rest_done, 2 * step + 2)
                    else:
                        pe.wait_ge(eg_out, step - NS + 1)
                    for t in range(2):
                        o = ps[:, t * (P + E):(t + 1) * (P + E)]
                        pe.matmul(o, xnT[:, (2 * n + t) * P:(2 * n + t + 1) * P], wv1[:], start=True, stop=False)
                        last = pe.matmul(o, one_row[:], bias_v[:], start=False, stop=True)
                    last.then_inc(v_ps, 1)

            pe.wait_ge(wt1_done, WT1)
            pe.wait_ge(later_in, 16 * LATER)
            turn(NS)
            project(NS)
            gate(NS)
            values1(NS)
            pe.wait_ge(heads_masked, 4)
            pe.wait_ge(key_lo, len(PE_PAIRS))
            pe.wait_ge(qk_in[0], 96 * (NS + 1))
            for q in range(4):
                rank(0, 0, q, ("ranks", 0, q - 1) if q else ("layer 0", 0, 0))
            turn_maxima(0)

            def body1(s, first, last):
                n = 2 * (s - NS)
                score1(s, 0, 0, ("ranks", n, 3))
                if not first:
                    out_project(1, 2 * s - 1)
                score1(s, 0, 1, ("scores", n, 0))
                weigh(s, 0, 0, False, (0,))
                if not last:
                    if not first:
                        pe.wait_ge(x_done, 2 * s - 1)
                    turn(s + 1)
                pe.wait_ge(qk_in[1], 96 * (s + 1))
                rank(n + 1, 1, 0, ("scores", n, 1))
                weigh(s, 0, 0, False, (1,))
                score1(s, 0, 2, ("ranks", n + 1, 0))
                weigh(s, 0, 1, False, (0,))
                if not last:
                    if not first:
                        pe.wait_ge(x_done, 2 * s)
                    project(s + 1)
                rank(n + 1, 1, 1, ("scores", n, 2))
                weigh(s, 0, 1, False, (1,))
                score1(s, 0, 3, ("ranks", n + 1, 1))
                weigh(s, 0, 2, False, (0,))
                rank(n + 1, 1, 2, ("scores", n, 3))
                weigh(s, 0, 2, False, (1,))
                if not last:
                    gate(s + 1)
                rank(n + 1, 1, 3, ("ranks", n + 1, 2))
                if not last:
                    values1(s + 1)
                weigh(s, 0, 3, False)
                values_read(2 * s + (2 if last else 4))
                if last:
                    pe.wait_ge(slots_done, 1)
                turn_maxima(n + 1)
                score1(s, 1, 0, ("ranks", n + 1, 3))
                out_project(0, 2 * s)
                score1(s, 1, 1, ("scores", n + 1, 0))
                weigh(s, 1, 0, False, (0,))
                if not last:
                    pe.wait_ge(qk_in[0], 96 * (s + 2))
                    rank(n + 2, 0, 0, ("scores", n + 1, 1))
                weigh(s, 1, 0, False, (1,))
                if routes_now(s):
                    pe.wait_ge(x_done, 2 * s + 1)
                    pe.wait_ge(routing, BOTH_AT)
                    count_tokens(rt[1])
                score1(s, 1, 2, ("scores", n + 1, 1) if last else ("ranks", n + 2, 0))
                weigh(s, 1, 1, False, (0,))
                if not last:
                    rank(n + 2, 0, 1, ("scores", n + 1, 2))
                weigh(s, 1, 1, False, (1,))
                score1(s, 1, 3, ("scores", n + 1, 2) if last else ("ranks", n + 2, 1))
                weigh(s, 1, 2, False, (0,))
                if not last:
                    rank(n + 2, 0, 2, ("scores", n + 1, 3))
                weigh(s, 1, 2, False, (1,))
                if not last:
                    rank(n + 2, 0, 3, ("ranks", n + 2, 2))
                weigh(s, 1, 3, False)
                if not last:
                    turn_maxima(n + 2)
            steps(pe, body1, NS)
            out_project(1, 2 * B - 1)

            def shared(s):
                pe.wait_ge(stat_in, 16 * (s + 1))
                if not (isinstance(s, int) and s == 0):
                    pe.wait_ge(gelu_done, HC * s)
                for c in range(HC):
                    pe.matmul(psS[c // 2][:, c % 2, :], ws1_sb[:, c * P:(c + 1) * P], xstat[:], start=True, stop=True).then_inc(hid_ps, 1)
                    if c == 1:
                        turn_weights(s)
                bias_product(s)
                pe.wait_ge(gelu_done, HC * (s + 1))
                if not (isinstance(s, int) and s == 0):
                    pe.wait_ge(y_used, s)
                for t in range(ST):
                    for c in range(HC):
                        last = pe.matmul(psN[0][:, t * D:(t + 1) * D], wide[2][:, c * SC + t * P:c * SC + (t + 1) * P],
                                         ws2_sb[:, c, :], start=(c == 0), stop=(c == HC - 1))
                last.then_inc(y_ps, 1)

            def turn_block(j, u, pair):
                pe.wait_ge(x_in[u], 32 * (pair + 1))
                ps = psB if u else psA
                for t in range(2):
                    last = pe.transpose(ps[:, t * P:(t + 1) * P], block_bufs["x", u][:, t * D:(t + 1) * D], ident[:])
                last.then_inc(xb_turned, 1)

            def hidden(j, u):
                pe.wait_ge(xb_done, j + 1)
                for c in range(HC):
                    pe.matmul(psS[u][:, c // 2, c % 2 * SLOTS:(c % 2 + 1) * SLOTS], block_bufs["w1", u][:, c * P:(c + 1) * P],
                              block_bufs["xT", u], start=True, stop=True).then_inc(hidb_ps, 1)

            def results(j, u, pair):
                pe.wait_ge(w2_in[u], 16 * (pair + 1))
                pe.wait_ge(gelub_done, HC * (j + 1))
                if not (isinstance(j, int) and j < 2):
                    pe.wait_ge(yb_done, j - 1)
                for t in range(2):
                    for c in range(HC):
                        last = pe.matmul(psN[u][:, t * D:(t + 1) * D], wide[u][:, c * SLOTS + t * P:c * SLOTS + (t + 1) * P],
                                         block_bufs["w2", u][:, c * D:(c + 1) * D], start=(c == 0), stop=(c == HC - 1))
                last.then_inc(yb_ps, 1)

            pe.wait_ge(heads_done, 2 * B)
            pe.wait_ge(x_done, 2 * B)
            pe.wait_ge(biased, 16 * NS)
            pe.wait_ge(exp1_done, 24 * NS)
            shared(0)
            pe.wait_ge(y_used, FRONT)
            pe.wait_ge(bias_added, FRONT)
            turn_block(0, 0, 0)
            turn_block(1, 1, 0)
            hidden(0, 0)
            for j in range(2):
                hidden(j + 1, 1 - j)
                turn_block(j + 2, j, 1)
                results(j, j, 0)
            with pe.Fori(1, BLOCKS // 2 - 1) as i:
                for u in range(2):
                    hidden(2 * i + u + 1, 1 - u)
                    turn_block(2 * i + u + 2, u, i + 1)
                    results(2 * i + u, u, i)
            hidden(BLOCKS - 1, 1)
            results(BLOCKS - 2, 0, BLOCKS // 2 - 1)
            results(BLOCKS - 1, 1, BLOCKS // 2 - 1)
            pe.wait_ge(yb_done, BLOCKS)
            with pe.Fori(FRONT, NS) as s:
                shared(s)


_INS = ["L0_attn_x", "L0_attn_Wqkv", "L0_attn_Wout", "L0_ffn_wg", "L0_ffn_W", "L0_ffn_b", "L1_attn_Wqkv", "L1_attn_bqkv",
        "L1_attn_Wout", "L1_attn_bout", "L1_attn_Wgate", "L1_attn_bgate", "L1_attn_pos_bias", "L1_ffn_gate_w",
        "L1_ffn_gate_b", "L1_ffn_w1", "L1_ffn_b1", "L1_ffn_w2", "L1_ffn_b2", "L1_ffn_ws1", "L1_ffn_bs1", "L1_ffn_ws2",
        "L1_ffn_bs2"]


def kernel(**inputs):
    import numpy as np
    import concourse.bacc as bacc
    from concourse.bass_utils import run_bass_kernel_spmd as run

    nc = bacc.Bacc("TRN2", target_bir_lowering=False, num_devices=1)
    arrays, args = {}, []
    for name in _INS:
        a = np.ascontiguousarray(inputs[name])
        arrays[f"in_{name}"] = a
        args.append(nc.dram_tensor(f"in_{name}", a.shape, mybir.dt.from_np(a.dtype), kind="ExternalInput").ap())
    args.append(nc.dram_tensor("out_x", (B, T, D), F32, kind="ExternalOutput").ap())
    build(nc, *args)
    r = run(nc, [arrays], core_ids=[0])
    return r.results[0]["out_x"]
```
